# Optimizing a Trainium2 kernel written in Bass

```python
import numpy as np
import jax
import jax.numpy as jnp

def _softmax(x, axis=-1):
    return jax.nn.softmax(x, axis=axis)

def _gelu(x):
    return jax.nn.gelu(x, approximate=True)

def _silu(x):
    return jax.nn.silu(x)

def _sigmoid(x):
    return jax.nn.sigmoid(x)

def _layernorm(x, axis=-1, eps=1e-05):
    m = jnp.mean(x, axis=axis, keepdims=True)
    v = jnp.var(x, axis=axis, keepdims=True)
    return (x - m) / jnp.sqrt(v + eps)

def _scatter_add(tgt, idx, src, axis=0):
    return tgt.at[idx].add(src)

def _segment_sum(src, seg, n):
    return jax.ops.segment_sum(src, seg, n)
kernel_name = 'mk_flamingo_gated_d2_seqx_r4_421506'

def setup_inputs(seed: int=0):
    np.random.seed(seed)
    _w = jnp.asarray

    def _rec_inputs():
        import jax
        import jax.numpy as jnp
        _rk = jax.random.key(seed)
        x = -0.0002928 + 1 * jax.random.normal(jax.random.fold_in(_rk, 1), (16, 128, 256), jnp.float32)
        _lenS = 128 - jax.random.randint(jax.random.fold_in(_rk, 7), (16,), 0, max(1, 128 // 4) + 1, jnp.int32)
        _lenS2 = 128 - jax.random.randint(jax.random.fold_in(_rk, 8), (16,), 0, max(1, 128 // 4) + 1, jnp.int32)
        _ctx_1024P = jax.random.normal(jax.random.fold_in(_rk, 11), (16, 16, 256), jnp.float32)
        _ctx_1024c = jax.random.dirichlet(jax.random.fold_in(_rk, 511), 0.3 * jnp.ones((16,), jnp.float32), (16, 128))
        _ctx_1024t = jnp.einsum('bsk,bkd->bsd', _ctx_1024c, _ctx_1024P)
        _ctx_1024t = _ctx_1024t * jax.lax.rsqrt(jnp.mean(jnp.square(_ctx_1024t)) + 1e-12) * 0.953939
        ctx_1024 = -1.39393e-06 + 0.999914 * (_ctx_1024t + 0.3 * jax.random.normal(jax.random.fold_in(_rk, 611), (16, 128, 256), jnp.float32))
        itok_BxSx2_0_63 = jax.random.randint(jax.random.fold_in(_rk, 12), (16, 128, 2), 0, 64, jnp.int32)
        _g = jax.random.normal(jax.random.fold_in(_rk, 9001), (2, 2), jnp.float32)
        _g = jnp.sign(_g) * jnp.maximum(jnp.abs(_g), 1.0) + (_g == 0) * 1.0
        g_xattn = _g[0]
        g_ffn = _g[1]
        return (x, ctx_1024, itok_BxSx2_0_63, g_xattn, g_ffn)
    x, ctx_1024, itok_BxSx2_0_63, g_xattn, g_ffn = _rec_inputs()

    def _L0_xattn_setup():
        import jax, jax.numpy as jnp
        import numpy as np
        ROPE_BASE = 100.0

        def _rope1d(tok, pos1d, base=ROPE_BASE):
            d = tok.shape[-1]
            inv_freq = 1.0 / base ** (jnp.arange(0, d, 2, dtype=jnp.float32) / d)
            ang = pos1d.astype(jnp.float32)[..., None] * inv_freq
            ang = jnp.concatenate([ang, ang], axis=-1)
            cos = jnp.cos(ang)[:, None]
            sin = jnp.sin(ang)[:, None]
            x1, x2 = jnp.split(tok, 2, axis=-1)
            rot = jnp.concatenate([-x2, x1], axis=-1)
            return tok * cos + rot * sin

        def _rope2d(tok, pos):
            ty, tx = jnp.split(tok, 2, axis=-1)
            ty = _rope1d(ty, pos[..., 0])
            tx = _rope1d(tx, pos[..., 1])
            return jnp.concatenate([ty, tx], axis=-1)
        key = jax.random.key(seed)
        ks = jax.random.split(key, 16)
        B, Nq, Nk, dim, H = (2, 512, 512, 256, 16)
        s = dim ** (-0.5)
        inp = {'query': jax.random.normal(ks[0], (B, Nq, dim), jnp.float32), 'key': jax.random.normal(ks[1], (B, Nk, dim), jnp.float32), 'value': jax.random.normal(ks[2], (B, Nk, dim), jnp.float32), 'Wq': jax.random.normal(ks[3], (dim, dim), jnp.float32) * s, 'bq': jnp.zeros((dim,), jnp.float32), 'Wk': jax.random.normal(ks[4], (dim, dim), jnp.float32) * s, 'bk': jnp.zeros((dim,), jnp.float32), 'Wv': jax.random.normal(ks[5], (dim, dim), jnp.float32) * s, 'bv': jnp.zeros((dim,), jnp.float32), 'Wp': jax.random.normal(ks[6], (dim, dim), jnp.float32) * s, 'bp': jnp.zeros((dim,), jnp.float32), 'qpos': jax.random.randint(ks[7], (B, Nq, 2), 0, 64, jnp.int64 if jax.config.jax_enable_x64 else jnp.int32), 'kpos': jax.random.randint(ks[8], (B, Nk, 2), 0, 64, jnp.int64 if jax.config.jax_enable_x64 else jnp.int32), 'num_cls': 1}
        return inp
    _L0_xattn_all = _L0_xattn_setup()
    _L0_xattn_in = {k: v for k, v in _L0_xattn_all.items() if k in ('Wq', 'bq', 'Wk', 'bk', 'Wv', 'bv', 'Wp', 'bp')}
    del _L0_xattn_all

    def _L0_ffn_setup():
        import jax, jax.numpy as jnp
        import numpy as np
        B, T, C, I, E = (4, 512, 256, 704, 7)

        def _swiglu(h, w1, w2, w3):
            return jax.nn.silu(h @ w1.T) * (h @ w3.T) @ w2.T
        key = jax.random.key(seed)
        ks = jax.random.split(key, 9)
        sc_c = 1.0 / np.sqrt(C)
        sc_i = 1.0 / np.sqrt(I)
        return {'x': jax.random.normal(ks[0], (B, T, C), jnp.float32), 'router_w': jax.random.normal(ks[1], (E, C), jnp.float32) * sc_c, 'routing_bias': jnp.zeros((E,), jnp.float32), 'sw1': jax.random.normal(ks[2], (I, C), jnp.float32) * sc_c, 'sw2': jax.random.normal(ks[3], (C, I), jnp.float32) * sc_i, 'sw3': jax.random.normal(ks[4], (I, C), jnp.float32) * sc_c, 'ew1': jax.random.normal(ks[5], (E, I, C), jnp.float32) * sc_c, 'ew2': jax.random.normal(ks[6], (E, C, I), jnp.float32) * sc_i, 'ew3': jax.random.normal(ks[7], (E, I, C), jnp.float32) * sc_c}
    _L0_ffn_all = _L0_ffn_setup()
    _L0_ffn_in = {k: v for k, v in _L0_ffn_all.items() if k in ('router_w', 'routing_bias', 'sw1', 'sw2', 'sw3', 'ew1', 'ew2', 'ew3')}
    del _L0_ffn_all

    def _L1_xattn_setup():
        import jax, jax.numpy as jnp
        import numpy as np
        EPS = 1e-05

        def layer_norm(x, g, b):
            mu = jnp.mean(x, axis=-1, keepdims=True)
            var = jnp.var(x, axis=-1, keepdims=True)
            return (x - mu) * jax.lax.rsqrt(var + EPS) * g + b
        key = jax.random.key(seed)
        ks = jax.random.split(key, 8)
        dim, heads, dim_head = (256, 16, 64)
        inner = heads * dim_head
        b, n, m = (8, 1024, 64)
        s = dim ** (-0.5)
        return {'x': jax.random.normal(ks[0], (b, n, dim), jnp.float32), 'latents': jax.random.normal(ks[1], (b, m, dim), jnp.float32), 'ln_m_g': jnp.ones((dim,), jnp.float32), 'ln_m_b': jnp.zeros((dim,), jnp.float32), 'ln_l_g': jnp.ones((dim,), jnp.float32), 'ln_l_b': jnp.zeros((dim,), jnp.float32), 'Wq': jax.random.normal(ks[2], (dim, inner), jnp.float32) * s, 'Wkv': jax.random.normal(ks[3], (dim, 2 * inner), jnp.float32) * s, 'Wout': jax.random.normal(ks[4], (inner, dim), jnp.float32) * s}
    _L1_xattn_all = _L1_xattn_setup()
    _L1_xattn_in = {k: v for k, v in _L1_xattn_all.items() if k in ('ln_m_g', 'ln_m_b', 'ln_l_g', 'ln_l_b', 'Wq', 'Wkv', 'Wout')}
    del _L1_xattn_all

    def _L1_ffn_setup():
        import jax, jax.numpy as jnp
        import numpy as np
        FP8_MAX = 448.0

        def quant_fp8(x):
            amax = jnp.max(jnp.abs(x)).astype(jnp.float32)
            scale = jnp.minimum(FP8_MAX / jnp.maximum(amax, 1e-12), FP8_MAX)
            x_fp8 = jnp.clip(x * scale, -FP8_MAX, FP8_MAX).astype(jnp.float8_e4m3fn)
            return (x_fp8, 1.0 / scale)
        key = jax.random.key(seed)
        k1, k2, k3 = jax.random.split(key, 3)
        B, S, IN, OUT = (4, 2048, 256, 256)
        input = jax.random.normal(k1, (B, S, IN), dtype=jnp.float32)
        bound = 1.0 / np.sqrt(IN)
        weight = jax.random.uniform(k2, (OUT, IN), dtype=jnp.float32, minval=-bound, maxval=bound)
        bias = jax.random.uniform(k3, (OUT,), dtype=jnp.float32, minval=-bound, maxval=bound)
        return {'input': input, 'weight': weight, 'bias': bias}
    _L1_ffn_all = _L1_ffn_setup()
    _L1_ffn_in = {k: v for k, v in _L1_ffn_all.items() if k in ('weight', 'bias')}
    del _L1_ffn_all
    return {'x': x, 'ctx_1024': ctx_1024, 'itok_BxSx2_0_63': itok_BxSx2_0_63, 'g_xattn': g_xattn, 'g_ffn': g_ffn, 'L0_xattn_Wq': _L0_xattn_in['Wq'], 'L0_xattn_bq': _L0_xattn_in['bq'], 'L0_xattn_Wk': _L0_xattn_in['Wk'], 'L0_xattn_bk': _L0_xattn_in['bk'], 'L0_xattn_Wv': _L0_xattn_in['Wv'], 'L0_xattn_bv': _L0_xattn_in['bv'], 'L0_xattn_Wp': _L0_xattn_in['Wp'], 'L0_xattn_bp': _L0_xattn_in['bp'], 'L0_ffn_router_w': _L0_ffn_in['router_w'], 'L0_ffn_routing_bias': _L0_ffn_in['routing_bias'], 'L0_ffn_sw1': _L0_ffn_in['sw1'], 'L0_ffn_sw2': _L0_ffn_in['sw2'], 'L0_ffn_sw3': _L0_ffn_in['sw3'], 'L0_ffn_ew1': _L0_ffn_in['ew1'], 'L0_ffn_ew2': _L0_ffn_in['ew2'], 'L0_ffn_ew3': _L0_ffn_in['ew3'], 'L1_xattn_ln_m_g': _L1_xattn_in['ln_m_g'], 'L1_xattn_ln_m_b': _L1_xattn_in['ln_m_b'], 'L1_xattn_ln_l_g': _L1_xattn_in['ln_l_g'], 'L1_xattn_ln_l_b': _L1_xattn_in['ln_l_b'], 'L1_xattn_Wq': _L1_xattn_in['Wq'], 'L1_xattn_Wkv': _L1_xattn_in['Wkv'], 'L1_xattn_Wout': _L1_xattn_in['Wout'], 'L1_ffn_weight': _L1_ffn_in['weight'], 'L1_ffn_bias': _L1_ffn_in['bias']}

def reference(x, ctx_1024, itok_BxSx2_0_63, g_xattn, g_ffn, L0_xattn_Wq, L0_xattn_bq, L0_xattn_Wk, L0_xattn_bk, L0_xattn_Wv, L0_xattn_bv, L0_xattn_Wp, L0_xattn_bp, L0_ffn_router_w, L0_ffn_routing_bias, L0_ffn_sw1, L0_ffn_sw2, L0_ffn_sw3, L0_ffn_ew1, L0_ffn_ew2, L0_ffn_ew3, L1_xattn_ln_m_g, L1_xattn_ln_m_b, L1_xattn_ln_l_g, L1_xattn_ln_l_b, L1_xattn_Wq, L1_xattn_Wkv, L1_xattn_Wout, L1_ffn_weight, L1_ffn_bias):
    import jax
    import jax.numpy as jnp

    def _L0_xattn_ref(query, key, value, Wq, bq, Wk, bk, Wv, bv, Wp, bp, qpos, kpos, num_cls):
        import jax, jax.numpy as jnp
        import numpy as np
        ROPE_BASE = 100.0

        def _rope1d(tok, pos1d, base=ROPE_BASE):
            d = tok.shape[-1]
            inv_freq = 1.0 / base ** (jnp.arange(0, d, 2, dtype=jnp.float32) / d)
            ang = pos1d.astype(jnp.float32)[..., None] * inv_freq
            ang = jnp.concatenate([ang, ang], axis=-1)
            cos = jnp.cos(ang)[:, None]
            sin = jnp.sin(ang)[:, None]
            x1, x2 = jnp.split(tok, 2, axis=-1)
            rot = jnp.concatenate([-x2, x1], axis=-1)
            return tok * cos + rot * sin

        def _rope2d(tok, pos):
            ty, tx = jnp.split(tok, 2, axis=-1)
            ty = _rope1d(ty, pos[..., 0])
            tx = _rope1d(tx, pos[..., 1])
            return jnp.concatenate([ty, tx], axis=-1)
        B, Nq, C = query.shape
        Nk = key.shape[1]
        H = 16
        Dh = C // H
        scale = Dh ** (-0.5)
        nc = int(num_cls)

        def split_heads(x, W, b, N):
            return (x @ W.T + b).reshape(B, N, H, Dh).transpose(0, 2, 1, 3)
        q = split_heads(query, Wq, bq, Nq)
        k = split_heads(key, Wk, bk, Nk)
        v = split_heads(value, Wv, bv, Nk)
        q_nc = _rope2d(q[:, :, nc:], qpos[:, nc:])
        k_nc = _rope2d(k[:, :, nc:], kpos[:, nc:])
        sim_rope = jnp.einsum('bhqd,bhkd->bhqk', q_nc, k_nc)
        if nc > 0:
            sim_qcls_k = jnp.einsum('bhqd,bhkd->bhqk', q[:, :, :nc], k[:, :, nc:])
            sim_q = jnp.einsum('bhqd,bhkd->bhqk', q, k[:, :, :nc])
            sim = jnp.concatenate([sim_qcls_k, sim_rope], axis=-2)
            sim = jnp.concatenate([sim_q, sim], axis=-1)
        else:
            sim = sim_rope
        attn = jax.nn.softmax(sim * scale, axis=-1)
        x = jnp.einsum('bhqk,bhkd->bhqd', attn, v)
        x = x.transpose(0, 2, 1, 3).reshape(B, Nq, C)
        return x @ Wp.T + bp

    def _L0_ffn_ref(x, router_w, routing_bias, sw1, sw2, sw3, ew1, ew2, ew3):
        import jax, jax.numpy as jnp
        import numpy as np
        B, T, C, I, E = (4, 512, 256, 704, 7)

        def _swiglu(h, w1, w2, w3):
            return jax.nn.silu(h @ w1.T) * (h @ w3.T) @ w2.T
        b, t, c = x.shape
        shared_out = _swiglu(x, sw1, sw2, sw3)
        logits = jnp.clip(x @ router_w.T + routing_bias, -50.0, 50.0)
        probs = jax.nn.sigmoid(logits)
        num_switched = 1
        topk_probs, topk_idx = jax.lax.top_k(probs, num_switched)
        topk_probs = jnp.clip(topk_probs, 1e-08, 1.0 - 1e-08)
        xf = x.reshape(-1, c)
        sel = topk_idx.reshape(-1)
        p = topk_probs.reshape(-1)
        switched = jnp.zeros_like(xf)
        n_experts = ew1.shape[0]
        for e in range(n_experts):
            y = _swiglu(xf, ew1[e], ew2[e], ew3[e])
            w = jnp.where(sel == e, p, 0.0)
            switched = switched + w[:, None] * y
        switched = switched.reshape(b, t, c)
        total_weight = 0.5 + topk_probs.sum(axis=-1)
        total_weight = jnp.clip(total_weight[..., None] + 1e-08, 0.5, 2.0)
        return 0.5 / total_weight * shared_out + switched / total_weight

    def _L1_xattn_ref(x, latents, ln_m_g, ln_m_b, ln_l_g, ln_l_b, Wq, Wkv, Wout):
        import jax, jax.numpy as jnp
        import numpy as np
        EPS = 1e-05

        def layer_norm(x, g, b):
            mu = jnp.mean(x, axis=-1, keepdims=True)
            var = jnp.var(x, axis=-1, keepdims=True)
            return (x - mu) * jax.lax.rsqrt(var + EPS) * g + b
        heads, dim_head = (16, 64)
        scale = dim_head ** (-0.5)
        x = layer_norm(x, ln_m_g, ln_m_b)
        lat = layer_norm(latents, ln_l_g, ln_l_b)
        b, m, _ = lat.shape
        q = lat @ Wq
        kv_input = jnp.concatenate([x, lat], axis=1)
        kv = kv_input @ Wkv
        k, v = jnp.split(kv, 2, axis=-1)

        def split_heads(t):
            return t.reshape(t.shape[0], t.shape[1], heads, dim_head).transpose(0, 2, 1, 3)
        q, k, v = (split_heads(q), split_heads(k), split_heads(v))
        dots = jnp.einsum('bhid,bhjd->bhij', q, k) * scale
        attn = jax.nn.softmax(dots, axis=-1)
        out = jnp.einsum('bhij,bhjd->bhid', attn, v)
        out = out.transpose(0, 2, 1, 3).reshape(b, m, heads * dim_head)
        return out @ Wout

    def _L1_ffn_ref(input, weight, bias):
        import jax, jax.numpy as jnp
        import numpy as np
        FP8_MAX = 448.0

        def quant_fp8(x):
            amax = jnp.max(jnp.abs(x)).astype(jnp.float32)
            scale = jnp.minimum(FP8_MAX / jnp.maximum(amax, 1e-12), FP8_MAX)
            x_fp8 = jnp.clip(x * scale, -FP8_MAX, FP8_MAX).astype(jnp.float8_e4m3fn)
            return (x_fp8, 1.0 / scale)
        prev_shape = input.shape
        x2d = input.reshape(-1, weight.shape[1])
        w_fp8, w_scale = quant_fp8(weight)
        x_fp8, x_scale = quant_fp8(x2d)
        acc = jnp.matmul(x_fp8.astype(jnp.float32), w_fp8.astype(jnp.float32).T)
        out2d = (acc * (x_scale * w_scale) + bias).astype(jnp.bfloat16)
        out = out2d.reshape(*prev_shape[:-1], weight.shape[0]).astype(input.dtype)
        return out
    x = x + jnp.tanh(g_xattn[0]) * _L0_xattn_ref(_layernorm(x, axis=-1), ctx_1024, ctx_1024, L0_xattn_Wq, L0_xattn_bq, L0_xattn_Wk, L0_xattn_bk, L0_xattn_Wv, L0_xattn_bv, L0_xattn_Wp, L0_xattn_bp, itok_BxSx2_0_63, itok_BxSx2_0_63, 1)
    x = x + jnp.tanh(g_ffn[0]) * _L0_ffn_ref(_layernorm(x, axis=-1), L0_ffn_router_w, L0_ffn_routing_bias, L0_ffn_sw1, L0_ffn_sw2, L0_ffn_sw3, L0_ffn_ew1, L0_ffn_ew2, L0_ffn_ew3)
    x = x + jnp.tanh(g_xattn[1]) * _L1_xattn_ref(ctx_1024, _layernorm(x, axis=-1), L1_xattn_ln_m_g, L1_xattn_ln_m_b, L1_xattn_ln_l_g, L1_xattn_ln_l_b, L1_xattn_Wq, L1_xattn_Wkv, L1_xattn_Wout)
    x = x + jnp.tanh(g_ffn[1]) * _L1_ffn_ref(_layernorm(x, axis=-1), L1_ffn_weight, L1_ffn_bias)
    return x

_drawn_inputs = setup_inputs


def setup_inputs(seed=0):
    import zlib

    import numpy as np

    out = dict(_drawn_inputs(seed))
    spreads = {'g_ffn': (-1.0, 0.59),
     'L0_xattn_bq': (0.0, 0.1),
     'L0_xattn_bk': (0.0, 0.353),
     'L0_xattn_bv': (0.0, 0.1),
     'L0_xattn_bp': (0.0, 0.1),
     'L0_ffn_routing_bias': (0.0, 0.1),
     'L1_xattn_ln_m_g': (1.0, 0.2),
     'L1_xattn_ln_m_b': (0.0, 0.1),
     'L1_xattn_ln_l_g': (1.0, 0.2),
     'L1_xattn_ln_l_b': (0.0, 0.1)}
    factors = {}
    for name, (base, spread) in spreads.items():
        noise = np.random.default_rng([zlib.crc32(name.encode()), seed]).standard_normal(out[name].shape)
        drawn = base * np.exp(spread * noise) if base else spread * noise
        out[name] = jnp.asarray(drawn.astype(out[name].dtype))
    for name, factor in factors.items():
        out[name] = (out[name] * factor).astype(out[name].dtype)
    return out
```

```python
from contextlib import ExitStack

import numpy as np

import concourse.bass as bass
from concourse import mybir

F32 = mybir.dt.float32
BF16 = mybir.dt.bfloat16
I32 = mybir.dt.int32
U32 = mybir.dt.uint32
ALU = mybir.AluOpType
ACT = mybir.ActivationFunctionType
AX = mybir.AxisListType

P = 128
NB = 16
D = 256
KT = D // P
EPS = 1e-5

H0, DH0 = 16, 16
SLOT = 64
KSTACK = 3 * DH0
ROPE_BASE = 100.0
NFREQ = DH0 // 4
ANGLE_STEPS = 11 + NFREQ


NE = 7
FF = 704
FT = -(-FF // P)
FLAST = FF - (FT - 1) * P
W1, W3, W2 = 0, KT * FF, 2 * KT * FF
WCOLS = W2 + FT * D
QC = WCOLS // 4
NTOK = NB * P
NT = (NTOK + NE * (P - 1)) // P
CH = 512
NCH = NTOK // CH

H1, DH1 = 16, 64
SIGMOID_ONE = 25 * float(np.log(2))


def wait(eng, sem, value):
    if isinstance(value, int) and value <= 0:
        return
    eng.wait_ge(sem, value)


def rotate(eng, n, first, step, last):
    first(0, 0)
    with eng.Fori(1, n - 2, 2) as i:
        step(i, 1)
        step(i + 1, 0)
    step(n - 1, 1)
    last(n, 0)


def stage_rope_attention(nc, T, C, tag="A"):
    xres = C["xres"]
    with ExitStack() as ctx:
        def sb(name, shape, dt=F32):
            return ctx.enter_context(nc.sbuf_tensor(tag + name, shape, dt))

        def ps(name, shape, dt=F32):
            return ctx.enter_context(nc.psum_tensor(tag + name, shape, dt))

        def sem(name):
            return nc.alloc_semaphore(name=tag + name)

        wq = sb("wq", [P, KT, D])
        wkv = sb("wkv", [P, KT, 2 * D])
        wp = sb("wp", [P, KT, D])
        bias = sb("bias", [P, 4, D])
        xn = sb("xn", [P, 2, D])
        xnT = sb("xnT", [P, 2, KT, P])
        cT = sb("cT", [P, 2, KT, P])
        q3 = sb("q3", [P, H0, SLOT])
        k3 = sb("k3", [P, H0, SLOT])
        v1 = sb("v1", [P, 2, H0, DH0 + 1])
        qT = sb("qT", [P, 2, H0 // 2, P])
        kT = sb("kT", [P, 2, H0 // 2, P])
        qrot = sb("qrot", [P, H0, DH0])
        krot = sb("krot", [P, H0, DH0])
        E = sb("E", [P, H0, P])
        PT = sb("PT", [P, H0, P])
        mx = sb("mx", [P, H0])
        rs = sb("rs", [P, H0])
        On = sb("On", [P, D])
        OT = sb("OT", [P, KT, P])
        stats = sb("stats", [P, 6])
        xw = sb("xw", [P, D])
        posi = sb("posi", [P, NB, 2], I32)
        posf = sb("posf", [P, NB, 2])
        ang = sb("ang", [P, NB, 2, NFREQ])
        turns = sb("turns", [P, NB, 2, NFREQ])
        red = sb("red", [P, 3, NB, 2, NFREQ])
        sc = sb("sc", [P, 2, NB, 2, NFREQ])
        cosT = sb("cosT", [P, NB, 2, 2, NFREQ])
        sinT = sb("sinT", [P, NB, 2, 2, NFREQ])

        pS = [ps(f"pS{j}", [P, 4, P]) for j in range(4)]
        pT = [ps(f"pT{j}", [P, 4, P]) for j in range(2)]
        pKV = ps("pKV", [P, 2 * D])
        pQ = ps("pQ", [P, 2 * D])
        psQ = pQ[:, 0:D]
        psO = pQ[:, 0:H0 * (DH0 + 1)].rearrange("p (h d) -> p h d", h=H0)
        psY = pQ[:, 0:D]

        ident, first, rest, mv, rstd, tg = (C[k] for k in ("ident", "first", "rest", "mv", "rstd", "tg"))

        s_w = sem("weights_in")
        s_ct = [sem(f"ctxT_in{u}") for u in range(2)]
        s_tab = sem("table_steps")
        s_sin = sem("sines")
        s_tabs = sem("tables_ready")
        s_one = sem("ones_ready")
        s_bpg = sem("gated_bias")
        s_xn = sem("xn")
        s_xTp = sem("xT_in_psum")
        s_xT = sem("xT")
        s_kvp = sem("kv_in_psum")
        s_qp = sem("q_in_psum")
        s_v = sem("v")
        s_kb = sem("k_biased")
        s_qb = sem("q_biased")
        s_krot = sem("k_rotated")
        s_qrot = sem("q_rotated")
        s_kcos = sem("k_cos")
        s_qcos = sem("q_cos")
        s_k3 = sem("k3_parts")
        s_q3 = sem("q3_parts")
        s_qTp = sem("qT_in_psum")
        s_qT = sem("qT_halves")
        s_kTp = sem("kT_in_psum")
        s_kT = sem("kT_halves")
        s_S = sem("scores")
        s_mx = sem("maxima")
        s_sub = sem("shifted")
        s_E = sem("exps")
        s_PTp = sem("PT_in_psum")
        s_PT = sem("PT")
        s_O = sem("O_in_psum")
        s_rs = sem("recip_sums")
        s_On = sem("O_normed")
        s_OTp = sem("OT_in_psum")
        s_OT = sem("OT")
        s_y = sem("y_in_psum")
        s_xb = sem("x_plus_bias")
        s_x1 = sem("x_new")
        s_bs = sem("bn_stats")
        s_keep = sem("x_and_stats_kept")
        bstats = C["bstats"]

        def head_at(c):
            return 8 * (c // 8) + 2 * (c % 4) + (c // 4) % 2

        def heads(ap):
            return ap.rearrange("p (h d) -> p h d", h=H0)

        def halves(ap):
            return ap.rearrange("p h (a s f) -> p h a s f", a=2, s=2)

        def table(tab, b, half=None):
            if half is None:
                t = tab[:, bass.ds(b, 1), :, :, :].rearrange("p o a s f -> p o (a s f)")
                return t.broadcast_to([P, H0, DH0])
            t = tab[:, bass.ds(b, 1), :, half, :]
            return t.broadcast_to([P, H0, 2, NFREQ])

        with nc.Block() as block:
            @block.sync
            def _(sp):
                sp.dma_start(wq[:], T["A_wq"]).then_inc(s_w, 16)
                sp.dma_start(wkv[:], T["A_wkv"]).then_inc(s_w, 16)
                sp.dma_start(wp[:], T["A_wp"]).then_inc(s_w, 16)
                sp.dma_start(posi[:], T["pos"]).then_inc(s_w, 16)
                sp.dma_start(bias[:].rearrange("p w n -> p (w n)"),
                             T["A_bias"].partition_broadcast(P)).then_inc(s_w, 16)

                def load(b, u):
                    wait(sp, s_kvp, b - 1)
                    sp.dma_start(cT[:, u], T["ctxT"][bass.ds(b, 1)].rearrange("o p k t -> (o p) k t")
                                 ).then_inc(s_ct[u], 16)

                load(0, 0)
                load(1, 1)
                with sp.Fori(2, NB - 1, 2) as i:
                    load(i, 0)
                    load(i + 1, 1)

            @block.gpsimd
            def _(pool):
                pool.memset(v1[:, :, :, DH0:DH0 + 1], 1.0).then_inc(s_one, 1)
                pool.memset(q3[:, :, KSTACK:SLOT], 0.0).then_inc(s_one, 1)
                pool.wait_ge(s_w, 16 * 5)
                pool.wait_ge(C["s_tanh"], 1)
                pool.tensor_scalar(bias[:, 3, :], bias[:, 3, :], tg[:, 0:1], None, ALU.mult).then_inc(s_bpg, 1)
                pool.wait_ge(s_bpg, 1)
                pool.wait_ge(s_tabs, 3)

                def rope_k(b, u):
                    pool.wait_ge(s_kb, b + 1)
                    wait(pool, s_kTp, 2 * b)
                    kb = k3[:, :, KSTACK:SLOT]
                    pool.tensor_tensor(k3[:, :, 0:DH0], kb, table(cosT, b), ALU.mult).then_inc(s_kcos, 1)
                    for s in range(2):
                        pool.tensor_tensor(halves(krot[:])[:, :, :, s, :], halves(kb)[:, :, :, 1 - s, :],
                                           table(sinT, b, s), ALU.mult).then_inc(s_krot, 1)
                    pool.tensor_scalar(k3[:, :, DH0:2 * DH0], kb, first[:], None, ALU.mult).then_inc(s_k3, 1)
                    pool.tensor_scalar(k3[:, :, 2 * DH0:3 * DH0], kb, rest[:], None, ALU.mult).then_inc(s_k3, 1)
                    pool.wait_ge(s_kcos, b + 1)
                    pool.wait_ge(s_krot, 2 * b + 2)
                    pool.tensor_tensor(k3[:, :, 0:DH0], k3[:, :, 0:DH0], krot[:], ALU.add).then_inc(s_k3, 1)
                    pool.wait_ge(s_xn, b + 1)
                    x = xres[:, bass.ds(b, 1), :].rearrange("p o n -> p (o n)")
                    pool.tensor_tensor(x, x, bias[:, 3, :], ALU.add).then_inc(s_xb, 1)

                rope_k(0, 0)
                with pool.Fori(1, NB) as i:
                    rope_k(i, 0)

            @block.scalar
            def _(act):
                act.wait_ge(s_tab, ANGLE_STEPS)
                act.activation(sc[:, 0], red[:, 0], ACT.Sin).then_inc(s_sin, 1)
                act.activation(sc[:, 1], red[:, 2], ACT.Sin).then_inc(s_sin, 1)

                def begin(b, u):
                    act.wait_ge(s_xTp, b + 1)
                    wait(act, s_qp, b - 1)
                    act.activation(xnT[:, u], pT[0][:, 0:KT], ACT.Copy).then_inc(s_xT, 1)

                def turn(b, u):
                    wait(act, s_S, 4 * b - 4)
                    for dst, src, done in ((qT, s_qTp, s_qT), (kT, s_kTp, s_kT)):
                        for h in range(2):
                            act.wait_ge(src, 2 * b + h + 1)
                            act.activation(dst[:, u, 4 * h:4 * h + 4], pT[1 - h][:], ACT.Copy).then_inc(done, 1)

                def attend(b, u):
                    def exp(j):
                        act.wait_ge(s_sub, 4 * b + j + 1)
                        act.activation(E[:, 4 * j:4 * j + 4], E[:, 4 * j:4 * j + 4], ACT.Exp,
                                       scale=DH0 ** -0.5).then_inc(s_E, 1)

                    def evac(j):
                        act.wait_ge(s_PTp, 4 * b + j + 1)
                        if j == 0:
                            wait(act, s_O, b)
                        act.activation(PT[:, 4 * j:4 * j + 4], pT[1 - j % 2][:], ACT.Copy).then_inc(s_PT, 1)

                    exp(0)
                    exp(1)
                    evac(0)
                    exp(2)
                    evac(1)
                    exp(3)
                    evac(2)
                    evac(3)
                    act.wait_ge(s_OTp, b + 1)
                    wait(act, s_y, b)
                    act.activation(OT[:], pT[1][:, 0:KT], ACT.Copy).then_inc(s_OT, 1)

                def start(b, u):
                    begin(b, u)
                    turn(b, u)

                def step(b, u):
                    start(b, u)
                    attend(b - 1, 1 - u)

                rotate(act, NB, start, step, lambda b, u: attend(b - 1, 1 - u))

            @block.tensor
            def _(pe):
                pe.wait_ge(s_w, 16 * 5)
                pe.wait_ge(C["s_ident"], 1)
                pe.wait_ge(s_one, 2)

                def project(b, u):
                    pe.wait_ge(s_xn, b + 1)
                    wait(pe, s_PT, 4 * b - 4)
                    wait(pe, s_kT, 2 * b)
                    for k in range(KT):
                        mm = pe.transpose(pT[0][:, k], xn[:, u, k * P:(k + 1) * P], ident[:])
                    mm.then_inc(s_xTp, 1)
                    pe.wait_ge(s_ct[u], 8 * (b + 2 - u))
                    wait(pe, s_v, b)
                    wait(pe, s_kb, b)
                    for k in range(KT):
                        mm = pe.matmul(pKV[:], cT[:, u, k], wkv[:, k], start=(k == 0), stop=(k == KT - 1))
                    mm.then_inc(s_kvp, 1)
                    pe.wait_ge(s_xT, b + 1)
                    wait(pe, s_x1, b - 1)
                    wait(pe, s_qb, b)
                    for k in range(KT):
                        mm = pe.matmul(psQ, xnT[:, u, k], wq[:, k], start=(k == 0), stop=(k == KT - 1))
                    mm.then_inc(s_qp, 1)

                def scores(b, u):
                    pe.wait_ge(s_qT, 2 * b + 2)
                    pe.wait_ge(s_kT, 2 * b + 2)
                    for j in range(0, 4, 2):
                        for n in range(4):
                            for r in range(2):
                                rows = slice(SLOT * r, SLOT * r + KSTACK)
                                mm = pe.matmul(pS[j + r][:, n], qT[rows, u, 2 * j + n], kT[rows, u, 2 * j + n],
                                               start=True, stop=True)
                        mm.then_inc(s_S, 2)

                def turn(b, u):
                    wait(pe, s_OT, b - 1)
                    for src, parts, ready, done, evac in ((q3, 3, s_q3, s_qTp, s_qT), (k3, 3, s_k3, s_kTp, s_kT)):
                        pe.wait_ge(ready, parts * (b + 1))
                        for h in range(2):
                            if src is q3:
                                if h == 1:
                                    pe.wait_ge(s_xT, b + 1)
                            else:
                                pe.wait_ge(s_qT, 2 * b + h + 1)
                            for n in range(4):
                                mm = pe.transpose(pT[1 - h][:, n], src[:, 8 * h + 2 * n:8 * h + 2 * n + 2].rearrange(
                                    "p h d -> p (h d)"), ident[:])
                            mm.then_inc(done, 1)

                def attend(b, u, turned):
                    for j in range(4):
                        pe.wait_ge(s_E, 4 * b + j + 1)
                        if j < 2:
                            pe.wait_ge(s_kT, 2 * turned)
                            wait(pe, s_OT, b)
                        else:
                            pe.wait_ge(s_PT, 4 * b + j - 1)
                        for n in range(4):
                            mm = pe.transpose(pT[1 - j % 2][:, n], E[:, 4 * j + n], ident[:])
                        mm.then_inc(s_PTp, 1)
                    pe.wait_ge(s_v, b + 1)
                    pe.wait_ge(s_qb, turned)
                    wait(pe, s_x1, b)
                    for c in range(H0):
                        if c % 4 == 0:
                            pe.wait_ge(s_PT, 4 * b + c // 4 + 1)
                        h = head_at(c)
                        mm = pe.matmul(psO[:, h], PT[:, c], v1[:, u, h], start=True, stop=True)
                    mm.then_inc(s_O, 1)
                    pe.wait_ge(s_On, b + 1)
                    for k in range(KT):
                        mm = pe.transpose(pT[1][:, k], On[:, k * P:(k + 1) * P], ident[:])
                    mm.then_inc(s_OTp, 1)
                    pe.wait_ge(s_OT, b + 1)
                    for k in range(KT):
                        mm = pe.matmul(psY, OT[:, k], wp[:, k], start=(k == 0), stop=(k == KT - 1))
                    mm.then_inc(s_y, 1)

                def start(b, u):
                    project(b, u)
                    turn(b, u)

                def step(b, u):
                    project(b, u)
                    scores(b - 1, 1 - u)
                    turn(b, u)
                    attend(b - 1, 1 - u, b + 1)

                def last(b, u):
                    scores(b - 1, 1 - u)
                    attend(b - 1, 1 - u, b)

                rotate(pe, NB, start, step, last)

            @block.vector
            def _(dve):
                n_tab = [0]

                def link(ins):
                    n_tab[0] += 1
                    ins.then_inc(s_tab, 1)
                    dve.wait_ge(s_tab, n_tab[0])

                dve.wait_ge(s_w, 16 * 5)
                link(dve.tensor_copy(posf[:], posi[:]))
                for f in range(NFREQ):
                    inv = np.float32(1.0) / np.float32(ROPE_BASE) ** np.float32(2 * f / (DH0 // 2))
                    ins = dve.tensor_scalar(ang[:, :, :, f], posf[:], float(inv), None, ALU.mult)
                    n_tab[0] += 1
                    ins.then_inc(s_tab, 1)
                dve.wait_ge(s_tab, n_tab[0])
                MAGIC = 1.5 * 2.0 ** 23
                TWO_PI = 2 * np.pi
                c1 = 6.28125
                c2 = float(np.float32(TWO_PI - c1).view(np.uint32) & np.uint32(0xFFFFF000)) and float(
                    (np.float32(TWO_PI - c1).view(np.uint32) & np.uint32(0xFFFFF000)).view(np.float32))
                c3 = float(np.float32(TWO_PI - c1 - c2))
                link(dve.tensor_scalar(turns[:], ang[:], float(1 / TWO_PI), MAGIC, ALU.mult, ALU.add))
                link(dve.tensor_scalar(turns[:], turns[:], -MAGIC, None, ALU.add))
                for c in (c1, c2, c3):
                    link(dve.scalar_tensor_tensor(ang[:], turns[:], -c, ang[:], ALU.mult, ALU.add))
                PI = float(np.nextafter(np.float32(np.pi), np.float32(0)))
                link(dve.tensor_scalar(red[:, 0], ang[:], PI, -PI, ALU.min, ALU.max))
                link(dve.tensor_scalar(red[:, 2], ang[:], float(np.pi / 2), None, ALU.add))
                link(dve.tensor_scalar(red[:, 1], red[:, 2], float(np.pi), -TWO_PI, ALU.is_gt, ALU.mult))
                link(dve.tensor_tensor(red[:, 2], red[:, 2], red[:, 1], ALU.add))
                link(dve.tensor_scalar(red[:, 2], red[:, 2], PI, -PI, ALU.min, ALU.max))
                assert n_tab[0] == ANGLE_STEPS
                dve.wait_ge(s_sin, 2)
                dve.wait_ge(C["s_masks"], 2)
                for s in range(2):
                    ins = dve.tensor_scalar(cosT[:, :, :, s, :], sc[:, 1], rest[:], None, ALU.mult)
                    link(ins)
                    ins = dve.tensor_scalar(sinT[:, :, :, s, :], sc[:, 0], rest[:], -1.0 if s == 0 else 1.0,
                                            ALU.mult, ALU.mult)
                    link(ins)
                dve.tensor_copy(rs[:, 0:1], first[:]).then_inc(s_tabs, 3)
                dve.wait_ge(C["s_rstd_" + tag], 1)

                def norm(b, u):
                    wait(dve, s_xTp, b - 1)
                    x = xres[:, bass.ds(b, 1), :].rearrange("p o n -> p (o n)")
                    m = mv[:, bass.ds(b, 1), 0:1].rearrange("p o n -> p (o n)")
                    r = rstd[:, bass.ds(b, 1)]
                    dve.tensor_scalar(xn[:, u], x, m, r, ALU.subtract, ALU.mult).then_inc(s_xn, 1)

                def rope_q(b, u):
                    dve.wait_ge(s_kvp, b + 1)
                    wait(dve, s_kTp, 2 * b)
                    wait(dve, s_k3, 3 * b)
                    dve.tensor_tensor(k3[:, :, KSTACK:SLOT], heads(pKV[:, 0:D]), heads(bias[:, 1, :]),
                                      ALU.add).then_inc(s_kb, 1)
                    wait(dve, s_O, b - 1)
                    dve.tensor_tensor(v1[:, u, :, 0:DH0], heads(pKV[:, D:2 * D]), heads(bias[:, 2, :]),
                                      ALU.add).then_inc(s_v, 1)
                    dve.wait_ge(s_qp, b + 1)
                    wait(dve, s_qTp, 2 * b)
                    qb = q3[:, :, DH0:2 * DH0]
                    dve.tensor_tensor(qb, heads(psQ), heads(bias[:, 0, :]), ALU.add).then_inc(s_qb, 1)
                    dve.wait_ge(s_qb, b + 1)
                    dve.tensor_tensor(q3[:, :, 0:DH0], qb, table(cosT, b), ALU.mult).then_inc(s_qcos, 1)
                    for s in range(2):
                        dve.tensor_tensor(halves(qrot[:])[:, :, :, s, :], halves(qb)[:, :, :, 1 - s, :],
                                          table(sinT, b, s), ALU.mult).then_inc(s_qrot, 1)
                    dve.tensor_scalar(q3[:, :, 2 * DH0:3 * DH0], qb, first[:], None, ALU.mult).then_inc(s_q3, 1)
                    dve.wait_ge(s_qcos, b + 1)
                    dve.wait_ge(s_qrot, 2 * b + 2)
                    dve.tensor_tensor(q3[:, :, 0:DH0], q3[:, :, 0:DH0], qrot[:], ALU.add).then_inc(s_q3, 2)

                def attend(b, u):
                    for j in range(4):
                        hs = slice(4 * j, 4 * j + 4)
                        dve.wait_ge(s_S, 4 * b + j + 1)
                        dve.tensor_reduce(mx[:, hs], pS[j][:], AX.X, ALU.max).then_inc(s_mx, 1)
                        dve.wait_ge(s_mx, 4 * b + j + 1)
                        dve.tensor_tensor(E[:, hs], pS[j][:], mx[:, hs].unsqueeze(2).broadcast_to([P, 4, P]),
                                          ALU.subtract).then_inc(s_sub, 1)
                    dve.wait_ge(s_O, b + 1)
                    dve.reciprocal(rs[:], psO[:, :, DH0]).then_inc(s_rs, 1)
                    dve.wait_ge(s_rs, b + 1)
                    wait(dve, s_OTp, b)
                    dve.tensor_tensor(heads(On[:]), psO[:, :, 0:DH0], rs[:].unsqueeze(2).broadcast_to([P, H0, DH0]),
                                      ALU.mult).then_inc(s_On, 1)
                    dve.wait_ge(s_y, b + 1)
                    dve.wait_ge(s_xb, b + 1)
                    x = xres[:, bass.ds(b, 1), :].rearrange("p o n -> p (o n)")
                    wait(dve, s_keep, 2 * b)
                    dve.scalar_tensor_tensor(xw[:], psY, tg[:, 0:1], x, ALU.mult, ALU.add).then_inc(s_x1, 1)
                    dve.wait_ge(s_x1, b + 1)
                    dve.bn_stats(stats[:], xw[:]).then_inc(s_bs, 1)
                    dve.tensor_scalar(x, xw[:], 0.0, None, ALU.add).then_inc(s_keep, 1)
                    dve.wait_ge(s_bs, b + 1)
                    dve.tensor_scalar(bstats[:, bass.ds(b, 1), :].rearrange("p o n -> p (o n)"), stats[:], 0.0, None,
                                      ALU.add).then_inc(s_keep, 1)

                def first_(b, u):
                    norm(0, 0)
                    rope_q(0, 0)
                    norm(1, 1)

                def step(b, u):
                    rope_q(b, u)
                    if not isinstance(b, int):
                        norm(b + 1, 1 - u)
                    attend(b - 1, 1 - u)

                rotate(dve, NB, first_, step, lambda b, u: attend(b - 1, 1 - u))


def norm_stats(nc, C, tag):
    def sem(name):
        return nc.alloc_semaphore(name=tag + name)

    mv, rstd, half, vare, bstats = (C[k] for k in ("mv", "rstd", "half", "vare", "bstats"))
    s_mv, s_ve, s_rstd = sem("mean_var"), sem("var_eps"), sem("rstd_ready")

    def vector(dve):
        for b in range(NB):
            dve.bn_aggr(mv[:, b], bstats[:, b]).then_inc(s_mv, 1)

    def gpsimd(pool):
        pool.wait_ge(s_mv, NB)
        pool.tensor_scalar(vare[:], mv[:, :, 1], EPS, None, ALU.add).then_inc(s_ve, 1)
        pool.wait_ge(s_ve, 1)
        pool.tensor_tensor(rstd[:], vare[:], half[:], ALU.pow).then_inc(s_rstd, 1)

    return vector, gpsimd, s_rstd


def row(ap, b):
    return ap[:, bass.ds(b, 1), :].rearrange("p o n -> p (o n)")


def stage_experts(nc, T, C, tag="B"):
    xres, ident, mv, rstd, tg = (C[k] for k in ("xres", "ident", "mv", "rstd", "tg"))
    with ExitStack() as ctx:
        def sb(name, shape, dt=F32):
            return ctx.enter_context(nc.sbuf_tensor(tag + name, shape, dt))

        def sem(name):
            return nc.alloc_semaphore(name=tag + name)

        we = sb("we", [P, 2, NE * WCOLS], BF16)
        ws = sb("ws", [P, 2, WCOLS], BF16)
        xT2 = sb("xT2", [P, 2, KT, NTOK], BF16)
        stage = sb("stage", [P, 2, QC])
        xw = sb("xw", [P, 2, D])
        xT = sb("xT", [P, 2, KT, P])
        rw = sb("rw", [P, KT, NE])
        rb = sb("rb", [P, NE])
        spare = [we[:, part, (NE - 1) * WCOLS:(NE - 1) * WCOLS + NTOK * D // P].bitcast(F32).rearrange(
            "p (b n) -> p b n", n=D) for part in range(2)]
        HB = NB // 2

        lg = sb("lg", [P, NB, NE])
        key = sb("key", [P, NB, NE])
        pr = sb("pr", [P, NB, NE])
        one = sb("one", [P, NB, NE])
        run = sb("run", [P, NB + 1, NE])
        tmp = sb("tmp", [P, NB, NE])
        pos = sb("pos", [P, NB])
        posi = sb("posi", [P, NB], I32)
        r16 = sb("r16", [P, NB])
        p16 = sb("p16", [P, NB])
        cshare = sb("cshare", [P, NB])
        croute = sb("croute", [P, NB])
        cnt = sb("cnt", [P, NE])
        cnti = sb("cnti", [P, NE], I32)
        ends = sb("ends", [P, NE + 1])
        pref_i = sb("pref_i", [P, NE], I32)
        pref = sb("pref", [P, NE])
        slot_i = sb("slot_i", [1, NT], I32)
        slot_f = sb("slot_f", [1, NT])
        past = sb("past", [1, NT, NE])
        eidf = sb("eidf", [1, NT])
        eid = sb("eid", [1, NT], I32)

        bank = [ctx.enter_context(nc.psum_tensor(f"{tag}bank{i}", [P, 512], F32)) for i in range(8)]

        def tile2(ap):
            return ap[:, 0:KT * P].rearrange("p (k t) -> p k t", k=KT)

        s_w = [sem(f"w_in{u}") for u in range(2)]
        s_hi = sem("w_high")
        s_lo = sem("w_low")
        s_r = sem("router_in")
        s_k1 = sem("constants1")
        s_k2 = sem("constants2")
        s_xw = sem("xn_for_transpose")
        s_xn = sem("xn_for_slots")
        s_xTp = sem("xT_in_psum")
        s_xT = sem("xT")
        s_xhi = sem("xT_high")
        s_xlo = sem("xT_low")
        s_lgp = sem("logits_in_psum")
        s_lg = sem("logits")
        s_c = sem("routing_steps")
        s_key = sem("clipped_logits")
        s_ex = sem("router_exp")
        s_one = sem("one_hot")
        s_cum = sem("counts_in_psum")
        s_scat = sem("scattered")
        s_h1 = sem("shared_h1")
        s_h3 = sem("shared_h3")
        s_si = sem("shared_silu")
        s_hd = sem("shared_hidden")
        s_hh = sem("shared_hidden_high")
        s_hl = sem("shared_hidden_low")
        s_yp1 = sem("shared_y_products")
        s_ys = sem("shared_added")
        s_xs = [sem(f"slots_in{u}") for u in range(2)]
        s_tp = sem("slotsT_in_psum")
        s_th = sem("slotsT_high")
        s_tl = sem("slotsT_low")
        s_e1 = sem("expert_h1")
        s_e3 = sem("expert_h3")
        s_es = sem("expert_silu")
        s_ed = sem("expert_hidden")
        s_eh = sem("expert_hidden_high")
        s_el = sem("expert_hidden_low")
        s_yp = sem("expert_y_in_psum")
        s_y = sem("expert_y")
        s_yst = [sem(f"y_stored{u}") for u in range(2)]
        s_yg = [sem(f"y_gathered{j}") for j in range(NB)]
        s_x2 = sem("x_new")
        s_bs = sem("bn_stats")

        stats_vector, stats_gpsimd, s_rstd = norm_stats(nc, C, tag)

        def each_tile(eng, body):
            body(0, 0, 0, 0)
            body(1, 1, 0, 1)
            with eng.Fori(2, HB - 1, 2) as i:
                body(i, 0, 0, i)
                body(i + 1, 1, 0, i + 1)
            with eng.Fori(0, HB - 1, 2) as i:
                body(i + HB, 0, 1, i)
                body(i + (HB + 1), 1, 1, i + 1)

        with nc.Block() as block, ExitStack() as rctx:
            below = rctx.enter_context(nc.sbuf_tensor(tag + "below", [P, P], F32))
            ones = rctx.enter_context(nc.sbuf_tensor(tag + "ones", [P, P], F32))

            @block.sync
            def _(sp):
                sp.dma_start(rw[:], T["B_rw"]).then_inc(s_r, 16)
                sp.dma_start(rb[:], T["B_rb"].partition_broadcast(P)).then_inc(s_r, 16)
                for q in range(4):
                    if q >= 2:
                        sp.wait_ge(s_lo, q - 1)
                        sp.wait_ge(s_hi, q - 1)
                    sp.dma_start(stage[:, q % 2], T["B_ws"][q]).then_inc(s_w[q % 2], 16)

            @block.gpsimd
            def _(pool):
                stats_gpsimd(pool)
                pool.memset(below[:], 1.0).then_inc(s_k1, 1)
                pool.memset(ones[:], 1.0).then_inc(s_k1, 1)
                pool.iota(pref_i[:], pattern=[[-1, NE]], base=NE, channel_multiplier=0).then_inc(s_k1, 1)
                pool.iota(slot_i[:], pattern=[[1, NT]], base=0, channel_multiplier=0).then_inc(s_k1, 1)
                pool.wait_ge(s_k1, 4)
                pool.affine_select(out=below[:], in_=below[:], compare_op=ALU.is_gt, fill=0.0, base=0,
                                   pattern=[[1, P]], channel_multiplier=-1).then_inc(s_k2, 1)

            @block.scalar
            def _(act):
                for q in range(4):
                    act.wait_ge(s_w[q % 2], 16 * (q // 2 + 1))
                    act.activation(ws[:, 0, q * QC:(q + 1) * QC], stage[:, q % 2], ACT.Copy).then_inc(s_hi, 1)

                def evac(j, u, part, place):
                    act.wait_ge(s_xTp, j + 1)
                    wait(act, s_lgp, j - 1)
                    wait(act, s_xlo, j - 1)
                    act.activation(xT[:, u], tile2(bank[u]), ACT.Copy).then_inc(s_xT, 1)

                each_tile(act, evac)
                act.wait_ge(s_key, 1)
                act.activation(pr[:], pr[:], ACT.Exp, scale=-1.0).then_inc(s_ex, 1)

            @block.tensor
            def _(pe):
                pe.wait_ge(s_r, 32)

                def turn(j, u, part, place):
                    pe.wait_ge(s_xw, j + 1)
                    wait(pe, s_xT, j - 1)
                    for k in range(KT):
                        mm = pe.transpose(bank[u][:, k * P:(k + 1) * P], xw[:, u, k * P:(k + 1) * P], ident[:])
                    mm.then_inc(s_xTp, 1)
                    pe.wait_ge(s_xT, j + 1)
                    wait(pe, s_lg, j - 1)
                    for k in range(KT):
                        mm = pe.matmul(bank[2 + u][:, 0:NE], xT[:, u, k], rw[:, k], start=(k == 0), stop=(k == KT - 1))
                    mm.then_inc(s_lgp, 1)

                each_tile(pe, turn)
                pe.wait_ge(s_k2, 1)
                pe.wait_ge(s_one, 1)
                hot = one[:].rearrange("p b e -> p (b e)")
                pe.matmul(bank[4][:, 0:NB * NE], below[:], hot, start=True, stop=True)
                pe.matmul(bank[5][:, 0:NB * NE], ones[:], hot, start=True, stop=True).then_inc(s_cum, 1)

            @block.vector
            def _(dve):
                n = [0]

                def link(ins):
                    n[0] += 1
                    ins.then_inc(s_c, 1)
                    dve.wait_ge(s_c, n[0])

                stats_vector(dve)
                for q in range(4):
                    dve.wait_ge(s_hi, q + 1)
                    cols = slice(q * QC, (q + 1) * QC)
                    dve.tensor_tensor(ws[:, 1, cols], stage[:, q % 2], ws[:, 0, cols], ALU.subtract).then_inc(s_lo, 1)
                dve.wait_ge(s_rstd, 1)

                def norm(j, u, part, place):
                    m = mv[:, bass.ds(j, 1), 0:1].rearrange("p o n -> p (o n)")
                    r = rstd[:, bass.ds(j, 1)]
                    wait(dve, s_xTp, j - 1)
                    dve.tensor_scalar(xw[:, u], row(xres, j), m, r, ALU.subtract, ALU.mult).then_inc(s_xw, 1)
                    dve.tensor_scalar(row(spare[part], place), row(xres, j), m, r,
                                      ALU.subtract, ALU.mult).then_inc(s_xn, 1)
                    dve.wait_ge(s_xT, j + 1)
                    hi, lo = (xT2[:, part2, :, bass.ds(j * P, P)] for part2 in range(2))
                    dve.tensor_scalar(hi, xT[:, u], 0.0, None, ALU.add).then_inc(s_xhi, 1)
                    dve.wait_ge(s_xhi, j + 1)
                    dve.tensor_tensor(lo, xT[:, u], hi, ALU.subtract).then_inc(s_xlo, 1)
                    dve.wait_ge(s_lgp, j + 1)
                    dve.tensor_tensor(row(lg, j), bank[2 + u][:, 0:NE], rb[:], ALU.add).then_inc(s_lg, 1)

                each_tile(dve, norm)
                dve.wait_ge(s_lg, NB)
                dve.tensor_scalar(pr[:], lg[:], -50.0, 50.0, ALU.max, ALU.min).then_inc(s_key, 1)
                link(dve.tensor_scalar(key[:], lg[:], -50.0, SIGMOID_ONE, ALU.max, ALU.min))
                dve.wait_ge(s_k1, 4)
                link(dve.tensor_copy(pref[:], pref_i[:]))
                link(dve.tensor_reduce(r16[:], key[:], AX.X, ALU.max))
                wide = [P, NB, NE]
                link(dve.tensor_tensor(key[:], key[:], r16[:].unsqueeze(2).broadcast_to(wide), ALU.is_equal))
                link(dve.tensor_tensor(key[:], key[:], pref[:].unsqueeze(1).broadcast_to(wide), ALU.mult))
                link(dve.tensor_reduce(r16[:], key[:], AX.X, ALU.max))
                dve.tensor_tensor(one[:], key[:], r16[:].unsqueeze(2).broadcast_to(wide), ALU.is_equal).then_inc(s_one, 1)
                dve.wait_ge(s_ex, 1)
                dve.wait_ge(s_one, 1)
                link(dve.tensor_scalar(pr[:], pr[:], 1.0, None, ALU.add))
                link(dve.reciprocal(pr[:], pr[:]))
                link(dve.tensor_tensor(tmp[:], pr[:], one[:], ALU.mult))
                link(dve.tensor_reduce(p16[:], tmp[:], AX.X, ALU.add))
                link(dve.tensor_scalar(p16[:], p16[:], 1e-8, float(np.float32(1.0 - 1e-8)), ALU.max, ALU.min))
                link(dve.tensor_scalar(r16[:], p16[:], 0.5, 1e-8, ALU.add, ALU.add))
                link(dve.tensor_scalar(r16[:], r16[:], 0.5, 2.0, ALU.max, ALU.min))
                link(dve.reciprocal(r16[:], r16[:]))
                link(dve.tensor_scalar(cshare[:], r16[:], tg[:, 2:3], 0.5, ALU.mult, ALU.mult))
                link(dve.tensor_tensor(croute[:], r16[:], p16[:], ALU.mult))
                link(dve.tensor_scalar(croute[:], croute[:], tg[:, 2:3], None, ALU.mult))
                link(dve.memset(run[:, 0], 0.0))
                link(dve.memset(ends[:, 0:1], 0.0))
                dve.wait_ge(s_cum, 1)
                total = bank[5][:, 0:NB * NE].rearrange("p (b e) -> p b e", b=NB)
                for b in range(NB):
                    link(dve.tensor_tensor(run[:, b + 1], run[:, b], total[:, b], ALU.add))
                link(dve.tensor_scalar(cnti[:], run[:, NB], float(P - 1), None, ALU.add))
                link(dve.tensor_scalar(cnti[:], cnti[:], P.bit_length() - 1, None, ALU.logical_shift_right))
                link(dve.tensor_copy(cnt[:], cnti[:]))
                for e in range(NE):
                    link(dve.tensor_tensor(ends[:, e + 1:e + 2], ends[:, e:e + 1], cnt[:, e:e + 1], ALU.add))
                link(dve.tensor_scalar(cnt[:], ends[:, 0:NE], float(P), None, ALU.mult))
                early = bank[4][:, 0:NB * NE].rearrange("p (b e) -> p b e", b=NB)
                link(dve.tensor_tensor(tmp[:], run[:, 0:NB], early, ALU.add))
                link(dve.tensor_tensor(tmp[:], tmp[:], cnt[:].unsqueeze(1).broadcast_to(wide), ALU.add))
                link(dve.tensor_tensor(tmp[:], tmp[:], one[:], ALU.mult))
                link(dve.tensor_reduce(pos[:], tmp[:], AX.X, ALU.add))
                link(dve.tensor_copy(posi[:], pos[:]))
                link(dve.tensor_copy(slot_f[:], slot_i[:]))
                link(dve.tensor_tensor(past[:], ends[0:1, 1:NE + 1].unsqueeze(1).broadcast_to([1, NT, NE]),
                                       slot_f[:].unsqueeze(2).broadcast_to([1, NT, NE]), ALU.is_le))
                link(dve.tensor_reduce(eidf[:], past[:], AX.X, ALU.add))
                link(dve.tensor_scalar(eid[:], eidf[:], float(NE - 1), None, ALU.min))

        act_s = sb("act_s", [P, 2, CH])
        hid = sb("hid", [P, FT * P])
        h2 = sb("h2", [P, 2, 2, FT * P], BF16)
        QLATE = 4 * (NE - 1)
        assert QLATE == NCH * FT

        def quarter(part, q):
            return we[:, part, bass.ds(q * QC, QC)]

        with nc.Block() as block:
            @block.sync
            def _(sp):
                def load(q, u):
                    sp.wait_ge(s_hi, q + 3)
                    sp.wait_ge(s_lo, q + 3)
                    sp.dma_start(stage[:, u], T["B_we"][bass.ds(q, 1)].rearrange("o p n -> (o p) n")).then_inc(
                        s_w[u], 16)

                with sp.Fori(0, 4 * NE - 1, 2) as q:
                    load(q, 0)
                    load(q + 1, 1)

            @block.gpsimd
            def _(pool):
                for j in range(NB):
                    pool.indirect_dma_start(
                        out=C["slots"].rearrange("t p n -> (t p) n"),
                        out_offset=bass.IndirectOffsetOnAxis(ap=posi[:, j:j + 1].bitcast(U32), axis=0),
                        in_=spare[j // HB][:, j % HB], in_offset=None).then_inc(s_scat, 16)
                pool.wait_ge(s_scat, 16 * NB)

            def m_rows(m):
                return P if m < FT - 1 else FLAST

            def before(n, m):
                return n if m == 0 else n - 1

            def rounds(eng, body):
                with eng.Fori(0, NCH) as c:
                    body(c)

            @block.scalar
            def _(act):
                def body(c):
                    for m in range(FT):
                        n, u, rows = c * FT + m, m % 2, m_rows(m)
                        act.wait_ge(s_h1, n + 1)
                        act.wait_ge(s_hd, before(n, m))
                        act.activation(act_s[0:rows, u], bank[u][0:rows], ACT.Silu).then_inc(s_si, 1)
                        act.wait_ge(s_hd, n + 1)
                        act.wait_ge(s_yp1, before(n, m))
                        act.activation(h2[0:rows, u, 0, 0:CH], hid[0:rows, 0:CH], ACT.Copy).then_inc(s_hh, 1)
                        high(n, u)

                def high(q, u):
                    act.wait_ge(s_w[u], q * 8 + (8 * (2 - u) + 32))
                    act.activation(quarter(0, q), stage[:, u], ACT.Copy).then_inc(s_hi, 1)

                rounds(act, body)
                act.wait_ge(s_scat, 16 * NB)
                for q in range(QLATE, 4 * NE):
                    high(q, q % 2)

            @block.tensor
            def _(pe):
                def hidden(c, m):
                    n, u, rows = c * FT + m, m % 2, m_rows(m)
                    for which, base, done in ((0, W1, s_h1), (1, W3, s_h3)):
                        if which == 0:
                            pe.wait_ge(s_si, before(n, m))
                        else:
                            pe.wait_ge(s_hd, before(n, m))
                        i = 0
                        for k in range(KT):
                            cols = slice(base + k * FF + m * P, base + k * FF + (m + 1) * P)
                            for a, b in ((0, 0), (0, 1), (1, 0)):
                                mm = pe.matmul(bank[2 * which + u][:], ws[:, a, cols],
                                               xT2[:, b, k, bass.ds(c * CH, CH)], start=(i == 0), stop=(i == 5))
                                i += 1
                        mm.then_inc(done, 1)

                def result(c, m):
                    n, u, rows = c * FT + m, m % 2, m_rows(m)
                    pe.wait_ge(s_hl, n + 1)
                    for t in range(CH // P):
                        if m == 0:
                            pe.wait_ge(s_ys, c * (CH // P))
                        for a, b in ((0, 0), (1, 0), (0, 1)):
                            mm = pe.matmul(bank[4 + t][:, 0:D], h2[0:rows, u, a, t * P:(t + 1) * P],
                                           ws[0:rows, b, W2 + m * D:W2 + (m + 1) * D],
                                           start=(m == 0 and a + b == 0), stop=(m == FT - 1 and b == 1))
                    mm.then_inc(s_yp1, 1)

                def body(c):
                    for m in range(FT):
                        hidden(c, m)
                        if m >= 1:
                            result(c, m - 1)
                    result(c, FT - 1)

                rounds(pe, body)

            @block.vector
            def _(dve):
                def low(q, u):
                    dve.wait_ge(s_hi, q + 5)
                    dve.tensor_tensor(quarter(1, q), stage[:, u], quarter(0, q), ALU.subtract).then_inc(s_lo, 1)

                def body(c):
                    for m in range(FT):
                        n, u, rows = c * FT + m, m % 2, m_rows(m)
                        dve.wait_ge(s_si, n + 1)
                        dve.wait_ge(s_h3, n + 1)
                        dve.wait_ge(s_hh, n)
                        dve.wait_ge(s_hl, n)
                        dve.tensor_tensor(hid[0:rows, 0:CH], act_s[0:rows, u], bank[2 + u][0:rows],
                                          ALU.mult).then_inc(s_hd, 1)
                        dve.wait_ge(s_hh, n + 1)
                        dve.tensor_tensor(h2[0:rows, u, 1, 0:CH], hid[0:rows, 0:CH], h2[0:rows, u, 0, 0:CH],
                                          ALU.subtract).then_inc(s_hl, 1)
                        low(n, u)
                    dve.wait_ge(s_yp1, c * FT + FT)
                    for t in range(CH // P):
                        j = c * (CH // P) + t
                        dve.scalar_tensor_tensor(row(xres, j), bank[4 + t][:, 0:D], cshare[:, bass.ds(j, 1)],
                                                 row(xres, j), ALU.mult, ALU.add).then_inc(s_ys, 1)

                rounds(dve, body)
                for q in range(QLATE, 4 * NE):
                    low(q, q % 2)

        xs = sb("xs", [P, 2, D])
        xh = sb("xh", [P, 2, 2, KT, P], BF16)
        ysb = sb("ysb", [P, 2, D])
        silu = act_s[:].rearrange("p u n -> p (u n)")
        with nc.Block() as block:
            @block.sync
            def _(sp):
                def load(t, u):
                    wait(sp, s_tp, t - 1)
                    sp.dma_start(xs[:, u], C["slots"][bass.ds(t, 1)].rearrange("o p n -> (o p) n")).then_inc(
                        s_xs[u], 16)

                def store(t, u):
                    sp.wait_ge(s_y, t + 1)
                    sp.dma_start(C["results"][bass.ds(t, 1)].rearrange("o p n -> (o p) n"), ysb[:, u]).then_inc(
                        s_yst[u], 16)

                load(0, 0)
                load(1, 1)
                with sp.Fori(0, NT - 3, 2) as t:
                    for u in range(2):
                        load(t + (2 + u), u)
                        store(t + u, u)
                for u in range(2):
                    store(NT - 2 + u, u)
                for u in range(2):
                    sp.wait_ge(s_yst[u], 16 * (NT // 2))

            def h_cols(m):
                return m // 4, slice(m % 4 * P, (m % 4 + 1) * P)

            @block.scalar
            def _(act):
                def split(t, u):
                    act.wait_ge(s_tp, t + 1)
                    wait(act, s_e3, t - 1)
                    act.activation(xh[:, u, 0], tile2(bank[0]), ACT.Copy).then_inc(s_th, 1)

                def silus(t, u):
                    wait(act, s_ed, t)
                    act.wait_ge(s_e1, t + 1)
                    for i, n in ((0, 512), (1, FT * P - 512)):
                        act.activation(silu[:, 512 * i:512 * i + n], bank[1 + i][:, 0:n], ACT.Silu).then_inc(s_es, 1)

                def high(t, u):
                    act.wait_ge(s_ed, t + 1)
                    wait(act, s_yp, t - 1)
                    act.activation(h2[:, u, 0], hid[:], ACT.Copy).then_inc(s_eh, 1)

                def result(t, u):
                    act.wait_ge(s_yp, t + 1)
                    if not isinstance(t, int) or t >= 2:
                        act.wait_ge(s_yst[u], t * 8 - 8 * u)
                    act.activation(ysb[:, u], bank[5 + u][:, 0:D], ACT.Copy).then_inc(s_y, 1)

                def first(t, u):
                    split(0, 0)
                    silus(0, 0)
                    split(1, 1)
                    high(0, 0)

                def step(t, u):
                    silus(t, u)
                    if not isinstance(t, int):
                        split(t + 1, 1 - u)
                    high(t, u)
                    result(t - 1, 1 - u)

                rotate(act, NT, first, step, lambda t, u: result(t - 1, 1 - u))

            @block.tensor
            def _(pe):
                def turn(t, u):
                    pe.wait_ge(s_xs[u], t * 8 + 8 * (2 - u))
                    wait(pe, s_th, t)
                    wait(pe, s_tl, t)
                    for k in range(KT):
                        mm = pe.transpose(bank[0][:, k * P:(k + 1) * P], xs[:, u, k * P:(k + 1) * P], ident[:])
                    mm.then_inc(s_tp, 1)

                def expert(t):
                    return pe.value_load(eid[0:1, bass.ds(t, 1)], min_val=0, max_val=NE - 1)

                def hidden(t, u):
                    e = expert(t)
                    pe.wait_ge(s_tl, t + 1)
                    for base, b0, done in ((W1, 1, s_e1), (W3, 3, s_e3)):
                        if base == W1:
                            wait(pe, s_es, 2 * t)
                        else:
                            wait(pe, s_ed, t)
                        for m in range(FT):
                            i = 0
                            bk, cols = h_cols(m)
                            for k in range(KT):
                                for a, b in ((0, 0), (0, 1), (1, 0)):
                                    mm = pe.matmul(bank[b0 + bk][:, cols],
                                                   we[:, a, bass.ds(e * WCOLS + (base + k * FF + m * P), P)],
                                                   xh[:, u, b, k], start=(i == 0), stop=(i == 5))
                                    i += 1
                        mm.then_inc(done, 1)

                def result(t, u):
                    e = expert(t)
                    pe.wait_ge(s_el, t + 1)
                    for m in range(FT):
                        rows = m_rows(m)
                        for a, b in ((0, 0), (1, 0), (0, 1)):
                            mm = pe.matmul(bank[5 + u][:, 0:D], h2[0:rows, u, a, m * P:(m + 1) * P],
                                           we[0:rows, b, bass.ds(e * WCOLS + (W2 + m * D), D)],
                                           start=(m == 0 and a + b == 0), stop=(m == FT - 1 and b == 1))
                    mm.then_inc(s_yp, 1)

                def first(t, u):
                    turn(0, 0)
                    hidden(0, 0)
                    turn(1, 1)

                def step(t, u):
                    hidden(t, u)
                    if not isinstance(t, int):
                        turn(t + 1, 1 - u)
                    result(t - 1, 1 - u)

                rotate(pe, NT, first, step, lambda t, u: result(t - 1, 1 - u))

            @block.vector
            def _(dve):
                def split(t, u):
                    dve.wait_ge(s_th, t + 1)
                    dve.tensor_tensor(xh[:, u, 1], tile2(bank[0]), xh[:, u, 0], ALU.subtract).then_inc(s_tl, 1)

                def product(t, u):
                    wait(dve, s_eh, t)
                    wait(dve, s_el, t)
                    dve.wait_ge(s_es, 2 * t + 2)
                    dve.wait_ge(s_e3, t + 1)
                    n = FT * P - 512
                    dve.tensor_tensor(hid[:, 0:512], silu[:, 0:512], bank[3][:], ALU.mult)
                    dve.tensor_tensor(hid[:, 512:512 + n], silu[:, 512:512 + n], bank[4][:, 0:n],
                                      ALU.mult).then_inc(s_ed, 1)

                def low(t, u):
                    dve.wait_ge(s_eh, t + 1)
                    dve.tensor_tensor(h2[:, u, 1], hid[:], h2[:, u, 0], ALU.subtract).then_inc(s_el, 1)

                def first(t, u):
                    split(0, 0)
                    product(0, 0)
                    split(1, 1)
                    low(0, 0)

                def step(t, u):
                    product(t, u)
                    if not isinstance(t, int):
                        split(t + 1, 1 - u)
                    low(t, u)

                rotate(dve, NT, first, step, lambda t, u: None)

        with nc.Block() as block:
            @block.gpsimd
            def _(pool):
                for j in range(NB):
                    pool.indirect_dma_start(
                        out=spare[j // HB][:, j % HB], out_offset=None,
                        in_=C["results"].rearrange("t p n -> (t p) n"),
                        in_offset=bass.IndirectOffsetOnAxis(ap=posi[:, j:j + 1].bitcast(U32), axis=0),
                    ).then_inc(s_yg[j], 16)

            @block.vector
            def _(dve):
                for j in range(NB):
                    dve.wait_ge(s_yg[j], 16)
                    dve.scalar_tensor_tensor(xres[:, j], spare[j // HB][:, j % HB], croute[:, j:j + 1], xres[:, j],
                                             ALU.mult, ALU.add).then_inc(s_x2, 1)
                for j in range(NB):
                    dve.wait_ge(s_x2, j + 1)
                    dve.bn_stats(C["bstats"][:, j], xres[:, j]).then_inc(s_bs, 1)


def stage_resampler(nc, T, C, tag="C"):
    xres, ident, mv, rstd, tg, half = (C[k] for k in ("xres", "ident", "mv", "rstd", "tg", "half"))
    with ExitStack() as ctx:
        def sb(name, shape, dt=F32):
            return ctx.enter_context(nc.sbuf_tensor(tag + name, shape, dt))

        def sem(name):
            return nc.alloc_semaphore(name=tag + name)

        NK = 2 * P
        INNER = H1 * DH1
        G = 4
        wq = sb("wq", [P, 2, KT, INNER], BF16)
        wk = sb("wk", [P, 2, KT, INNER], BF16)
        wv = sb("wv", [P, 2, KT, INNER], BF16)
        wo = sb("wo", [P, 2, INNER // P, D], BF16)
        weights = (wq, wk, wv, wo)
        stage = sb("stage", [P, 2, KT * INNER])
        gb = sb("gb", [P, 2, 2, KT])
        cx = sb("cx", [P, NB, D])
        lat = sb("lat", [P, NB, D])
        st2 = sb("st2", [P, 2, NB, 6])
        mv2 = sb("mv2", [P, 2, NB, 2])
        var2 = sb("var2", [P, 2, NB])
        rstd2 = sb("rstd2", [P, 2, NB])
        xc = sb("xc", [P, 2, D])
        kvf = sb("kvf", [P, KT, NK])
        kv2 = sb("kv2", [P, 2, 2, KT, NK], BF16)
        qT = sb("qT", [P, 2, H1 // 2, P])
        kT = sb("kT", [P, 2, H1 // 2, NK])
        v1 = sb("v1", [P, 2, 2, H1, DH1 + 1])
        E = sb("E", [P, 2, 4, NK])
        PT = sb("PT", [P, 2, 4, 2, P])
        mx = sb("mx", [P, 2, 4])
        rs = sb("rs", [P, 4])
        On = sb("On", [P, INNER])
        OT = sb("OT", [P, 2, INNER // P, P], BF16)

        pS = [ctx.enter_context(nc.psum_tensor(f"{tag}pS{i}", [P, 4, NK], F32)) for i in range(2)]
        pF = ctx.enter_context(nc.psum_tensor(f"{tag}pF", [P, 512], F32))
        pT = [ctx.enter_context(nc.psum_tensor(f"{tag}pT{i}", [P, 4, P], F32)) for i in range(2)]
        pO = ctx.enter_context(nc.psum_tensor(f"{tag}pO", [P, 512], F32))
        psO = pO[:, 0:4 * (DH1 + 1)].rearrange("p (h d) -> p h d", h=4)

        s_w = [sem(f"w_in{u}") for u in range(2)]
        s_gb = sem("scales_in")
        s_cx = sem("ctx_in")
        s_hi = sem("w_high")
        s_lo = sem("w_low")
        s_one = sem("ones_ready")
        s_st = sem("ctx_stats")
        s_lat = sem("lat_normed")
        s_ls = sem("lat_stats")
        s_mv2 = sem("mean_var2")
        s_ve2 = sem("var_eps2")
        s_rs2 = sem("rstd2_ready")
        s_xc = sem("rows_normed")
        s_Tp = sem("rowsT_in_psum")
        s_aff = sem("rowsT_scaled")
        s_kvh = sem("kv_input_high")
        s_kvl = sem("kv_input_low")
        s_qp = sem("q_in_psum")
        s_q = sem("q")
        s_kp = sem("k_in_psum")
        s_k = sem("k")
        s_vp = sem("v_in_psum")
        s_v = sem("v")
        s_S = sem("scores")
        s_mx = sem("maxima")
        s_sub = sem("shifted")
        s_E = sem("exps")
        s_PTp = sem("PT_in_psum")
        s_PT = sem("PT")
        s_O = sem("O_in_psum")
        s_rs = sem("recip_sums")
        s_On = sem("O_normed")
        s_OTp = sem("OT_in_psum")
        s_OTh = sem("OT_high")
        s_OTl = sem("OT_low")
        s_y = sem("y_in_psum")
        s_x = sem("x_new")
        s_bs = sem("bn_stats")

        stats_vector, stats_gpsimd, s_rstd = norm_stats(nc, C, tag)

        with nc.Block() as block:
            @block.sync
            def _(sp):
                sp.dma_start(gb[:], T["C_gb"]).then_inc(s_gb, 16)
                sp.dma_start(cx[:], T["ctx"]).then_inc(s_cx, 16)
                for i in range(4):
                    if i >= 2:
                        sp.wait_ge(s_hi, i - 1)
                        sp.wait_ge(s_lo, i - 1)
                    sp.dma_start(stage[:, i % 2], T["C_w"][i]).then_inc(s_w[i % 2], 16)
                sp.wait_ge(s_gb, 16)

            def parts(i):
                return (weights[i][:, part].rearrange("p k n -> p (k n)") for part in range(2))

            @block.gpsimd
            def _(pool):
                stats_gpsimd(pool)
                pool.memset(v1[:, :, :, :, DH1:DH1 + 1], 1.0).then_inc(s_one, 1)
                pool.wait_ge(s_mv2, 2 * NB)
                for i in range(2):
                    pool.tensor_scalar(var2[:, i], mv2[:, i, :, 1], EPS, None, ALU.add).then_inc(s_ve2, 1)
                pool.wait_ge(s_ve2, 2)
                for i in range(2):
                    pool.tensor_tensor(rstd2[:, i], var2[:, i], half[:], ALU.pow).then_inc(s_rs2, 1)

            @block.scalar
            def _(act):
                for i in range(4):
                    hi, lo = parts(i)
                    act.wait_ge(s_w[i % 2], 16 * (i // 2 + 1))
                    act.activation(hi, stage[:, i % 2], ACT.Copy).then_inc(s_hi, 1)

            @block.vector
            def _(dve):
                stats_vector(dve)
                dve.wait_ge(s_cx, 16)
                for b in range(NB):
                    dve.bn_stats(st2[:, 0, b], cx[:, b]).then_inc(s_st, 1)
                dve.wait_ge(s_rstd, 1)
                for b in range(NB):
                    dve.tensor_scalar(lat[:, b], xres[:, b], mv[:, b, 0:1], rstd[:, b:b + 1],
                                      ALU.subtract, ALU.mult).then_inc(s_lat, 1)
                for b in range(NB):
                    dve.wait_ge(s_lat, b + 1)
                    dve.bn_stats(st2[:, 1, b], lat[:, b]).then_inc(s_ls, 1)
                for i, s in ((0, s_st), (1, s_ls)):
                    dve.wait_ge(s, NB)
                    for b in range(NB):
                        dve.bn_aggr(mv2[:, i, b], st2[:, i, b]).then_inc(s_mv2, 1)
                for i in range(4):
                    hi, lo = parts(i)
                    dve.wait_ge(s_hi, i + 1)
                    dve.tensor_tensor(lo, stage[:, i % 2], hi, ALU.subtract).then_inc(s_lo, 1)

        def heads_of(ap, g):
            return ap[:, 4 * g:4 * g + 4, :].rearrange("p (n r) d -> p r n d", r=2)

        with nc.Block() as block:
            def interleaved(eng, F, A):
                def step(b, u):
                    run(b, u, True, True)

                def run(b, u, f, a):
                    for kind, what, i in ORDER:
                        if kind == "F" and f and what in F:
                            F[what](b, u, i)
                        if kind == "A" and a and what in A:
                            A[what](b - 1, 1 - u, i)

                rotate(eng, NB, lambda b, u: run(b, u, True, False), step, lambda b, u: run(b, u, False, True))

            @block.scalar
            def _(act):
                def kv_high(b, u, i):
                    act.wait_ge(s_aff, 4 * b + 4)
                    act.activation(kv2[:, u, 0], kvf[:], ACT.Copy).then_inc(s_kvh, 1)

                def q(b, u, i):
                    act.wait_ge(s_qp, 2 * b + i + 1)
                    act.activation(qT[:, u, 4 * i:4 * i + 4].rearrange("p m t -> p (m t)"), pF[:], ACT.Copy
                                   ).then_inc(s_q, 1)

                def k(b, u, i):
                    act.wait_ge(s_kp, 4 * b + i + 1)
                    act.activation(kT[:, u, 2 * i:2 * i + 2].rearrange("p m t -> p (m t)"), pF[:], ACT.Copy
                                   ).then_inc(s_k, 1)

                def exp(b, u, g):
                    act.wait_ge(s_sub, 4 * b + g + 1)
                    act.activation(E[:, g % 2], E[:, g % 2], ACT.Exp, scale=DH1 ** -0.5).then_inc(s_E, 1)

                def turned(b, u, g):
                    if g >= 2:
                        act.wait_ge(s_O, 4 * b + g - 1)
                    for r in range(2):
                        act.wait_ge(s_PTp, 8 * b + 2 * g + r + 1)
                        act.activation(PT[:, g % 2, 2 * r:2 * r + 2].rearrange("p n k t -> p (n k) t"), pT[r][:],
                                       ACT.Copy).then_inc(s_PT, 1)

                def o_high(b, u, g):
                    act.wait_ge(s_OTp, 4 * b + g + 1)
                    wait(act, s_y, b)
                    act.activation(OT[:, 0, 2 * g:2 * g + 2].rearrange("p m t -> p (m t)"), pO[:, 0:2 * P],
                                   ACT.Copy).then_inc(s_OTh, 1)

                interleaved(act, {"T": kv_high, "q": q, "k": k},
                            {"S": lambda b, u, g: None, "exp": exp, "PT": turned, "OT": o_high})

            @block.tensor
            def _(pe):
                pe.wait_ge(s_one, 1)

                def turn(b, u, i):
                    pe.wait_ge(s_xc, 2 * b + 2)
                    wait(pe, s_v, 4 * b)
                    for src in range(2):
                        for k in range(KT):
                            mm = pe.transpose(pF[:, (2 * k + src) * P:(2 * k + src + 1) * P],
                                              xc[:, src, k * P:(k + 1) * P], ident[:])
                    mm.then_inc(s_Tp, 1)

                def product(out, lhs, rhs, done=None):
                    i = 0
                    for k in range(KT):
                        for a, c in ((0, 0), (0, 1), (1, 0)):
                            mm = pe.matmul(out, lhs(a, k), rhs(c, k), start=(i == 0), stop=(i == 3 * KT - 1))
                            i += 1
                    return mm

                def q(b, u, i):
                    if i == 0:
                        pe.wait_ge(s_kvl, b + 1)
                    else:
                        pe.wait_ge(s_q, 2 * b + 1)
                    for m in range(4 * i, 4 * i + 4):
                        mm = product(pF[:, m % 4 * P:(m % 4 + 1) * P], lambda a, k: wq[:, a, k, m * P:(m + 1) * P],
                                     lambda c, k: kv2[:, u, c, k, P:NK])
                    mm.then_inc(s_qp, 1)

                def k_(b, u, i):
                    if i == 0:
                        pe.wait_ge(s_q, 2 * b + 2)
                    else:
                        pe.wait_ge(s_k, 4 * b + i)
                    for m in range(2 * i, 2 * i + 2):
                        mm = product(pF[:, m % 2 * NK:(m % 2 + 1) * NK],
                                     lambda a, k: wk[:, a, k, m * P:(m + 1) * P], lambda c, k: kv2[:, u, c, k])
                    mm.then_inc(s_kp, 1)

                def v(b, u, i):
                    if i == 0:
                        pe.wait_ge(s_k, 4 * b + 4)
                    else:
                        pe.wait_ge(s_v, 4 * b + i)
                    t, h = i // 2, i % 2
                    product(pF[:], lambda a, k: kv2[:, u, a, k, t * P:(t + 1) * P],
                            lambda c, k: wv[:, c, k, h * 512:(h + 1) * 512]).then_inc(s_vp, 1)

                def scores(b, u, g):
                    if g == 0:
                        pe.wait_ge(s_q, 2 * b + 2)
                        pe.wait_ge(s_k, 4 * b + 4)
                    if g >= 2:
                        pe.wait_ge(s_sub, 4 * b + g - 1)
                    for n in range(2):
                        for r in range(2):
                            rows = slice(DH1 * r, DH1 * (r + 1))
                            mm = pe.matmul(pS[g % 2][:, 2 * r + n], qT[rows, u, 2 * g + n], kT[rows, u, 2 * g + n],
                                           start=True, stop=True)
                    mm.then_inc(s_S, 1)

                def turn_p(b, u, g):
                    pe.wait_ge(s_E, 4 * b + g + 1)
                    for r in range(2):
                        if g >= 1:
                            pe.wait_ge(s_PT, 8 * b + 2 * g - 1 + r)
                        for n in range(2):
                            for k in range(2):
                                mm = pe.transpose(pT[r][:, 2 * n + k], E[:, g % 2, 2 * r + n, k * P:(k + 1) * P],
                                                  ident[:])
                        mm.then_inc(s_PTp, 1)

                def weigh(b, u, g):
                    pe.wait_ge(s_PT, 8 * b + 2 * g + 2)
                    if g == 0:
                        pe.wait_ge(s_v, 4 * b + 4)
                        wait(pe, s_x, b)
                    else:
                        pe.wait_ge(s_OTl, 4 * b + g)
                    for r in range(2):
                        for n in range(2):
                            h = 4 * g + 2 * n + r
                            for k in range(2):
                                mm = pe.matmul(psO[:, 2 * r + n], PT[:, g % 2, 2 * r + n, k], v1[:, u, k, h],
                                               start=(k == 0), stop=(k == 1))
                    mm.then_inc(s_O, 1)

                def turn_o(b, u, g):
                    pe.wait_ge(s_On, 4 * b + g + 1)
                    for m in range(2):
                        mm = pe.transpose(pO[:, m * P:(m + 1) * P], On[:, (2 * g + m) * P:(2 * g + m + 1) * P], ident[:])
                    mm.then_inc(s_OTp, 1)

                def result(b, u, i):
                    pe.wait_ge(s_OTl, 4 * b + 4)
                    n = INNER // P
                    for m in range(n):
                        for a, c in ((0, 0), (1, 0), (0, 1)):
                            mm = pe.matmul(pO[:, 0:D], OT[:, a, m], wo[:, c, m], start=(m == 0 and a + c == 0),
                                           stop=(m == n - 1 and c == 1))
                    mm.then_inc(s_y, 1)

                interleaved(pe, {"T": turn, "q": q, "k": k_, "v": v},
                            {"S": scores, "PT": turn_p, "PV": weigh, "OT": turn_o, "y": result})

            @block.vector
            def _(dve):
                def norm(b, u, i):
                    for src, rows in ((0, cx), (1, lat)):
                        m = mv2[:, src, bass.ds(b, 1), 0:1].rearrange("p o n -> p (o n)")
                        dve.tensor_scalar(xc[:, src], row(rows, b), m, rstd2[:, src, bass.ds(b, 1)],
                                          ALU.subtract, ALU.mult).then_inc(s_xc, 1)

                def scale(b, u, i):
                    dve.wait_ge(s_Tp, b + 1)
                    wait(dve, s_kvh, b)
                    wait(dve, s_kvl, b)
                    for src in range(2):
                        for k in range(KT):
                            dve.tensor_scalar(kvf[:, k, src * P:(src + 1) * P],
                                              pF[:, (2 * k + src) * P:(2 * k + src + 1) * P],
                                              gb[:, src, 0, k:k + 1], gb[:, src, 1, k:k + 1],
                                              ALU.mult, ALU.add).then_inc(s_aff, 1)
                    dve.wait_ge(s_kvh, b + 1)
                    dve.tensor_tensor(kv2[:, u, 1], kvf[:], kv2[:, u, 0], ALU.subtract).then_inc(s_kvl, 1)

                def norm_next(b, u, i):
                    if not isinstance(b, int):
                        norm(b + 1, 1 - u, 0)
                    elif b == 0:
                        norm(1, 1, 0)

                def v(b, u, i):
                    dve.wait_ge(s_vp, 4 * b + i + 1)
                    t, h = i // 2, i % 2
                    dve.tensor_copy(v1[:, u, t, 8 * h:8 * h + 8, 0:DH1], pF[:].rearrange("p (h d) -> p h d", d=DH1)
                                    ).then_inc(s_v, 1)

                def shift(b, u, g):
                    dve.wait_ge(s_S, 4 * b + g + 1)
                    if g >= 2:
                        dve.wait_ge(s_sub, 4 * b + g - 1)
                    else:
                        wait(dve, s_x, b)
                    dve.tensor_reduce(mx[:, g % 2], pS[g % 2][:], AX.X, ALU.max).then_inc(s_mx, 1)
                    dve.wait_ge(s_mx, 4 * b + g + 1)
                    if g >= 2:
                        dve.wait_ge(s_PTp, 8 * b + 2 * g - 2)
                    dve.tensor_tensor(E[:, g % 2], pS[g % 2][:], mx[:, g % 2].unsqueeze(2).broadcast_to([P, 4, NK]),
                                      ALU.subtract).then_inc(s_sub, 1)

                def o_norm(b, u, g):
                    dve.wait_ge(s_O, 4 * b + g + 1)
                    dve.reciprocal(rs[:], psO[:, :, DH1]).then_inc(s_rs, 1)
                    dve.wait_ge(s_rs, 4 * b + g + 1)
                    on = heads_of(On[:].rearrange("p (h d) -> p h d", d=DH1), g)
                    for r in range(2):
                        ins = dve.tensor_tensor(on[:, r], psO[:, 2 * r:2 * r + 2, 0:DH1],
                                                rs[:, 2 * r:2 * r + 2].unsqueeze(2).broadcast_to([P, 2, DH1]),
                                                ALU.mult)
                    ins.then_inc(s_On, 1)

                def o_low(b, u, g):
                    dve.wait_ge(s_OTh, 4 * b + g + 1)
                    dve.tensor_tensor(OT[:, 1, 2 * g:2 * g + 2].rearrange("p m t -> p (m t)"), pO[:, 0:2 * P],
                                      OT[:, 0, 2 * g:2 * g + 2].rearrange("p m t -> p (m t)"),
                                      ALU.subtract).then_inc(s_OTl, 1)

                def add(b, u, i):
                    dve.wait_ge(s_y, b + 1)
                    dve.scalar_tensor_tensor(row(xres, b), pO[:, 0:D], tg[:, 1:2], row(xres, b), ALU.mult,
                                             ALU.add).then_inc(s_x, 1)

                norm(0, 0, 0)
                interleaved(dve, {"T": scale, "norm": norm_next, "v": v},
                            {"exp": shift, "PV": o_norm, "OT": o_low, "y": add})


ORDER = [("F", "T", 0), ("A", "S", 0), ("F", "q", 0), ("A", "S", 1), ("A", "exp", 0), ("F", "q", 1),
         ("A", "PT", 0), ("F", "k", 0), ("A", "exp", 1), ("A", "PV", 0), ("F", "k", 1), ("A", "S", 2),
         ("A", "OT", 0), ("A", "PT", 1), ("F", "k", 2), ("A", "exp", 2), ("A", "PV", 1), ("F", "k", 3),
         ("A", "S", 3), ("A", "OT", 1), ("A", "PT", 2), ("F", "norm", 0), ("F", "v", 0), ("A", "exp", 3),
         ("A", "PV", 2), ("F", "v", 1), ("A", "OT", 2), ("A", "PT", 3), ("F", "v", 2), ("A", "PV", 3),
         ("A", "OT", 3), ("F", "v", 3), ("A", "y", 0)]


def stage_linear(nc, T, C, out, tag="D"):
    xres, mv, rstd, tg, ident = (C[k] for k in ("xres", "mv", "rstd", "tg", "ident"))
    FP8_MAX = 448.0
    with ExitStack() as ctx:
        def sb(name, shape, dt=F32):
            return ctx.enter_context(nc.sbuf_tensor(tag + name, shape, dt))

        def sem(name):
            return nc.alloc_semaphore(name=tag + name)

        xn = sb("xn", [P, NB, D])
        w = sb("w", [P, KT, D])
        bias = sb("bias", [P, D])
        xq = sb("xq", [P, NB, D], BF16)
        wq = sb("wq", [P, KT, D], BF16)
        size = sb("size", [P, 2, 4 * D])
        sz = sb("sz", [P, 2, 4 * D])
        am = sb("am", [P, 2])
        amr = sb("amr", [P, 2])
        sc = sb("sc", [P, 2])
        back = sb("back", [P, 3])
        amb = sb("amb", [P, NB])
        idb = sb("idb", [P, P], BF16)
        xT = sb("xT", [P, 2, KT, P], BF16)
        yf = sb("yf", [P, 2, D])
        yb = sb("yb", [P, 2, D], BF16)
        fin = sb("fin", [P, 2, D])
        pT = [ctx.enter_context(nc.psum_tensor(f"{tag}pT{i}", [P, KT, P], BF16)) for i in range(2)]
        pY = [ctx.enter_context(nc.psum_tensor(f"{tag}pY{i}", [P, 512], F32)) for i in range(2)]

        s_in = sem("weights_in")
        s_id = sem("identity")
        s_bs = sem("bn_stats")
        s_xn = sem("xn")
        s_am = sem("sizes")
        s_amm = sem("greatest_of_partition")
        s_amr = sem("greatest")
        s_c = sem("scale_steps")
        s_q = sem("rounding_steps")
        s_xq = sem("x_rounded")
        s_wq = sem("w_rounded")
        s_Tp = sem("xT_in_psum")
        s_T = sem("xT")
        s_y = sem("y_in_psum")
        s_yf = sem("y_scaled")
        s_yb = sem("y_rounded")
        s_fin = sem("out_ready")
        s_out = [sem(f"out_stored{u}") for u in range(2)]

        stats_vector, stats_gpsimd, s_rstd = norm_stats(nc, C, tag)
        RW = 4 * D

        with nc.Block() as block:
            @block.sync
            def _(sp):
                sp.dma_start(w[:], T["D_w"]).then_inc(s_in, 16)
                sp.dma_start(bias[:], T["D_bias"].partition_broadcast(P)).then_inc(s_in, 16)
                for b in range(NB):
                    sp.wait_ge(s_fin, b + 1)
                    sp.dma_start(out[:, b], fin[:, b % 2]).then_inc(s_out[b % 2], 16)
                for u in range(2):
                    sp.wait_ge(s_out[u], 16 * NB // 2)

            @block.gpsimd
            def _(pool):
                pool.tensor_copy(idb[:], ident[:]).then_inc(s_id, 1)
                pool.wait_ge(s_bs, NB)
                stats_gpsimd(pool)
                pool.wait_ge(s_amm, 2)
                pool.partition_all_reduce(amr[:], am[:], P, bass.bass_isa.ReduceOp.max).then_inc(s_amr, 1)

            @block.scalar
            def _(act):
                def round_y(b):
                    act.wait_ge(s_yf, b + 1)
                    act.activation(yb[:, b % 2], yf[:, b % 2], ACT.Copy).then_inc(s_yb, 1)

                for b in range(NB):
                    u = b % 2
                    act.wait_ge(s_Tp, b + 1)
                    if b >= 2:
                        act.wait_ge(s_y, b - 1)
                    act.activation(xT[:, u], pT[u][:], ACT.Copy).then_inc(s_T, 1)
                    if b >= 1:
                        round_y(b - 1)
                round_y(NB - 1)

            @block.tensor
            def _(pe):
                pe.wait_ge(s_id, 1)
                pe.wait_ge(s_wq, 1)

                def turn(b):
                    u = b % 2
                    pe.wait_ge(s_xq, b // 4 + 1)
                    if b >= 2:
                        pe.wait_ge(s_T, b - 1)
                    for k in range(KT):
                        mm = pe.transpose(pT[u][:, k], xq[:, b, k * P:(k + 1) * P], idb[:])
                    mm.then_inc(s_Tp, 1)

                turn(0)
                for b in range(NB):
                    u = b % 2
                    if b + 1 < NB:
                        turn(b + 1)
                    pe.wait_ge(s_T, b + 1)
                    if b >= 2:
                        pe.wait_ge(s_yf, b - 1)
                    for k in range(KT):
                        mm = pe.matmul(pY[u][:, 0:D], xT[:, u, k], wq[:, k], start=(k == 0), stop=(k == KT - 1))
                    mm.then_inc(s_y, 1)

            @block.vector
            def _(dve):
                nc_, nq = [0], [0]

                def link(ins):
                    nc_[0] += 1
                    ins.then_inc(s_c, 1)
                    dve.wait_ge(s_c, nc_[0])

                for b in range(NB):
                    dve.bn_stats(C["bstats"][:, b], xres[:, b]).then_inc(s_bs, 1)
                dve.wait_ge(s_bs, NB)
                stats_vector(dve)
                dve.wait_ge(s_in, 32)
                dve.tensor_reduce(am[:, 1:2], w[:].rearrange("p k n -> p (k n)"), AX.X, ALU.max,
                                  apply_absolute_value=True).then_inc(s_amm, 1)
                dve.wait_ge(s_rstd, 1)
                for b in range(NB):
                    dve.tensor_scalar(xn[:, b], xres[:, b], mv[:, b, 0:1], rstd[:, b:b + 1], ALU.subtract,
                                      ALU.mult).then_inc(s_xn, 1)
                for b in range(NB):
                    dve.wait_ge(s_xn, b + 1)
                    dve.tensor_reduce(amb[:, b:b + 1], xn[:, b], AX.X, ALU.max,
                                      apply_absolute_value=True).then_inc(s_am, 1)
                dve.wait_ge(s_am, NB)
                dve.tensor_reduce(am[:, 0:1], amb[:], AX.X, ALU.max).then_inc(s_amm, 1)
                dve.wait_ge(s_amr, 1)
                link(dve.tensor_scalar(sc[:], amr[:], 1e-12, None, ALU.max))
                link(dve.reciprocal(sc[:], sc[:]))
                link(dve.tensor_scalar(sc[:], sc[:], FP8_MAX, FP8_MAX, ALU.mult, ALU.min))
                link(dve.reciprocal(back[:, 0:2], sc[:]))
                link(dve.tensor_tensor(back[:, 2:3], back[:, 0:1], back[:, 1:2], ALU.mult))

                def step(ins):
                    nq[0] += 1
                    ins.then_inc(s_q, 1)
                    return nq[0]

                def to_fp8(dst, src, which, u, done):
                    n = src.shape[-1]
                    s, z = size[:, u, 0:n], sz[:, u, 0:n]
                    dve.wait_ge(s_q, step(dve.tensor_scalar(z, src, sc[:, which:which + 1], FP8_MAX, ALU.mult, ALU.min)))
                    dve.wait_ge(s_q, step(dve.tensor_scalar(z, z, -FP8_MAX, None, ALU.max)))
                    dve.wait_ge(s_q, step(dve.tensor_scalar(s.bitcast(U32), z.bitcast(U32), 0x7F800000, None,
                                                            ALU.bitwise_and)))
                    dve.wait_ge(s_q, step(dve.tensor_scalar(s, s, 2.0 ** -6, 1.5 * 2.0 ** 20, ALU.max, ALU.mult)))
                    dve.wait_ge(s_q, step(dve.tensor_tensor(z, z, s, ALU.add)))
                    dve.tensor_tensor(dst, z, s, ALU.subtract).then_inc(done, 1)

                to_fp8(wq[:].rearrange("p k n -> p (k n)"), w[:].rearrange("p k n -> p (k n)"), 1, 0, s_wq)
                for r in range(4):
                    if r >= 1:
                        dve.wait_ge(s_xq, r)
                    to_fp8(xq[:, 4 * r:4 * r + 4].rearrange("p b n -> p (b n)"),
                           xn[:, 4 * r:4 * r + 4].rearrange("p b n -> p (b n)"), 0, (r + 1) % 2, s_xq)

                def add(b):
                    u = b % 2
                    dve.wait_ge(s_yb, b + 1)
                    if b >= 2:
                        dve.wait_ge(s_out[u], 16 * (b // 2))
                    dve.scalar_tensor_tensor(fin[:, u], yb[:, u], tg[:, 3:4], xres[:, b], ALU.mult,
                                             ALU.add).then_inc(s_fin, 1)

                for b in range(NB):
                    u = b % 2
                    dve.wait_ge(s_y, b + 1)
                    if b >= 2:
                        dve.wait_ge(s_yb, b - 1)
                    dve.scalar_tensor_tensor(yf[:, u], pY[u][:, 0:D], back[:, 2:3], bias[:], ALU.mult,
                                             ALU.add).then_inc(s_yf, 1)
                    if b >= 1:
                        add(b - 1)
                add(NB - 1)


def build(nc, T, out):
    with ExitStack() as ctx:
        def sb(name, shape, dt=F32):
            return ctx.enter_context(nc.sbuf_tensor(name, shape, dt))

        def sem(name):
            return ctx.enter_context(nc.semaphore(name))

        C = {}
        C["xres"] = xres = sb("xres", [P, NB, D])
        C["ident"] = ident = sb("ident", [P, P])
        C["first"] = first = sb("first", [P, 1])
        C["rest"] = rest = sb("rest", [P, 1])
        C["mv"] = mv = sb("mv", [P, NB, 2])
        C["rstd"] = rstd = sb("rstd", [P, NB])
        C["tg"] = tg = sb("tg", [P, 4])
        C["half"] = half = sb("half", [P, NB])
        C["vare"] = vare = sb("vare", [P, NB])
        zero = sb("zero", [P, D])
        C["bstats"] = stats0 = sb("bstats", [P, NB, 6])
        C["s_ident"] = s_ident = sem("ident_ready")
        C["s_masks"] = s_masks = sem("masks_ready")
        C["s_tanh"] = s_tanh = sem("tanh_ready")
        C["s_rstd_A"] = s_rstd = sem("rstd_ready")
        C["slots"] = nc.dram_tensor(
            "slots", (NT, P, D), F32, kind="Internal").ap()
        C["results"] = nc.dram_tensor("results", (NT, P, D), F32, kind="Internal").ap()
        s_zm = sem("zeros_made")
        s_z = sem("slots_zeroed")
        s_x = [sem(f"x_in{q}") for q in range(4)]
        s_g = sem("gates_in")
        s_m = sem("setup_memsets")
        s_st = sem("setup_stats")
        s_mv0 = sem("setup_mean_var")
        s_p = sem("setup_var_eps")

        with nc.Block() as block:
            @block.sync
            def _(sp):
                sp.dma_start(tg[:], T["gates"].partition_broadcast(P)).then_inc(s_g, 16)
                for q in range(4):
                    sp.dma_start(xres[:, 4 * q:4 * q + 4], T["x"][:, 4 * q:4 * q + 4]).then_inc(s_x[q], 16)
                sp.wait_ge(s_zm, 1)
                for t in range(NT):
                    sp.dma_start(C["slots"][t], zero[:]).then_inc(s_z, 16)
                sp.wait_ge(s_z, 16 * NT)

            @block.scalar
            def _(act):
                act.wait_ge(s_g, 16)
                act.activation(tg[:], tg[:], ACT.Tanh).then_inc(s_tanh, 1)

            @block.gpsimd
            def _(pool):
                pool.memset(zero[:], 0.0).then_inc(s_zm, 1)
                pool.memset(ident[:], 0.0).then_inc(s_m, 1)
                pool.memset(half[:], -0.5).then_inc(s_m, 1)
                pool.memset(first[:], 0.0).then_inc(s_m, 1)
                pool.memset(rest[:], 0.0).then_inc(s_m, 1)
                pool.wait_ge(s_m, 4)
                pool.affine_select(out=ident[:], in_=ident[:], compare_op=ALU.not_equal, fill=1.0, base=0,
                                   pattern=[[-1, P]], channel_multiplier=1).then_inc(s_ident, 1)
                pool.affine_select(out=first[:], in_=first[:], compare_op=ALU.not_equal, fill=1.0, base=0,
                                   pattern=[[0, 1]], channel_multiplier=1).then_inc(s_masks, 1)
                pool.affine_select(out=rest[:], in_=rest[:], compare_op=ALU.is_equal, fill=1.0, base=0,
                                   pattern=[[0, 1]], channel_multiplier=1).then_inc(s_masks, 1)
                pool.wait_ge(s_mv0, NB)
                pool.tensor_scalar(vare[:], mv[:, :, 1], EPS, None, ALU.add).then_inc(s_p, 1)
                pool.wait_ge(s_p, 1)
                pool.tensor_tensor(rstd[:], vare[:], half[:], ALU.pow).then_inc(s_rstd, 1)

            @block.vector
            def _(dve):
                for b in range(NB):
                    if b % 4 == 0:
                        dve.wait_ge(s_x[b // 4], 16)
                    dve.bn_stats(stats0[:, b], xres[:, b]).then_inc(s_st, 1)
                for b in range(NB):
                    dve.wait_ge(s_st, b + 1)
                    dve.bn_aggr(mv[:, b], stats0[:, b]).then_inc(s_mv0, 1)

        with nc.cleanup_on_exit():
            stage_rope_attention(nc, T, C)
        with nc.cleanup_on_exit():
            stage_experts(nc, T, C)
        with nc.cleanup_on_exit():
            stage_resampler(nc, T, C)
        stage_linear(nc, T, C, out)


def kernel(**inputs):
    import concourse.bacc as bacc
    from concourse.bass_utils import run_bass_kernel_spmd

    a = {k: np.asarray(v) for k, v in inputs.items()}

    def kmajor(w):
        return np.ascontiguousarray(w.T.reshape(KT, P, -1).transpose(1, 0, 2))

    def expert(w1, w3, w2):
        w2t = np.zeros((FT * P, D), w2.dtype)
        w2t[:FF] = w2.T
        parts = [kmajor(w1).reshape(P, -1), kmajor(w3).reshape(P, -1),
                 w2t.reshape(FT, P, D).transpose(1, 0, 2).reshape(P, -1)]
        return np.concatenate(parts, axis=1).reshape(P, 4, QC).transpose(1, 0, 2)

    def outof(w):
        return w.reshape(-1, P, w.shape[1]).transpose(1, 0, 2).reshape(P, -1)

    def bypart(v):
        return v.reshape(KT, P).T

    wkv = a["L1_xattn_Wkv"]
    arrays = {
        "ctx": np.ascontiguousarray(a["ctx_1024"].transpose(1, 0, 2)),
        "C_w": np.stack([outof(a["L1_xattn_Wq"]), outof(wkv[:, :H1 * DH1]), outof(wkv[:, H1 * DH1:]),
                         outof(a["L1_xattn_Wout"])]),
        "C_gb": np.stack([np.stack([bypart(a["L1_xattn_ln_m_g"]), bypart(a["L1_xattn_ln_m_b"])], 1),
                          np.stack([bypart(a["L1_xattn_ln_l_g"]), bypart(a["L1_xattn_ln_l_b"])], 1)], 1),
        "D_w": kmajor(a["L1_ffn_weight"]),
        "D_bias": a["L1_ffn_bias"],
        "B_rw": kmajor(a["L0_ffn_router_w"]),
        "B_rb": a["L0_ffn_routing_bias"],
        "B_ws": np.ascontiguousarray(expert(a["L0_ffn_sw1"], a["L0_ffn_sw3"], a["L0_ffn_sw2"])),
        "B_we": np.concatenate([expert(a["L0_ffn_ew1"][e], a["L0_ffn_ew3"][e], a["L0_ffn_ew2"][e])
                                for e in range(NE)]),
        "x": np.ascontiguousarray(a["x"].transpose(1, 0, 2)),
        "ctxT": np.ascontiguousarray(a["ctx_1024"].transpose(0, 2, 1).reshape(NB, KT, P, P).transpose(0, 2, 1, 3)),
        "pos": np.ascontiguousarray(a["itok_BxSx2_0_63"].transpose(1, 0, 2)),
        "gates": np.concatenate([a["g_xattn"], a["g_ffn"]]),
        "A_wq": kmajor(a["L0_xattn_Wq"]),
        "A_wkv": kmajor(np.concatenate([a["L0_xattn_Wk"], a["L0_xattn_Wv"]])),
        "A_wp": kmajor(a["L0_xattn_Wp"]),
        "A_bias": np.concatenate([a["L0_xattn_bq"], a["L0_xattn_bk"], a["L0_xattn_bv"], a["L0_xattn_bp"]]),
    }
    nc = bacc.Bacc("TRN2", target_bir_lowering=False, num_devices=1)
    T = {n: nc.dram_tensor(f"in_{n}", v.shape, mybir.dt.from_np(v.dtype), kind="ExternalInput").ap()
         for n, v in arrays.items()}
    out = nc.dram_tensor("out", (P, NB, D), F32, kind="ExternalOutput").ap()
    build(nc, T, out)
    r = run_bass_kernel_spmd(nc, [{f"in_{n}": v for n, v in arrays.items()}], core_ids=[0])
    return np.ascontiguousarray(r.results[0]["out"].transpose(1, 0, 2))
```

```python
from contextlib import ExitStack

import numpy as np

import concourse.bass as bass
from concourse import mybir

F32 = mybir.dt.float32
BF16 = mybir.dt.bfloat16
I32 = mybir.dt.int32
U32 = mybir.dt.uint32
ALU = mybir.AluOpType
ACT = mybir.ActivationFunctionType
AX = mybir.AxisListType

P = 128
NB = 16
D = 256
KT = D // P
EPS = 1e-5

H0, DH0 = 16, 16
SLOT = 64
KSTACK = 3 * DH0
ROPE_BASE = 100.0
NFREQ = DH0 // 4
ANGLE_STEPS = 11 + NFREQ

NE = 7
FF = 704
FT = -(-FF // P)
FLAST = FF - (FT - 1) * P
W1, W3, W2 = 0, KT * FF, 2 * KT * FF
WCOLS = W2 + FT * D
QC = WCOLS // 4
NTOK = NB * P
NT = (NTOK + NE * (P - 1)) // P
CH = 512
NCH = NTOK // CH

H1, DH1 = 16, 64
SIGMOID_ONE = 25 * float(np.log(2))


def wait(eng, sem, value):
    if isinstance(value, int) and value <= 0:
        return
    eng.wait_ge(sem, value)


def rotate(eng, n, first, step, last):
    first(0, 0)
    step(1, 1)
    with eng.Fori(2, n - 3, 2) as i:
        step(i, 0)
        step(i + 1, 1)
    step(n - 2, 0)
    step(n - 1, 1)
    last(n, 0)


def ahead(b, n):
    return not isinstance(b, int) or b + 1 < n


def stage_rope_attention(nc, T, C, tag="A"):
    xres = C["xres"]
    with ExitStack() as ctx:
        def sb(name, shape, dt=F32):
            return ctx.enter_context(nc.sbuf_tensor(tag + name, shape, dt))

        def ps(name, shape, dt=F32):
            return ctx.enter_context(nc.psum_tensor(tag + name, shape, dt))

        def sem(name):
            return nc.alloc_semaphore(name=tag + name)

        wq = sb("wq", [P, KT, D])
        wkv = sb("wkv", [P, KT, 2 * D])
        wp = sb("wp", [P, KT, D])
        bias = sb("bias", [P, 4, D])
        xn = sb("xn", [P, 2, D])
        xnT = sb("xnT", [P, 2, KT, P])
        cT = sb("cT", [P, 2, KT, P])
        q3 = sb("q3", [P, H0, SLOT])
        k3 = sb("k3", [P, H0, SLOT])
        v1 = sb("v1", [P, 2, H0, DH0 + 1])
        qT = sb("qT", [P, 2, H0 // 2, P])
        kT = sb("kT", [P, 2, H0 // 2, P])
        qrot = sb("qrot", [P, H0, DH0])
        krot = sb("krot", [P, H0, DH0])
        E = sb("E", [P, H0, P])
        PT = sb("PT", [P, H0, P])
        mx = sb("mx", [P, H0])
        rs = sb("rs", [P, H0])
        On = sb("On", [P, D])
        OT = sb("OT", [P, KT, P])
        stats = sb("stats", [P, 6])
        xw = sb("xw", [P, D])
        cx = sb("cx", [P, NB, D])
        ctx_stats = sb("ctx_stats", [P, NB, 6])
        posf = sb("posf", [P, NB, 2])
        ang = sb("ang", [P, NB, 2, NFREQ])
        turns = sb("turns", [P, NB, 2, NFREQ])
        red = sb("red", [P, 3, NB, 2, NFREQ])
        sc = sb("sc", [P, 2, NB, 2, NFREQ])
        cosT = sb("cosT", [P, NB, 2, 2, NFREQ])
        sinT = sb("sinT", [P, NB, 2, 2, NFREQ])

        pS = [ps(f"pS{j}", [P, 4, P]) for j in range(4)]
        pT = [ps(f"pT{j}", [P, 4, P]) for j in range(2)]
        pKV = ps("pKV", [P, 2 * D])
        pQ = ps("pQ", [P, 2 * D])
        psQ = pQ[:, 0:D]
        psO = pQ[:, 0:H0 * (DH0 + 1)].rearrange("p (h d) -> p h d", h=H0)
        psY = pQ[:, 0:D]

        ident, first, rest, mv, rstd, tg = (C[k] for k in ("ident", "first", "rest", "mv", "rstd", "tg"))

        s_wkv = sem("kv_weights_in")
        s_w = sem("q_weights_and_biases_in")
        s_wp = sem("output_weights_in")
        s_ct = [sem(f"ctxT_in{u}") for u in range(2)]
        s_tab = sem("table_steps")
        s_sin = sem("sines")
        s_tabs = sem("tables_ready")
        s_one = sem("ones_ready")
        s_bpg = sem("gated_bias")
        s_xn = sem("xn")
        s_xTp = sem("xT_in_psum")
        s_xT = sem("xT")
        s_kvp = sem("kv_in_psum")
        s_qp = sem("q_in_psum")
        s_v = sem("v")
        s_kb = sem("k_biased")
        s_qb = sem("q_biased")
        s_krot = sem("k_rotated")
        s_qrot = sem("q_rotated")
        s_kcos = sem("k_cos")
        s_qcos = sem("q_cos")
        s_k3 = sem("k3_parts")
        s_q3 = sem("q3_parts")
        s_qTp = sem("qT_in_psum")
        s_qT = sem("qT_halves")
        s_kTp = sem("kT_in_psum")
        s_kT = sem("kT_halves")
        s_S = sem("scores")
        s_mx = sem("maxima")
        s_sub = sem("shifted")
        s_E = sem("exps")
        s_PTp = sem("PT_in_psum")
        s_PT = sem("PT")
        s_O = sem("O_in_psum")
        s_rs = sem("recip_sums")
        s_On = sem("O_normed")
        s_OTp = sem("OT_in_psum")
        s_OT = sem("OT")
        s_y = sem("y_in_psum")
        s_xb = sem("x_plus_bias")
        s_x1 = sem("x_new")
        s_bs = sem("bn_stats")
        s_keep = sem("x_and_stats_kept")
        s_bs0 = sem("first_bn_stats")
        s_cx = sem("ctx_in")
        s_cst = sem("ctx_bn_stats")
        s_cmv = sem("ctx_mean_var")
        bstats = C["bstats"]
        stats_vector, stats_gpsimd, s_rstd = norm_stats(nc, C, tag)

        def head_at(c):
            return 8 * (c // 8) + 2 * (c % 4) + (c // 4) % 2

        def heads(ap):
            return ap.rearrange("p (h d) -> p h d", h=H0)

        def halves(ap):
            return ap.rearrange("p h (a s f) -> p h a s f", a=2, s=2)

        def table(tab, b, half=None):
            if half is None:
                t = tab[:, bass.ds(b, 1), :, :, :].rearrange("p o a s f -> p o (a s f)")
                return t.broadcast_to([P, H0, DH0])
            t = tab[:, bass.ds(b, 1), :, half, :]
            return t.broadcast_to([P, H0, 2, NFREQ])

        with nc.Block() as block:
            @block.sync
            def _(sp):
                sp.dma_start(wkv[:], T["A_wkv"]).then_inc(s_wkv, 16)
                def load(b, u):
                    wait(sp, s_kvp, b - 1)
                    sp.dma_start(cT[:, u], T["ctxT"][bass.ds(b, 1)].rearrange("o p k t -> (o p) k t")
                                 ).then_inc(s_ct[u], 16)

                load(0, 0)
                sp.dma_start(wq[:], T["A_wq"]).then_inc(s_w, 16)
                sp.dma_start(bias[:].rearrange("p w n -> p (w n)"),
                             T["A_bias"].partition_broadcast(P)).then_inc(s_w, 16)
                for c in range(1, NB // GC):
                    bs = slice(GC * c, GC * (c + 1))
                    sp.dma_start(xres[:, bs], T["x"][:, bs]).then_inc(C["s_x"][c], 16)
                load(1, 1)
                sp.dma_start(wp[:], T["A_wp"]).then_inc(s_wp, 16)
                sp.dma_start(cx[:], T["ctx"]).then_inc(s_cx, 16)
                sp.wait_ge(C["s_zero"], 1)
                for t in range(NT):
                    sp.dma_start(C["slots"][t], C["zero"][:]).then_inc(C["s_zeroed"], 16)
                with sp.Fori(2, NB - 1, 2) as i:
                    load(i, 0)
                    load(i + 1, 1)

            @block.gpsimd
            def _(pool):
                pool.memset(v1[:, :, :, DH0:DH0 + 1], 1.0).then_inc(s_one, 1)
                pool.memset(q3[:, :, KSTACK:SLOT], 0.0).then_inc(s_one, 1)
                pool.wait_ge(s_w, 16 * 2)
                pool.wait_ge(C["s_tanh"], 1)
                pool.tensor_scalar(bias[:, 3, :], bias[:, 3, :], tg[:, 0:1], None, ALU.mult).then_inc(s_bpg, 1)
                pool.wait_ge(s_bpg, 1)
                stats_gpsimd(pool, 0)
                stats_gpsimd(pool, 1)
                pool.wait_ge(s_tabs, 1)

                def rope_k(b, u):
                    pool.wait_ge(s_kb, b + 1)
                    wait(pool, s_kTp, 2 * b)
                    kb = k3[:, :, KSTACK:SLOT]
                    pool.tensor_tensor(k3[:, :, 0:DH0], kb, table(cosT, b), ALU.mult).then_inc(s_kcos, 1)
                    for s in range(2):
                        pool.tensor_tensor(halves(krot[:])[:, :, :, s, :], halves(kb)[:, :, :, 1 - s, :],
                                           table(sinT, b, s), ALU.mult).then_inc(s_krot, 1)
                    pool.tensor_scalar(k3[:, :, DH0:2 * DH0], kb, first[:], None, ALU.mult).then_inc(s_k3, 1)
                    pool.tensor_scalar(k3[:, :, 2 * DH0:3 * DH0], kb, rest[:], None, ALU.mult).then_inc(s_k3, 1)
                    pool.wait_ge(s_kcos, b + 1)
                    pool.wait_ge(s_krot, 2 * b + 2)
                    pool.tensor_tensor(k3[:, :, 0:DH0], k3[:, :, 0:DH0], krot[:], ALU.add).then_inc(s_k3, 1)
                    pool.wait_ge(s_xn, b + 1)
                    x = xres[:, bass.ds(b, 1), :].rearrange("p o n -> p (o n)")
                    pool.tensor_tensor(x, x, bias[:, 3, :], ALU.add).then_inc(s_xb, 1)

                rope_k(0, 0)
                for c in range(2, NB // GC):
                    stats_gpsimd(pool, c)
                with pool.Fori(1, NB) as i:
                    rope_k(i, 0)

            @block.scalar
            def _(act):
                act.wait_ge(s_tab, ANGLE_STEPS)
                act.activation(sc[:, 0], red[:, 0], ACT.Sin).then_inc(s_sin, 1)
                act.activation(sc[:, 1], red[:, 2], ACT.Sin).then_inc(s_sin, 1)

                def begin(b, u):
                    act.wait_ge(s_xTp, b + 1)
                    wait(act, s_qp, b - 1)
                    act.activation(xnT[:, u], pT[0][:, 0:KT], ACT.Copy).then_inc(s_xT, 1)

                def turn(b, u, which):
                    wait(act, s_S, 4 * b - 4)
                    dst, first_bank, src, done = {"q": (qT, 0, s_qTp, s_qT), "k": (kT, 2, s_kTp, s_kT)}[which]
                    for h in range(2):
                        act.wait_ge(src, 2 * b + h + 1)
                        act.activation(dst[:, u, 4 * h:4 * h + 4], pS[first_bank + h][:], ACT.Copy).then_inc(done, 1)

                def exp(b, j):
                    act.wait_ge(s_sub, 4 * b + j + 1)
                    act.activation(E[:, 4 * j:4 * j + 4], E[:, 4 * j:4 * j + 4], ACT.Exp,
                                   scale=DH0 ** -0.5).then_inc(s_E, 1)

                def evac(b, j):
                    act.wait_ge(s_PTp, 4 * b + j + 1)
                    if j == 0:
                        wait(act, s_O, b)
                    act.activation(PT[:, 4 * j:4 * j + 4], pT[1 - j % 2][:], ACT.Copy).then_inc(s_PT, 1)

                def out(b):
                    act.wait_ge(s_OTp, b + 1)
                    wait(act, s_y, b)
                    act.activation(OT[:], pT[1][:, 0:KT], ACT.Copy).then_inc(s_OT, 1)

                def start(b, u):
                    begin(b, u)
                    turn(b, u, "q")
                    turn(b, u, "k")

                def step(b, u):
                    exp(b - 1, 0)
                    begin(b, u)
                    for j in range(1, 4):
                        exp(b - 1, j)
                    for j in range(4):
                        evac(b - 1, j)
                    turn(b, u, "q")
                    out(b - 1)
                    turn(b, u, "k")

                def last(b, u):
                    for j in range(4):
                        exp(b - 1, j)
                    for j in range(4):
                        evac(b - 1, j)
                    out(b - 1)

                rotate(act, NB, start, step, last)

            @block.tensor
            def _(pe):
                pe.wait_ge(s_wkv, 16)
                pe.wait_ge(C["s_ident"], 1)
                pe.wait_ge(s_one, 2)

                def project_kv(b, u):
                    pe.wait_ge(s_ct[u], 8 * (b + 2 - u))
                    wait(pe, s_v, b)
                    wait(pe, s_kb, b)
                    for k in range(KT):
                        mm = pe.matmul(pKV[:], cT[:, u, k], wkv[:, k], start=(k == 0), stop=(k == KT - 1))
                    mm.then_inc(s_kvp, 1)

                def project(b, u):
                    if isinstance(b, int) and b == 0:
                        project_kv(b, u)
                    pe.wait_ge(s_xn, b + 1)
                    wait(pe, s_PT, 4 * b - 4)
                    for k in range(KT):
                        mm = pe.transpose(pT[0][:, k], xn[:, u, k * P:(k + 1) * P], ident[:])
                    mm.then_inc(s_xTp, 1)
                    if isinstance(b, int) and b == 0:
                        pe.wait_ge(s_w, 16 * 2)
                    else:
                        project_kv(b, u)
                    pe.wait_ge(s_xT, b + 1)
                    wait(pe, s_x1, b - 1)
                    wait(pe, s_qb, b)
                    for k in range(KT):
                        mm = pe.matmul(psQ, xnT[:, u, k], wq[:, k], start=(k == 0), stop=(k == KT - 1))
                    mm.then_inc(s_qp, 1)

                def scores(b, u):
                    pe.wait_ge(s_qT, 2 * b + 2)
                    pe.wait_ge(s_kT, 2 * b + 2)
                    for j in range(0, 4, 2):
                        for n in range(4):
                            for r in range(2):
                                rows = slice(SLOT * r, SLOT * r + KSTACK)
                                mm = pe.matmul(pS[j + r][:, n], qT[rows, u, 2 * j + n], kT[rows, u, 2 * j + n],
                                               start=True, stop=True)
                        mm.then_inc(s_S, 2)

                def turn(b, u, which):
                    src, first_bank, ready, done = {"q": (q3, 0, s_q3, s_qTp), "k": (k3, 2, s_k3, s_kTp)}[which]
                    pe.wait_ge(ready, 3 * (b + 1))
                    wait(pe, s_sub, 4 * b - 2 + first_bank)
                    for h in range(2):
                        for n in range(4):
                            mm = pe.transpose(pS[first_bank + h][:, n],
                                              src[:, 8 * h + 2 * n:8 * h + 2 * n + 2].rearrange("p h d -> p (h d)"),
                                              ident[:])
                        mm.then_inc(done, 1)

                def weigh(b, u, begun):
                    for j in range(4):
                        pe.wait_ge(s_E, 4 * b + j + 1)
                        if j == 0:
                            wait(pe, s_OT, b)
                        elif j == 1:
                            pe.wait_ge(s_xT, begun)
                        else:
                            pe.wait_ge(s_PT, 4 * b + j - 1)
                        for n in range(4):
                            mm = pe.transpose(pT[1 - j % 2][:, n], E[:, 4 * j + n], ident[:])
                        mm.then_inc(s_PTp, 1)
                    pe.wait_ge(s_v, b + 1)
                    pe.wait_ge(s_qb, begun)
                    wait(pe, s_x1, b)
                    for c in range(H0):
                        if c % 4 == 0:
                            pe.wait_ge(s_PT, 4 * b + c // 4 + 1)
                        h = head_at(c)
                        mm = pe.matmul(psO[:, h], PT[:, c], v1[:, u, h], start=True, stop=True)
                    mm.then_inc(s_O, 1)

                def turn_out(b):
                    pe.wait_ge(s_On, b + 1)
                    pe.wait_ge(s_PT, 4 * b + 3)
                    for k in range(KT):
                        mm = pe.transpose(pT[1][:, k], On[:, k * P:(k + 1) * P], ident[:])
                    mm.then_inc(s_OTp, 1)

                def result(b):
                    if isinstance(b, int) and b == 0:
                        pe.wait_ge(s_wp, 16)
                    pe.wait_ge(s_OT, b + 1)
                    for k in range(KT):
                        mm = pe.matmul(psY, OT[:, k], wp[:, k], start=(k == 0), stop=(k == KT - 1))
                    mm.then_inc(s_y, 1)

                def start(b, u):
                    project(b, u)
                    turn(b, u, "q")
                    turn(b, u, "k")

                def step(b, u):
                    scores(b - 1, 1 - u)
                    project(b, u)
                    weigh(b - 1, 1 - u, b + 1)
                    turn(b, u, "q")
                    turn_out(b - 1)
                    turn(b, u, "k")
                    result(b - 1)

                def last(b, u):
                    scores(b - 1, 1 - u)
                    weigh(b - 1, 1 - u, b)
                    turn_out(b - 1)
                    result(b - 1)

                rotate(pe, NB, start, step, last)

            @block.vector
            def _(dve):
                n_tab = [0]

                def link(ins):
                    n_tab[0] += 1
                    ins.then_inc(s_tab, 1)
                    dve.wait_ge(s_tab, n_tab[0])

                dve.wait_ge(C["s_pos"], 16)
                link(dve.tensor_copy(posf[:], C["pos"][:]))
                for f in range(NFREQ):
                    inv = np.float32(1.0) / np.float32(ROPE_BASE) ** np.float32(2 * f / (DH0 // 2))
                    ins = dve.tensor_scalar(ang[:, :, :, f], posf[:], float(inv), None, ALU.mult)
                    n_tab[0] += 1
                    ins.then_inc(s_tab, 1)
                dve.wait_ge(s_tab, n_tab[0])
                MAGIC = 1.5 * 2.0 ** 23
                TWO_PI = 2 * np.pi
                c1 = 6.28125
                c2 = float((np.float32(TWO_PI - c1).view(np.uint32) & np.uint32(0xFFFFF000)).view(np.float32))
                c3 = float(np.float32(TWO_PI - c1 - c2))
                link(dve.tensor_scalar(turns[:], ang[:], float(1 / TWO_PI), MAGIC, ALU.mult, ALU.add))
                link(dve.tensor_scalar(turns[:], turns[:], -MAGIC, None, ALU.add))
                for c in (c1, c2, c3):
                    link(dve.scalar_tensor_tensor(ang[:], turns[:], -c, ang[:], ALU.mult, ALU.add))
                PI = float(np.nextafter(np.float32(np.pi), np.float32(0)))
                link(dve.tensor_scalar(red[:, 0], ang[:], PI, -PI, ALU.min, ALU.max))
                link(dve.tensor_scalar(red[:, 2], ang[:], float(np.pi / 2), None, ALU.add))
                link(dve.tensor_scalar(red[:, 1], red[:, 2], float(np.pi), -TWO_PI, ALU.is_gt, ALU.mult))
                link(dve.tensor_tensor(red[:, 2], red[:, 2], red[:, 1], ALU.add))
                link(dve.tensor_scalar(red[:, 2], red[:, 2], PI, -PI, ALU.min, ALU.max))
                assert n_tab[0] == ANGLE_STEPS
                dve.wait_ge(s_sin, 2)
                dve.wait_ge(C["s_masks"], 2)
                for s in range(2):
                    ins = dve.tensor_scalar(cosT[:, :, :, s, :], sc[:, 1], rest[:], None, ALU.mult)
                    link(ins)
                    ins = dve.tensor_scalar(sinT[:, :, :, s, :], sc[:, 0], rest[:], -1.0 if s == 0 else 1.0,
                                            ALU.mult, ALU.mult)
                    link(ins)
                dve.tensor_copy(rs[:, 0:1], first[:]).then_inc(s_tabs, 1)

                def statistics(c):
                    dve.wait_ge(C["s_x"][c], 16)
                    for b in range(GC * c, GC * (c + 1)):
                        dve.bn_stats(bstats[:, b], xres[:, b]).then_inc(s_bs0, 1)
                    dve.wait_ge(s_bs0, GC * (c + 1))
                    stats_vector(dve, c)

                def norm(b, u):
                    wait(dve, s_xTp, b - 1)
                    x = xres[:, bass.ds(b, 1), :].rearrange("p o n -> p (o n)")
                    m = mv[:, bass.ds(b, 1), 0:1].rearrange("p o n -> p (o n)")
                    r = rstd[:, bass.ds(b, 1)]
                    dve.tensor_scalar(xn[:, u], x, m, r, ALU.subtract, ALU.mult).then_inc(s_xn, 1)

                def rope_q(b, u):
                    dve.wait_ge(s_kvp, b + 1)
                    wait(dve, s_kTp, 2 * b)
                    wait(dve, s_k3, 3 * b)
                    dve.tensor_tensor(k3[:, :, KSTACK:SLOT], heads(pKV[:, 0:D]), heads(bias[:, 1, :]),
                                      ALU.add).then_inc(s_kb, 1)
                    wait(dve, s_O, b - 1)
                    dve.tensor_tensor(v1[:, u, :, 0:DH0], heads(pKV[:, D:2 * D]), heads(bias[:, 2, :]),
                                      ALU.add).then_inc(s_v, 1)
                    dve.wait_ge(s_qp, b + 1)
                    wait(dve, s_qTp, 2 * b)
                    qb = q3[:, :, DH0:2 * DH0]
                    dve.tensor_tensor(qb, heads(psQ), heads(bias[:, 0, :]), ALU.add).then_inc(s_qb, 1)
                    dve.wait_ge(s_qb, b + 1)
                    dve.tensor_tensor(q3[:, :, 0:DH0], qb, table(cosT, b), ALU.mult).then_inc(s_qcos, 1)
                    for s in range(2):
                        dve.tensor_tensor(halves(qrot[:])[:, :, :, s, :], halves(qb)[:, :, :, 1 - s, :],
                                          table(sinT, b, s), ALU.mult).then_inc(s_qrot, 1)
                    dve.tensor_scalar(q3[:, :, 2 * DH0:3 * DH0], qb, first[:], None, ALU.mult).then_inc(s_q3, 1)
                    dve.wait_ge(s_qcos, b + 1)
                    dve.wait_ge(s_qrot, 2 * b + 2)
                    dve.tensor_tensor(q3[:, :, 0:DH0], q3[:, :, 0:DH0], qrot[:], ALU.add).then_inc(s_q3, 2)

                def shift(b):
                    for j in range(4):
                        hs = slice(4 * j, 4 * j + 4)
                        dve.wait_ge(s_S, 4 * b + j + 1)
                        dve.tensor_reduce(mx[:, hs], pS[j][:], AX.X, ALU.max).then_inc(s_mx, 1)
                        dve.wait_ge(s_mx, 4 * b + j + 1)
                        dve.tensor_tensor(E[:, hs], pS[j][:], mx[:, hs].unsqueeze(2).broadcast_to([P, 4, P]),
                                          ALU.subtract).then_inc(s_sub, 1)

                def finish(b):
                    dve.wait_ge(s_O, b + 1)
                    dve.reciprocal(rs[:], psO[:, :, DH0]).then_inc(s_rs, 1)
                    dve.wait_ge(s_rs, b + 1)
                    wait(dve, s_OTp, b)
                    dve.tensor_tensor(heads(On[:]), psO[:, :, 0:DH0], rs[:].unsqueeze(2).broadcast_to([P, H0, DH0]),
                                      ALU.mult).then_inc(s_On, 1)
                    dve.wait_ge(s_y, b + 1)
                    dve.wait_ge(s_xb, b + 1)
                    x = xres[:, bass.ds(b, 1), :].rearrange("p o n -> p (o n)")
                    wait(dve, s_keep, 2 * b)
                    dve.scalar_tensor_tensor(xw[:], psY, tg[:, 0:1], x, ALU.mult, ALU.add).then_inc(s_x1, 1)
                    dve.wait_ge(s_x1, b + 1)
                    dve.bn_stats(stats[:], xw[:]).then_inc(s_bs, 1)
                    dve.tensor_scalar(x, xw[:], 0.0, None, ALU.add).then_inc(s_keep, 1)
                    dve.wait_ge(s_bs, b + 1)
                    dve.tensor_scalar(bstats[:, bass.ds(b, 1), :].rearrange("p o n -> p (o n)"), stats[:], 0.0, None,
                                      ALU.add).then_inc(s_keep, 1)

                def first_(b, u):
                    statistics(0)
                    dve.wait_ge(s_rstd, 1)
                    norm(0, 0)
                    statistics(1)
                    dve.wait_ge(s_w, 16 * 2)
                    rope_q(0, 0)
                    for c in range(2, NB // GC):
                        statistics(c)
                    norm(1, 1)

                def step(b, u):
                    shift(b - 1)
                    rope_q(b, u)
                    if isinstance(b, int) and b == 1:
                        dve.wait_ge(s_rstd, NB // GC)
                        dve.wait_ge(s_cx, 16)
                    dve.bn_stats(row(ctx_stats, b), row(cx, b)).then_inc(s_cst, 1)
                    if ahead(b, NB):
                        norm(b + 1, 1 - u)
                    finish(b - 1)

                def last(b, u):
                    shift(b - 1)
                    dve.bn_stats(ctx_stats[:, 0], cx[:, 0]).then_inc(s_cst, 1)
                    dve.wait_ge(s_cst, NB)
                    for j in range(NB):
                        dve.bn_aggr(C["ctx_mv"][:, j], ctx_stats[:, j]).then_inc(s_cmv, 1)
                    finish(b - 1)

                rotate(dve, NB, first_, step, last)


GC = 4


def norm_stats(nc, C, tag):
    def sem(name):
        return nc.alloc_semaphore(name=tag + name)

    mv, rstd, half, vare, bstats = (C[k] for k in ("mv", "rstd", "half", "vare", "bstats"))
    s_mv, s_ve, s_rstd = sem("mean_var"), sem("var_eps"), sem("rstd_ready")

    def vector(dve, c):
        for b in range(GC * c, GC * (c + 1)):
            dve.bn_aggr(mv[:, b], bstats[:, b]).then_inc(s_mv, 1)

    def gpsimd(pool, c):
        bs = slice(GC * c, GC * (c + 1))
        pool.wait_ge(s_mv, GC * (c + 1))
        pool.tensor_scalar(vare[:, bs], mv[:, bs, 1], EPS, None, ALU.add).then_inc(s_ve, 1)
        pool.wait_ge(s_ve, c + 1)
        pool.tensor_tensor(rstd[:, bs], vare[:, bs], half[:, bs], ALU.pow).then_inc(s_rstd, 1)

    return vector, gpsimd, s_rstd


FP8_MAX = 448.0
FP8_SCALE_STEPS = 4
FP8_STEPS = 4


def fp8_scale(dve, sc, greatest, steps):
    for i, make in enumerate((
            lambda: dve.tensor_scalar(sc[:, 1:2], greatest[:], 1e-12, None, ALU.max),
            lambda: dve.reciprocal(sc[:, 1:2], sc[:, 1:2]),
            lambda: dve.tensor_scalar(sc[:, 0:1], sc[:, 1:2], FP8_MAX, FP8_MAX, ALU.mult, ALU.min),
            lambda: dve.reciprocal(sc[:, 1:2], sc[:, 0:1]))):
        make().then_inc(steps, 1)
        dve.wait_ge(steps, i + 1)


def to_fp8(dve, dst, src, sc, place, steps, n, done, between=lambda i: None):
    z, s = place
    dve.tensor_scalar(z, src, sc[:, 0:1], FP8_MAX, ALU.mult, ALU.min).then_inc(steps, 1)
    between(0)
    dve.wait_ge(steps, n + 1)
    dve.tensor_scalar(s.bitcast(U32), z.bitcast(U32), 0x7F800000, None, ALU.bitwise_and).then_inc(steps, 1)
    between(1)
    dve.wait_ge(steps, n + 2)
    dve.tensor_scalar(s, s, 2.0 ** -6, 1.5 * 2.0 ** 20, ALU.max, ALU.mult).then_inc(steps, 1)
    dve.wait_ge(steps, n + 3)
    dve.scalar_tensor_tensor(z, z, -FP8_MAX, s, ALU.max, ALU.add).then_inc(steps, 1)
    dve.wait_ge(steps, n + 4)
    dve.tensor_tensor(dst, z, s, ALU.subtract).then_inc(done, 1)


def row(ap, b):
    return ap[:, bass.ds(b, 1), :].rearrange("p o n -> p (o n)")


def stage_experts(nc, T, C, tag="B"):
    xres, ident, mv, rstd, tg = (C[k] for k in ("xres", "ident", "mv", "rstd", "tg"))
    with ExitStack() as ctx:
        def sb(name, shape, dt=F32):
            return ctx.enter_context(nc.sbuf_tensor(tag + name, shape, dt))

        def sem(name):
            return nc.alloc_semaphore(name=tag + name)

        we = sb("we", [P, 2, NE * WCOLS], BF16)
        ws = C["wide"][:, 0:2 * WCOLS].rearrange("p (a n) -> p a n", a=2)
        xT2 = C["wide"][:, 2 * WCOLS:2 * (WCOLS + KT * NTOK)].rearrange("p (a k t) -> p a k t", a=2, k=KT)
        stage = sb("stage", [P, 2, QC])
        cvar = sb("cvar", [P, NB])
        am = sb("am", [P, 1])
        amr = sb("amr", [P, 1])
        rw = sb("rw", [P, KT, NE])
        rb = sb("rb", [P, NE])
        spare = we[:, 0, (NE - 2) * WCOLS:(NE - 2) * WCOLS + 2 * NB * D].bitcast(F32).rearrange(
            "p (b n) -> p b n", n=D)

        lg = sb("lg", [P, NB, NE])
        key = sb("key", [P, NB, NE])
        pr = sb("pr", [P, NB, NE])
        one = sb("one", [P, NB, NE])
        run = sb("run", [P, NB + 1, NE])
        tmp = sb("tmp", [P, NB, NE])
        pos = sb("pos", [P, NB])
        posi = C["slot_of"]
        r16 = sb("r16", [P, NB])
        p16 = sb("p16", [P, NB])
        cshare = sb("cshare", [P, NB])
        croute = C["croute"]
        cnt = sb("cnt", [P, NE])
        cnti = sb("cnti", [P, NE], I32)
        ends = sb("ends", [P, NE + 1])
        pref_i = sb("pref_i", [P, NE], I32)
        pref = sb("pref", [P, NE])
        slot_i = sb("slot_i", [1, NT], I32)
        slot_f = sb("slot_f", [1, NT])
        past = sb("past", [1, NT, NE])
        eidf = sb("eidf", [1, NT])
        eid = sb("eid", [1, NT], I32)

        bank = [ctx.enter_context(nc.psum_tensor(f"{tag}bank{i}", [P, 512], F32)) for i in range(8)]

        def tile2(ap):
            return ap[:, 0:KT * P].rearrange("p (k t) -> p k t", k=KT)

        s_w = [sem(f"w_in{u}") for u in range(2)]
        s_hi = sem("w_high")
        s_lo = sem("w_low")
        s_r = sem("router_in")
        s_k1 = sem("constants1")
        s_k2 = sem("constants2")
        s_xw = sem("xn_for_transpose")
        s_xn = sem("xn_for_slots")
        s_xTp = sem("xT_in_psum")
        s_xT = sem("xT")
        s_xhi = sem("xT_high")
        s_xlo = sem("xT_low")
        s_lgp = sem("logits_in_psum")
        s_lg = sem("logits")
        s_c = sem("routing_steps")
        s_key = sem("clipped_logits")
        s_ex = sem("router_exp")
        s_one = sem("one_hot")
        s_cum = sem("counts_in_psum")
        s_scat = sem("scattered")
        s_h1 = sem("shared_h1")
        s_h3 = sem("shared_h3")
        s_si = sem("shared_silu")
        s_hd = sem("shared_hidden")
        s_hh = sem("shared_hidden_high")
        s_hl = sem("shared_hidden_low")
        s_yp1 = sem("shared_y_products")
        s_ys = sem("shared_added")
        s_xs = [sem(f"slots_in{u}") for u in range(2)]
        s_tp = sem("slotsT_in_psum")
        s_th = sem("slotsT_high")
        s_tl = sem("slotsT_low")
        s_e1 = sem("expert_h1")
        s_e3 = sem("expert_h3")
        s_es = sem("expert_silu")
        s_hTp = sem("expert_hiddenT_in_psum")
        s_ed = sem("expert_hidden")
        s_pad = sem("hidden_padding")
        s_eh = sem("expert_hidden_high")
        s_el = sem("expert_hidden_low")
        s_yp = sem("expert_y_in_psum")
        s_y = sem("expert_y")
        s_yst = [sem(f"y_stored{u}") for u in range(2)]
        s_cve = sem("ctx_var_eps")
        s_crs = sem("ctx_rstd")
        s_lw = sem("linear_weights_in")
        s_am = sem("linear_weights_greatest")
        s_amr = sem("linear_weights_greatest_of_all")
        s_q = sem("linear_rounding_steps")
        s_wq = sem("linear_weights_rounded")

        stats_vector, stats_gpsimd, s_rstd = norm_stats(nc, C, tag)

        with nc.Block() as block, ExitStack() as rctx:
            below = rctx.enter_context(nc.sbuf_tensor(tag + "below", [P, P], F32))
            ones = rctx.enter_context(nc.sbuf_tensor(tag + "ones", [P, P], F32))
            xw = rctx.enter_context(nc.sbuf_tensor(tag + "xw", [P, 2, D], F32))
            xT = rctx.enter_context(nc.sbuf_tensor(tag + "xT", [P, 2, KT, P], F32))

            @block.sync
            def _(sp):
                sp.dma_start(rw[:], T["B_rw"]).then_inc(s_r, 16)
                sp.dma_start(rb[:], T["B_rb"].partition_broadcast(P)).then_inc(s_r, 16)
                sp.dma_start(C["linear_w"][:], T["D_w"]).then_inc(s_lw, 16)
                for q in range(4):
                    if q >= 2:
                        sp.wait_ge(s_lo, q - 1)
                        sp.wait_ge(s_hi, q - 1)
                    sp.dma_start(stage[:, q % 2], T["B_ws"][q]).then_inc(s_w[q % 2], 16)

            @block.gpsimd
            def _(pool):
                for c in range(NB // GC):
                    stats_gpsimd(pool, c)
                pool.memset(below[:], 1.0).then_inc(s_k1, 1)
                pool.memset(ones[:], 1.0).then_inc(s_k1, 1)
                pool.iota(pref_i[:], pattern=[[-1, NE]], base=NE, channel_multiplier=0).then_inc(s_k1, 1)
                pool.iota(slot_i[:], pattern=[[1, NT]], base=0, channel_multiplier=0).then_inc(s_k1, 1)
                pool.wait_ge(s_k1, 4)
                pool.affine_select(out=below[:], in_=below[:], compare_op=ALU.is_gt, fill=0.0, base=0,
                                   pattern=[[1, P]], channel_multiplier=-1).then_inc(s_k2, 1)

                def low(q):
                    pool.wait_ge(s_hi, q + 1)
                    cols = slice(q * QC, (q + 1) * QC)
                    pool.tensor_tensor(ws[:, 1, cols], stage[:, q % 2], ws[:, 0, cols], ALU.subtract).then_inc(s_lo, 1)

                low(0)
                low(1)
                pool.tensor_scalar(cvar[:], C["ctx_mv"][:, :, 1], EPS, None, ALU.add).then_inc(s_cve, 1)
                pool.wait_ge(s_cve, 1)
                pool.tensor_tensor(C["ctx_rstd"][:], cvar[:], C["half"][:], ALU.pow).then_inc(s_crs, 1)
                pool.wait_ge(s_am, 1)
                pool.partition_all_reduce(amr[:], am[:], P, bass.bass_isa.ReduceOp.max).then_inc(s_amr, 1)
                low(2)
                low(3)

            @block.scalar
            def _(act):
                def high(q):
                    act.wait_ge(s_w[q % 2], 16 * (q // 2 + 1))
                    act.activation(ws[:, 0, q * QC:(q + 1) * QC], stage[:, q % 2], ACT.Copy).then_inc(s_hi, 1)

                def evac(j, u):
                    act.wait_ge(s_xTp, j + 1)
                    wait(act, s_lgp, j - 1)
                    wait(act, s_xlo, j - 1)
                    act.activation(xT[:, u], tile2(bank[u]), ACT.Copy).then_inc(s_xT, 1)
                    act.activation(xT2[:, 0, :, bass.ds(j * P, P)], tile2(bank[u]), ACT.Copy).then_inc(s_xhi, 1)

                high(0)
                high(1)
                rotate(act, NB, evac, evac, lambda j, u: None)
                act.wait_ge(s_key, 1)
                act.activation(pr[:], pr[:], ACT.Exp, scale=-1.0).then_inc(s_ex, 1)
                high(2)
                high(3)

            @block.tensor
            def _(pe):
                pe.wait_ge(s_r, 32)

                def turn(j, u):
                    pe.wait_ge(s_xw, j + 1)
                    wait(pe, s_xT, j - 1)
                    wait(pe, s_xhi, j - 1)
                    for k in range(KT):
                        mm = pe.transpose(bank[u][:, k * P:(k + 1) * P], xw[:, u, k * P:(k + 1) * P], ident[:])
                    mm.then_inc(s_xTp, 1)

                def logits(j, u):
                    pe.wait_ge(s_xT, j + 1)
                    for k in range(KT):
                        mm = pe.matmul(bank[2][:, bass.ds(j * NE, NE)], xT[:, u, k], rw[:, k], start=(k == 0),
                                       stop=(k == KT - 1))
                    mm.then_inc(s_lgp, 1)

                def step(j, u):
                    turn(j, u)
                    logits(j - 1, 1 - u)

                rotate(pe, NB, turn, step, lambda j, u: logits(j - 1, 1 - u))
                pe.wait_ge(s_k2, 1)
                pe.wait_ge(s_one, 1)
                hot = one[:].rearrange("p b e -> p (b e)")
                pe.matmul(bank[4][:, 0:NB * NE], below[:], hot, start=True, stop=True)
                pe.matmul(bank[5][:, 0:NB * NE], ones[:], hot, start=True, stop=True).then_inc(s_cum, 1)

            @block.vector
            def _(dve):
                n = [0]

                def link(ins):
                    n[0] += 1
                    ins.then_inc(s_c, 1)
                    dve.wait_ge(s_c, n[0])

                for c in range(NB // GC):
                    stats_vector(dve, c)
                dve.wait_ge(s_lw, 16)
                dve.tensor_reduce(am[:], C["linear_w"][:].rearrange("p k n -> p (k n)"), AX.X, ALU.max,
                                  apply_absolute_value=True).then_inc(s_am, 1)
                dve.wait_ge(s_rstd, 1)

                def norm(j, u):
                    m = mv[:, bass.ds(j, 1), 0:1].rearrange("p o n -> p (o n)")
                    r = rstd[:, bass.ds(j, 1)]
                    wait(dve, s_xTp, j - 1)
                    dve.tensor_scalar(xw[:, u], row(xres, j), m, r, ALU.subtract, ALU.mult).then_inc(s_xw, 1)
                    dve.tensor_scalar(row(spare, j), row(xres, j), m, r, ALU.subtract, ALU.mult).then_inc(s_xn, 1)

                def low(j, u):
                    hi, lo = (xT2[:, part, :, bass.ds(j * P, P)] for part in range(2))
                    dve.wait_ge(s_xhi, j + 1)
                    dve.tensor_tensor(lo, xT[:, u], hi, ALU.subtract).then_inc(s_xlo, 1)

                def step(j, u):
                    if isinstance(j, int) and j == 1:
                        dve.wait_ge(s_rstd, NB // GC)
                    norm(j, u)
                    low(j - 1, 1 - u)

                rotate(dve, NB, norm, step, lambda j, u: low(j - 1, 1 - u))
                dve.wait_ge(s_lgp, NB)
                dve.tensor_tensor(lg[:], bank[2][:, 0:NB * NE].rearrange("p (b e) -> p b e", b=NB),
                                  rb[:].unsqueeze(1).broadcast_to([P, NB, NE]), ALU.add).then_inc(s_lg, 1)
                dve.wait_ge(s_lg, 1)
                dve.tensor_scalar(pr[:], lg[:], -50.0, 50.0, ALU.max, ALU.min).then_inc(s_key, 1)
                link(dve.tensor_scalar(key[:], lg[:], -50.0, SIGMOID_ONE, ALU.max, ALU.min))
                dve.wait_ge(s_k1, 4)
                link(dve.tensor_copy(pref[:], pref_i[:]))
                link(dve.tensor_reduce(r16[:], key[:], AX.X, ALU.max))
                wide = [P, NB, NE]
                link(dve.tensor_tensor(key[:], key[:], r16[:].unsqueeze(2).broadcast_to(wide), ALU.is_equal))
                link(dve.tensor_tensor(key[:], key[:], pref[:].unsqueeze(1).broadcast_to(wide), ALU.mult))
                link(dve.tensor_reduce(r16[:], key[:], AX.X, ALU.max))
                dve.tensor_tensor(one[:], key[:], r16[:].unsqueeze(2).broadcast_to(wide), ALU.is_equal).then_inc(s_one, 1)
                dve.wait_ge(s_ex, 1)
                dve.wait_ge(s_one, 1)
                link(dve.tensor_scalar(pr[:], pr[:], 1.0, None, ALU.add))
                link(dve.reciprocal(pr[:], pr[:]))
                link(dve.tensor_tensor(tmp[:], pr[:], one[:], ALU.mult))
                link(dve.tensor_reduce(p16[:], tmp[:], AX.X, ALU.add))
                link(dve.tensor_scalar(p16[:], p16[:], 1e-8, float(np.float32(1.0 - 1e-8)), ALU.max, ALU.min))
                link(dve.tensor_scalar(r16[:], p16[:], 0.5, 1e-8, ALU.add, ALU.add))
                link(dve.tensor_scalar(r16[:], r16[:], 0.5, 2.0, ALU.max, ALU.min))
                link(dve.reciprocal(r16[:], r16[:]))
                link(dve.tensor_scalar(cshare[:], r16[:], tg[:, 2:3], 0.5, ALU.mult, ALU.mult))
                link(dve.tensor_tensor(croute[:], r16[:], p16[:], ALU.mult))
                link(dve.tensor_scalar(croute[:], croute[:], tg[:, 2:3], None, ALU.mult))
                link(dve.memset(run[:, 0], 0.0))
                link(dve.memset(ends[:, 0:1], 0.0))
                dve.wait_ge(s_cum, 1)
                total = bank[5][:, 0:NB * NE].rearrange("p (b e) -> p b e", b=NB)
                for b in range(NB):
                    link(dve.tensor_tensor(run[:, b + 1], run[:, b], total[:, b], ALU.add))
                link(dve.tensor_scalar(cnti[:], run[:, NB], float(P - 1), None, ALU.add))
                link(dve.tensor_scalar(cnti[:], cnti[:], P.bit_length() - 1, None, ALU.logical_shift_right))
                link(dve.tensor_copy(cnt[:], cnti[:]))
                for e in range(NE):
                    link(dve.tensor_tensor(ends[:, e + 1:e + 2], ends[:, e:e + 1], cnt[:, e:e + 1], ALU.add))
                link(dve.tensor_scalar(cnt[:], ends[:, 0:NE], float(P), None, ALU.mult))
                early = bank[4][:, 0:NB * NE].rearrange("p (b e) -> p b e", b=NB)
                link(dve.tensor_tensor(tmp[:], run[:, 0:NB], early, ALU.add))
                link(dve.tensor_tensor(tmp[:], tmp[:], cnt[:].unsqueeze(1).broadcast_to(wide), ALU.add))
                link(dve.tensor_tensor(tmp[:], tmp[:], one[:], ALU.mult))
                link(dve.tensor_reduce(pos[:], tmp[:], AX.X, ALU.add))
                link(dve.tensor_copy(posi[:], pos[:]))
                link(dve.tensor_copy(slot_f[:], slot_i[:]))
                link(dve.tensor_tensor(past[:], ends[0:1, 1:NE + 1].unsqueeze(1).broadcast_to([1, NT, NE]),
                                       slot_f[:].unsqueeze(2).broadcast_to([1, NT, NE]), ALU.is_le))
                link(dve.tensor_reduce(eidf[:], past[:], AX.X, ALU.add))
                link(dve.tensor_scalar(eid[:], eidf[:], float(NE - 1), None, ALU.min))

        act_s = sb("act_s", [P, 2, CH])
        hid = sb("hid", [P, FT * P])
        h2 = sb("h2", [P, 2, 2, FT * P], BF16)
        ysb = sb("ysb", [P, 2, D])
        QLATE = 4 * (NE - 2)

        def quarters(c, m):
            extra = 2
            if isinstance(c, int) and c == 0:
                return (2 * m, 2 * m + 1) if m < extra else (m + extra,)
            if isinstance(c, int) and c == NCH - 1:
                q0 = FT * c + extra
                return (q0 + 2 * m, q0 + 2 * m + 1) if m < extra else (q0 + m + extra,)
            return (c * FT + (m + extra),)

        assert 4 * NE == NCH * FT + 4 and FT % 2 == 0 and FT * (NCH - 1) + 2 <= QLATE

        def quarter(part, q):
            return we[:, part, bass.ds(q * QC, QC)]

        with nc.Block() as block:
            @block.sync
            def _(sp):
                def load(q, u):
                    sp.wait_ge(s_hi, q + 3)
                    sp.wait_ge(s_lo, q + 3)
                    sp.dma_start(stage[:, u], T["B_we"][bass.ds(q, 1)].rearrange("o p n -> (o p) n")).then_inc(
                        s_w[u], 16)

                with sp.Fori(0, 4 * NE - 1, 2) as q:
                    load(q, 0)
                    load(q + 1, 1)

            @block.gpsimd
            def _(pool):
                pool.wait_ge(C["s_zeroed"], 16 * NT)
                for j in range(NB):
                    pool.indirect_dma_start(
                        out=C["slots"].rearrange("t p n -> (t p) n"),
                        out_offset=bass.IndirectOffsetOnAxis(ap=posi[:, j:j + 1].bitcast(U32), axis=0),
                        in_=spare[:, j], in_offset=None).then_inc(s_scat, 16)
                pool.wait_ge(s_scat, 16 * NB)
                pool.memset(hid[:, FF:FT * P], 0.0).then_inc(s_pad, 1)
                for u in range(2):
                    pool.memset(ysb[:, u], 0.0).then_inc(s_yst[u], 16)

            def m_rows(m):
                return P if m < FT - 1 else FLAST

            def before(n, m):
                return n if m == 0 else n - 1

            def rounds(eng, body):
                body(0)
                with eng.Fori(1, NCH - 1) as c:
                    body(c)
                body(NCH - 1)

            @block.scalar
            def _(act):
                def body(c):
                    for m in range(FT):
                        n, u, rows = c * FT + m, m % 2, m_rows(m)
                        act.wait_ge(s_h1, n + 1)
                        wait(act, s_hd, before(n, m))
                        act.activation(act_s[0:rows, u], bank[u][0:rows], ACT.Silu).then_inc(s_si, 1)
                        act.wait_ge(s_hd, n + 1)
                        wait(act, s_yp1, before(n, m))
                        act.activation(h2[0:rows, u, 0, 0:CH], hid[0:rows, 0:CH], ACT.Copy).then_inc(s_hh, 1)
                        for i, q in enumerate(quarters(c, m)):
                            if isinstance(q, int) and q == QLATE:
                                act.wait_ge(s_scat, 16 * NB)
                            high(q, (m + i) % 2 if len(quarters(c, m)) == 1 else i)

                def high(q, u):
                    act.wait_ge(s_w[u], q * 8 + (8 * (2 - u) + 32))
                    act.activation(quarter(0, q), stage[:, u], ACT.Copy).then_inc(s_hi, 1)

                rounds(act, body)

            @block.tensor
            def _(pe):
                def hidden(c, m):
                    n, u, rows = c * FT + m, m % 2, m_rows(m)
                    for which, base, done in ((0, W1, s_h1), (1, W3, s_h3)):
                        if which == 0:
                            wait(pe, s_si, before(n, m))
                        else:
                            wait(pe, s_hd, before(n, m))
                        i = 0
                        for k in range(KT):
                            cols = slice(base + k * FF + m * P, base + k * FF + (m + 1) * P)
                            for a, b in ((0, 0), (0, 1), (1, 0)):
                                mm = pe.matmul(bank[2 * which + u][:], ws[:, a, cols],
                                               xT2[:, b, k, bass.ds(c * CH, CH)], start=(i == 0), stop=(i == 5))
                                i += 1
                        mm.then_inc(done, 1)

                def result(c, m):
                    n, u, rows = c * FT + m, m % 2, m_rows(m)
                    pe.wait_ge(s_hl, n + 1)
                    for t in range(CH // P):
                        if m == 0:
                            wait(pe, s_ys, c * (CH // P))
                        for a, b in ((0, 0), (1, 0), (0, 1)):
                            mm = pe.matmul(bank[4 + t][:, 0:D], h2[0:rows, u, a, t * P:(t + 1) * P],
                                           ws[0:rows, b, W2 + m * D:W2 + (m + 1) * D],
                                           start=(m == 0 and a + b == 0), stop=(m == FT - 1 and b == 1))
                    mm.then_inc(s_yp1, 1)

                def body(c):
                    for m in range(FT):
                        hidden(c, m)
                        if m >= 1:
                            result(c, m - 1)
                    result(c, FT - 1)

                rounds(pe, body)

            @block.vector
            def _(dve):
                def low(q, u):
                    dve.wait_ge(s_hi, q + 5)
                    dve.tensor_tensor(quarter(1, q), stage[:, u], quarter(0, q), ALU.subtract).then_inc(s_lo, 1)

                def body(c):
                    for m in range(FT):
                        n, u, rows = c * FT + m, m % 2, m_rows(m)
                        dve.wait_ge(s_si, n + 1)
                        dve.wait_ge(s_h3, n + 1)
                        wait(dve, s_hh, n)
                        wait(dve, s_hl, n)
                        dve.tensor_tensor(hid[0:rows, 0:CH], act_s[0:rows, u], bank[2 + u][0:rows],
                                          ALU.mult).then_inc(s_hd, 1)
                        dve.wait_ge(s_hh, n + 1)
                        dve.tensor_tensor(h2[0:rows, u, 1, 0:CH], hid[0:rows, 0:CH], h2[0:rows, u, 0, 0:CH],
                                          ALU.subtract).then_inc(s_hl, 1)
                        for i, q in enumerate(quarters(c, m)):
                            low(q, (m + i) % 2 if len(quarters(c, m)) == 1 else i)
                    dve.wait_ge(s_yp1, c * FT + FT)
                    for t in range(CH // P):
                        j = c * (CH // P) + t
                        dve.scalar_tensor_tensor(row(xres, j), bank[4 + t][:, 0:D], cshare[:, bass.ds(j, 1)],
                                                 row(xres, j), ALU.mult, ALU.add).then_inc(s_ys, 1)

                rounds(dve, body)

        xs = sb("xs", [P, 2, D])
        xh = sb("xh", [P, 2, 2, KT, P], BF16)
        silu = act_s[:].rearrange("p u n -> p (u n)")
        HT_BANKS = ((0, 4 * P), (1, (FT - 4) * P))
        with nc.Block() as block:
            @block.sync
            def _(sp):
                def load(t, u):
                    wait(sp, s_tp, t - 1)
                    sp.dma_start(xs[:, u], C["slots"][bass.ds(t, 1)].rearrange("o p n -> (o p) n")).then_inc(
                        s_xs[u], 16)

                def store(t, u):
                    sp.wait_ge(s_y, t + 1)
                    sp.dma_start(C["results"][bass.ds(t, 1)].rearrange("o p n -> (o p) n"), ysb[:, u]).then_inc(
                        s_yst[u], 16)

                load(0, 0)
                load(1, 1)
                with sp.Fori(0, NT - 3, 2) as t:
                    for u in range(2):
                        load(t + (2 + u), u)
                        store(t + u, u)
                for u in range(2):
                    store(NT - 2 + u, u)
                for u in range(2):
                    sp.wait_ge(s_yst[u], 16 * (NT // 2 + 1))

            HH = FF // 2

            @block.gpsimd
            def _(pool):
                n = KT * H1 * DH1 // 2
                for i in range(8):
                    pool.wait_ge(s_y, 2 * i + 2)
                    pool.dma_start(C["wide"][:, 2 * n * i:2 * n * (i + 1)].bitcast(F32),
                                   T["C_w"][i // 2][:, i % 2 * n:(i % 2 + 1) * n]).then_inc(C["s_wide"], 16)

            @block.scalar
            def _(act):
                def split(t, u):
                    act.wait_ge(s_tp, t + 1)
                    wait(act, s_e3, t - 1)
                    act.activation(xh[:, u, 0], tile2(bank[0]), ACT.Copy).then_inc(s_th, 1)

                def silus(t, u):
                    wait(act, s_ed, t)
                    act.wait_ge(s_e1, t + 1)
                    for i in range(2):
                        act.activation(silu[:, HH * i:HH * (i + 1)], bank[1 + i][:, 0:HH], ACT.Silu).then_inc(s_es, 1)

                def high(t, u):
                    act.wait_ge(s_hTp, t + 1)
                    wait(act, s_yp, t - 1)
                    for i, n in HT_BANKS:
                        ins = act.activation(h2[:, u, 0, 4 * P * i:4 * P * i + n], bank[6 + i][:, 0:n], ACT.Copy)
                    ins.then_inc(s_eh, 1)

                def result(t, u):
                    act.wait_ge(s_yp, t + 1)
                    act.wait_ge(s_yst[u], t * 8 + 8 * (2 - u))
                    act.activation(ysb[:, u], bank[5][:, 0:D], ACT.Copy).then_inc(s_y, 1)

                def first(t, u):
                    split(0, 0)
                    silus(0, 0)
                    split(1, 1)
                    high(0, 0)

                def step(t, u):
                    silus(t, u)
                    if ahead(t, NT):
                        split(t + 1, 1 - u)
                    result(t - 1, 1 - u)
                    high(t, u)

                rotate(act, NT, first, step, lambda t, u: result(t - 1, 1 - u))

            @block.tensor
            def _(pe):
                def turn(t, u):
                    pe.wait_ge(s_xs[u], t * 8 + 8 * (2 - u))
                    wait(pe, s_th, t)
                    wait(pe, s_tl, t)
                    for k in range(KT):
                        mm = pe.transpose(bank[0][:, k * P:(k + 1) * P], xs[:, u, k * P:(k + 1) * P], ident[:])
                    mm.then_inc(s_tp, 1)

                def expert(t):
                    return pe.value_load(eid[0:1, bass.ds(t, 1)], min_val=0, max_val=NE - 1)

                def hidden(t, u):
                    e = expert(t)
                    pe.wait_ge(s_tl, t + 1)
                    for base, b0, done in ((W1, 1, s_e1), (W3, 3, s_e3)):
                        if base == W1:
                            wait(pe, s_es, 2 * t)
                        else:
                            wait(pe, s_ed, t)
                        for i in range(2):
                            for k in range(KT):
                                for a, b in ((0, 0), (0, 1), (1, 0)):
                                    mm = pe.matmul(bank[b0 + i][:, 0:HH], xh[:, u, b, k],
                                                   we[:, a, bass.ds(e * WCOLS + (base + k * FF + i * HH), HH)],
                                                   start=(k + a + b == 0), stop=(k == KT - 1 and a == 1))
                        mm.then_inc(done, 1)

                def turn_hidden(t, u):
                    pe.wait_ge(s_ed, t + 1)
                    wait(pe, s_eh, t)
                    wait(pe, s_el, t)
                    for m in range(FT):
                        mm = pe.transpose(bank[6 + m // 4][:, m % 4 * P:(m % 4 + 1) * P], hid[:, m * P:(m + 1) * P],
                                          ident[:])
                    mm.then_inc(s_hTp, 1)

                def result(t, u):
                    e = expert(t)
                    pe.wait_ge(s_el, t + 1)
                    wait(pe, s_y, t)
                    for m in range(FT):
                        rows = m_rows(m)
                        for a, b in ((0, 0), (1, 0), (0, 1)):
                            mm = pe.matmul(bank[5][:, 0:D], h2[0:rows, u, a, m * P:(m + 1) * P],
                                           we[0:rows, b, bass.ds(e * WCOLS + (W2 + m * D), D)],
                                           start=(m == 0 and a + b == 0), stop=(m == FT - 1 and b == 1))
                    mm.then_inc(s_yp, 1)

                def first(t, u):
                    turn(0, 0)
                    hidden(0, 0)
                    turn(1, 1)
                    turn_hidden(0, 0)

                def step(t, u):
                    hidden(t, u)
                    if ahead(t, NT):
                        turn(t + 1, 1 - u)
                    result(t - 1, 1 - u)
                    turn_hidden(t, u)

                rotate(pe, NT, first, step, lambda t, u: result(t - 1, 1 - u))

            @block.vector
            def _(dve):
                def split(t, u):
                    dve.wait_ge(s_th, t + 1)
                    dve.tensor_tensor(xh[:, u, 1], tile2(bank[0]), xh[:, u, 0], ALU.subtract).then_inc(s_tl, 1)

                def product(t, u):
                    wait(dve, s_hTp, t)
                    dve.wait_ge(s_es, 2 * t + 2)
                    dve.wait_ge(s_e3, t + 1)
                    for i in range(2):
                        ins = dve.tensor_tensor(hid[:, HH * i:HH * (i + 1)], silu[:, HH * i:HH * (i + 1)],
                                                bank[3 + i][:, 0:HH], ALU.mult)
                    ins.then_inc(s_ed, 1)

                def low(t, u):
                    dve.wait_ge(s_eh, t + 1)
                    for i, n in HT_BANKS:
                        cols = slice(4 * P * i, 4 * P * i + n)
                        ins = dve.tensor_tensor(h2[:, u, 1, cols], bank[6 + i][:, 0:n], h2[:, u, 0, cols],
                                                ALU.subtract)
                    ins.then_inc(s_el, 1)

                def first(t, u):
                    split(0, 0)
                    product(0, 0)
                    split(1, 1)
                    low(0, 0)

                def step(t, u):
                    product(t, u)
                    if ahead(t, NT):
                        split(t + 1, 1 - u)
                    low(t, u)

                rotate(dve, NT, first, step, lambda t, u: None)
                dve.wait_ge(s_hTp, NT)
                fp8_scale(dve, C["linear_sc"], amr, s_q)
                to_fp8(dve, C["linear_wq"][:].rearrange("p k n -> p (k n)"),
                       C["linear_w"][:].rearrange("p k n -> p (k n)"), C["linear_sc"],
                       (hid[:, 0:KT * D], silu[:, 0:KT * D]), s_q, FP8_SCALE_STEPS, s_wq)


def stage_resampler(nc, T, C, tag="C"):
    xres, ident, mv, tg, half = (C[k] for k in ("xres", "ident", "mv", "tg", "half"))
    with ExitStack() as ctx:
        def sb(name, shape, dt=F32):
            return ctx.enter_context(nc.sbuf_tensor(tag + name, shape, dt))

        def sem(name):
            return nc.alloc_semaphore(name=tag + name)

        NK = 2 * P
        INNER = H1 * DH1
        wq = sb("wq", [P, 2, KT, INNER], BF16)
        wk = sb("wk", [P, 2, KT, INNER], BF16)
        wv = sb("wv", [P, 2, KT, INNER], BF16)
        wo = sb("wo", [P, 2, INNER // P, D], BF16)
        weights = (wq, wk, wv, wo)
        raw = C["wide"][:, 0:8 * KT * INNER].bitcast(F32).rearrange("p (i n) -> p i n", i=4)
        gb = sb("gb", [P, 2, 2, KT])
        cx = sb("cx", [P, NB, D])
        rows = C["rows"]
        mvctx = C["ctx_mv"]
        rlat = sb("rlat", [P, NB])
        xw = sb("xw", [P, D])
        stats = sb("stats", [P, 6])
        mv1 = sb("mv1", [P, 2])
        ve1 = sb("ve1", [P, 1])
        r1 = sb("r1", [P, 1])
        xc = sb("xc", [P, 2, D])
        kvf = sb("kvf", [P, KT, NK])
        kv2 = sb("kv2", [P, 2, 2, KT, NK], BF16)
        qT = sb("qT", [P, 2, 2, H1 // 2, P], BF16)
        kT = sb("kT", [P, 2, 2, H1 // 2, NK], BF16)
        whole = sb("whole", [P, 6, 512])
        v1 = sb("v1", [P, 2, 2, 2, H1, DH1 + 1], BF16)
        E = sb("E", [P, 2, 4, NK])
        PT = sb("PT", [P, 2, 2, 4, 2, P], BF16)
        mx = sb("mx", [P, 2, 4])
        mxs = sb("mxs", [P, 2, 4])
        rs = sb("rs", [P, 4])
        On = sb("On", [P, INNER])
        OT = sb("OT", [P, 2, INNER // P, P], BF16)

        pS = [ctx.enter_context(nc.psum_tensor(f"{tag}pS{i}", [P, 4, NK], F32)) for i in range(2)]
        pF = ctx.enter_context(nc.psum_tensor(f"{tag}pF", [P, 512], F32))
        pT = [ctx.enter_context(nc.psum_tensor(f"{tag}pT{i}", [P, 4, P], F32)) for i in range(2)]
        pO = ctx.enter_context(nc.psum_tensor(f"{tag}pO", [P, 512], F32))
        psO = pO[:, 0:4 * (DH1 + 1)].rearrange("p (h d) -> p h d", h=4)

        s_yg = [sem(f"y_gathered{j}") for j in range(NB)]
        s_x2 = sem("x_with_experts")
        s_bs2 = sem("bn_stats_of_x")
        s_gb = sem("scales_in")
        s_cx = sem("ctx_in")
        s_hi = sem("w_high")
        s_lo = sem("w_low")
        s_lo3 = sem("output_w_low")
        s_one = sem("ones_ready")
        s_mv = sem("mean_var")
        s_ve2 = sem("latents_scale_steps")
        s_rs2 = sem("latents_scale")
        s_xc = sem("rows_normed")
        s_Tp = sem("rowsT_in_psum")
        s_aff = sem("rowsT_scaled")
        s_kvh = sem("kv_input_high")
        s_kvl = sem("kv_input_low")
        s_qp = sem("q_in_psum")
        s_q = sem("q")
        s_kp = sem("k_in_psum")
        s_k = sem("k")
        s_qh = sem("q_high")
        s_ql = sem("q_low")
        s_kh = sem("k_high")
        s_kl = sem("k_low")
        s_vp = sem("v_in_psum")
        s_vh = sem("v_high")
        s_v = sem("v_low")
        s_S = sem("scores")
        s_mx = sem("maxima")
        s_mxs = sem("maxima_scaled")
        s_E = sem("exps")
        s_PTp = sem("PT_in_psum")
        s_PTh = sem("PT_high")
        s_PT = sem("PT_low")
        s_O = sem("O_in_psum")
        s_rs = sem("recip_sums")
        s_On = sem("O_normed")
        s_OTp = sem("OT_in_psum")
        s_OTh = sem("OT_high")
        s_OTl = sem("OT_low")
        s_y = sem("y_in_psum")
        s_x = sem("x_new")
        s_bs = sem("new_bn_stats")
        s_keep = sem("x_kept")
        s_mv1 = sem("new_mean_var")
        s_ve1 = sem("new_var_eps")
        s_r1 = sem("new_rstd")
        s_xr = sem("new_rows_normed")
        s_amb = sem("new_rows_greatest")

        rctx = C["ctx_rstd"]

        def flat(ap):
            return ap.rearrange("p m t -> p (m t)")

        def parts(i):
            return (weights[i][:, part].rearrange("p k n -> p (k n)") for part in range(2))

        def heads_of(ap, g):
            return ap[:, 4 * g:4 * g + 4, :].rearrange("p (n r) d -> p r n d", r=2)

        even, odd = (pS[i][:].rearrange("p m t -> p (m t)") for i in range(2))
        turned_o = (even[:, 0:512], even[:, 512:1024])
        turned_rows = odd[:, 512:1024]
        projected = (pF[:], odd[:, 0:512])

        def v_part(u, part, i):
            return v1[:, u, part, i // 2, 8 * (i % 2):8 * (i % 2) + 8, 0:DH1]

        with nc.Block() as block:
            def for_next(part):
                def run(b, u, i):
                    if ahead(b, NB):
                        part(b + 1, 1 - u, i)
                return run

            def interleaved(eng, F, A):
                def step(b, u):
                    run(b, u, True, True)

                def run(b, u, f, a):
                    for kind, what, i in ORDER:
                        if kind == "F" and f and what in F:
                            F[what](b, u, i)
                        if kind == "A" and a and what in A:
                            A[what](b - 1, 1 - u, i)

                rotate(eng, NB, lambda b, u: run(b, u, True, False), step, lambda b, u: run(b, u, False, True))

            @block.sync
            def _(sp):
                sp.dma_start(gb[:], T["C_gb"]).then_inc(s_gb, 16)
                sp.dma_start(cx[:], T["ctx"]).then_inc(s_cx, 16)

            @block.scalar
            def _(act):
                act.wait_ge(C["s_wide"], 16 * 8)
                for i in range(4):
                    hi, _ = parts(i)
                    act.activation(hi, raw[:, i], ACT.Copy).then_inc(s_hi, 1)

                def kv_high(b, u, i):
                    act.wait_ge(s_aff, 4 * b + 4)
                    act.activation(kv2[:, u, 0], kvf[:], ACT.Copy).then_inc(s_kvh, 1)

                def q(b, u, i):
                    act.wait_ge(s_qp, 2 * b + i + 1)
                    wait(act, s_ql, 2 * b)
                    act.activation(whole[:, i], projected[i], ACT.Copy).then_inc(s_q, 1)
                    act.wait_ge(s_q, 2 * b + i + 1)
                    act.activation(flat(qT[:, u, 0, 4 * i:4 * i + 4]), whole[:, i], ACT.Copy).then_inc(s_qh, 1)

                def k(b, u, i):
                    act.wait_ge(s_kp, 4 * b + i + 1)
                    wait(act, s_kl, 4 * b)
                    act.activation(whole[:, 2 + i], pF[:], ACT.Copy).then_inc(s_k, 1)
                    act.wait_ge(s_k, 4 * b + i + 1)
                    act.activation(flat(kT[:, u, 0, 2 * i:2 * i + 2]), whole[:, 2 + i], ACT.Copy).then_inc(s_kh, 1)

                def exp(b, u, g):
                    act.wait_ge(s_mxs, 4 * b + g + 1)
                    if g >= 2:
                        act.wait_ge(s_PTp, 8 * b + 2 * g - 2)
                    else:
                        wait(act, s_PTp, 8 * b + 2 * g - 2)
                    for h in range(4):
                        ins = act.activation(E[:, g % 2, h], pS[g % 2][:, h], ACT.Exp, bias=mxs[:, g % 2, h:h + 1],
                                             scale=DH1 ** -0.5)
                    ins.then_inc(s_E, 1)

                def turned(b, u, g):
                    if g >= 2:
                        act.wait_ge(s_O, 4 * b + g - 1)
                    for r in range(2):
                        act.wait_ge(s_PTp, 8 * b + 2 * g + r + 1)
                        act.activation(PT[:, g % 2, 0, 2 * r:2 * r + 2].rearrange("p n k t -> p (n k) t"),
                                       pT[r][:], ACT.Copy).then_inc(s_PTh, 1)

                def v(b, u, i):
                    act.wait_ge(s_vp, 4 * b + i + 1)
                    wait(act, s_O, 4 * b - 4)
                    act.activation(v_part(u, 0, i), projected[i % 2].rearrange("p (h d) -> p h d", d=DH1),
                                   ACT.Copy).then_inc(s_vh, 1)

                def o_high(b, u, g):
                    act.wait_ge(s_OTp, 2 * b + g + 1)
                    wait(act, s_y, b)
                    act.activation(OT[:, 0, 4 * g:4 * g + 4].rearrange("p m t -> p (m t)"), turned_o[g],
                                   ACT.Copy).then_inc(s_OTh, 1)

                kv_high(0, 0, 0)
                q(0, 0, 0)
                interleaved(act, {"T": for_next(kv_high), "q0": for_next(q), "q": q, "k": k, "v": v},
                            {"S": lambda b, u, g: None, "exp": exp, "PT": turned, "OT": o_high})

            @block.gpsimd
            def _(pool):
                def gather(j):
                    pool.indirect_dma_start(
                        out=rows[:, j], out_offset=None, in_=C["results"].rearrange("t p n -> (t p) n"),
                        in_offset=bass.IndirectOffsetOnAxis(ap=C["slot_of"][:, j:j + 1].bitcast(U32), axis=0),
                    ).then_inc(s_yg[j], 16)

                def scale_latents(c):
                    bs = slice(GC * c, GC * (c + 1))
                    pool.wait_ge(s_mv, GC * (c + 1))
                    pool.tensor_scalar(C["vare"][:, bs], mv[:, bs, 1], 1.0 + EPS, EPS * EPS, ALU.mult,
                                       ALU.add).then_inc(s_ve2, 1)
                    pool.wait_ge(s_ve2, c + 1)
                    pool.tensor_tensor(rlat[:, bs], C["vare"][:, bs], half[:, bs], ALU.pow).then_inc(s_rs2, 1)

                for part, value in enumerate((1.0, 0.0)):
                    pool.memset(v1[:, :, part, :, :, DH1:DH1 + 1], value).then_inc(s_one, 1)
                for j in range(NB - GC):
                    gather(j)
                scale_latents(0)
                for j in range(NB - GC, NB):
                    gather(j)
                scale_latents(1)
                hi, lo = parts(3)
                pool.wait_ge(s_hi, 4)
                pool.tensor_tensor(lo, raw[:, 3], hi, ALU.subtract).then_inc(s_lo3, 1)
                scale_latents(2)
                scale_latents(3)

                def low_parts(b, u):
                    for i in range(2):
                        pool.wait_ge(s_qh, 2 * b + i + 1)
                        pool.tensor_tensor(flat(qT[:, u, 1, 4 * i:4 * i + 4]), whole[:, i],
                                           flat(qT[:, u, 0, 4 * i:4 * i + 4]), ALU.subtract).then_inc(s_ql, 1)
                    for i in range(4):
                        pool.wait_ge(s_kh, 4 * b + i + 1)
                        pool.tensor_tensor(flat(kT[:, u, 1, 2 * i:2 * i + 2]), whole[:, 2 + i],
                                           flat(kT[:, u, 0, 2 * i:2 * i + 2]), ALU.subtract).then_inc(s_kl, 1)

                def rstd_new(b):
                    pool.wait_ge(s_mv1, b + 1)
                    pool.tensor_tensor(ve1[:], mv1[:, 1:2], C["eps"][:], ALU.add).then_inc(s_ve1, 1)
                    pool.wait_ge(s_ve1, b + 1)
                    pool.tensor_tensor(r1[:], ve1[:], half[:, 0:1], ALU.pow).then_inc(s_r1, 1)

                def step(b, u):
                    low_parts(b, u)
                    rstd_new(b - 1)

                rotate(pool, NB, low_parts, step, lambda b, u: rstd_new(b - 1))

            @block.tensor
            def _(pe):
                pe.wait_ge(s_one, 2)

                def turn(b, u, i):
                    pe.wait_ge(s_xc, 2 * b + 2)
                    wait(pe, s_E, 4 * b - 4)
                    for src in range(2):
                        for k in range(KT):
                            mm = pe.transpose(turned_rows[:, (2 * k + src) * P:(2 * k + src + 1) * P],
                                              xc[:, src, k * P:(k + 1) * P], ident[:])
                    mm.then_inc(s_Tp, 1)

                def product(out, lhs, rhs, done=None):
                    i = 0
                    for k in range(KT):
                        for a, c in ((0, 0), (0, 1), (1, 0)):
                            mm = pe.matmul(out, lhs(a, k), rhs(c, k), start=(i == 0), stop=(i == 3 * KT - 1))
                            i += 1
                    return mm

                def q(b, u, i):
                    if isinstance(b, int) and b == 0:
                        pe.wait_ge(s_lo, 1)
                    if i == 0:
                        pe.wait_ge(s_kvl, b + 1)
                    wait(pe, s_v, 4 * b - 1 + i)
                    for m in range(4 * i, 4 * i + 4):
                        mm = product(projected[i][:, m % 4 * P:(m % 4 + 1) * P], lambda a, k: wq[:, a, k, m * P:(m + 1) * P],
                                     lambda c, k: kv2[:, u, c, k, P:NK])
                    mm.then_inc(s_qp, 1)

                def k_(b, u, i):
                    if isinstance(b, int) and b == 0:
                        pe.wait_ge(s_lo, 2)
                    if i == 0:
                        pe.wait_ge(s_q, 2 * b + 1)
                    else:
                        pe.wait_ge(s_k, 4 * b + i)
                    for m in range(2 * i, 2 * i + 2):
                        mm = product(pF[:, m % 2 * NK:(m % 2 + 1) * NK],
                                     lambda a, k: wk[:, a, k, m * P:(m + 1) * P], lambda c, k: kv2[:, u, c, k])
                    mm.then_inc(s_kp, 1)

                def v(b, u, i):
                    if isinstance(b, int) and b == 0:
                        pe.wait_ge(s_lo, 3)
                    if i == 0:
                        pe.wait_ge(s_k, 4 * b + 4)
                    elif i == 1:
                        wait(pe, s_E, 4 * b)
                    else:
                        pe.wait_ge(s_v, 4 * b + i - 1)
                    t, h = i // 2, i % 2
                    product(projected[i % 2], lambda a, k: kv2[:, u, a, k, t * P:(t + 1) * P],
                            lambda c, k: wv[:, c, k, h * 512:(h + 1) * 512]).then_inc(s_vp, 1)

                def scores(b, u, g):
                    if g == 0:
                        pe.wait_ge(s_ql, 2 * b + 2)
                        pe.wait_ge(s_kl, 4 * b + 4)
                        wait(pe, s_OTl, 2 * b)
                    elif g == 1 and ahead(b, NB):
                        pe.wait_ge(s_q, 2 * b + 4)
                    elif g == 1:
                        pe.wait_ge(s_v, 4 * b + 4)
                    if g >= 2:
                        pe.wait_ge(s_E, 4 * b + g - 1)
                    for n in range(2):
                        for i, (a, c) in enumerate(((0, 0), (1, 0), (0, 1))):
                            for r in range(2):
                                rows = slice(DH1 * r, DH1 * (r + 1))
                                mm = pe.matmul(pS[g % 2][:, 2 * r + n], qT[rows, u, a, 2 * g + n],
                                               kT[rows, u, c, 2 * g + n], start=(i == 0), stop=(i == 2))
                    mm.then_inc(s_S, 1)

                def turn_p(b, u, g):
                    pe.wait_ge(s_E, 4 * b + g + 1)
                    for r in range(2):
                        if g >= 1:
                            pe.wait_ge(s_PT, 8 * b + 2 * g - 1 + r)
                        for n in range(2):
                            for k in range(2):
                                mm = pe.transpose(pT[r][:, 2 * n + k], E[:, g % 2, 2 * r + n, k * P:(k + 1) * P],
                                                  ident[:])
                        mm.then_inc(s_PTp, 1)

                def weigh(b, u, g):
                    pe.wait_ge(s_PT, 8 * b + 2 * g + 2)
                    if g == 0:
                        pe.wait_ge(s_v, 4 * b + 4)
                        wait(pe, s_x, b)
                    else:
                        pe.wait_ge(s_On, 4 * b + g)
                    for r in range(2):
                        for n in range(2):
                            h = 4 * g + 2 * n + r
                            for k in range(2):
                                for a, c in ((0, 0), (0, 1), (1, 0)):
                                    mm = pe.matmul(psO[:, 2 * r + n], PT[:, g % 2, a, 2 * r + n, k],
                                                   v1[:, u, c, k, h], start=(k + a + c == 0), stop=(k + a == 2))
                    mm.then_inc(s_O, 1)

                def turn_o(b, u, g):
                    pe.wait_ge(s_On, 4 * b + 2 * g + 2)
                    if g == 0:
                        pe.wait_ge(s_E, 4 * b + 3)
                    for m in range(4):
                        mm = pe.transpose(turned_o[g][:, m * P:(m + 1) * P],
                                          On[:, (4 * g + m) * P:(4 * g + m + 1) * P], ident[:])
                    mm.then_inc(s_OTp, 1)

                def result(b, u, i):
                    if isinstance(b, int) and b == 0:
                        pe.wait_ge(s_lo3, 1)
                    pe.wait_ge(s_OTl, 2 * b + 2)
                    n = INNER // P
                    for m in range(n):
                        for a, c in ((0, 0), (1, 0), (0, 1)):
                            mm = pe.matmul(pO[:, 0:D], OT[:, a, m], wo[:, c, m], start=(m == 0 and a + c == 0),
                                           stop=(m == n - 1 and c == 1))
                    mm.then_inc(s_y, 1)

                turn(0, 0, 0)
                q(0, 0, 0)
                interleaved(pe, {"T": for_next(turn), "q0": for_next(q), "q": q, "k": k_, "v": v},
                            {"S": scores, "PT": turn_p, "PV": weigh, "OT": turn_o, "y": result})

            @block.vector
            def _(dve):
                def low(i):
                    hi, lo = parts(i)
                    dve.wait_ge(s_hi, i + 1)
                    dve.tensor_tensor(lo, raw[:, i], hi, ALU.subtract).then_inc(s_lo, 1)

                def combine(c):
                    for j in range(GC * c, GC * (c + 1)):
                        dve.wait_ge(s_yg[j], 16)
                        dve.scalar_tensor_tensor(xres[:, j], rows[:, j], C["croute"][:, j:j + 1], xres[:, j],
                                                 ALU.mult, ALU.add).then_inc(s_x2, 1)
                        dve.wait_ge(s_x2, j + 1)
                        dve.bn_stats(C["bstats"][:, j], xres[:, j]).then_inc(s_bs2, 1)
                    dve.wait_ge(s_bs2, GC * (c + 1))
                    for j in range(GC * c, GC * (c + 1)):
                        dve.bn_aggr(mv[:, j], C["bstats"][:, j]).then_inc(s_mv, 1)

                def norm(b, u, i):
                    for src, ap, means, scales in ((0, cx, mvctx, rctx), (1, xres, mv, rlat)):
                        m = means[:, bass.ds(b, 1), 0:1].rearrange("p o n -> p (o n)")
                        dve.tensor_scalar(xc[:, src], row(ap, b), m, scales[:, bass.ds(b, 1)],
                                          ALU.subtract, ALU.mult).then_inc(s_xc, 1)

                def scale(b, u, i):
                    dve.wait_ge(s_Tp, b + 1)
                    wait(dve, s_kvh, b)
                    wait(dve, s_kvl, b)
                    for src in range(2):
                        for k in range(KT):
                            dve.tensor_scalar(kvf[:, k, src * P:(src + 1) * P],
                                              turned_rows[:, (2 * k + src) * P:(2 * k + src + 1) * P],
                                              gb[:, src, 0, k:k + 1], gb[:, src, 1, k:k + 1],
                                              ALU.mult, ALU.add).then_inc(s_aff, 1)
                    dve.wait_ge(s_kvh, b + 1)
                    dve.tensor_tensor(kv2[:, u, 1], kvf[:], kv2[:, u, 0], ALU.subtract).then_inc(s_kvl, 1)
                    if isinstance(b, int) and b == 0:
                        for c in range(1, NB // GC):
                            combine(c)
                        dve.wait_ge(s_rs2, NB // GC)

                def v(b, u, i):
                    dve.wait_ge(s_vh, 4 * b + i + 1)
                    dve.tensor_tensor(v_part(u, 1, i), projected[i % 2].rearrange("p (h d) -> p h d", d=DH1),
                                      v_part(u, 0, i), ALU.subtract).then_inc(s_v, 1)

                def p_low(b, u, g):
                    for r in range(2):
                        dve.wait_ge(s_PTh, 8 * b + 2 * g + r + 1)
                        low = PT[:, g % 2, 1, 2 * r:2 * r + 2].rearrange("p n k t -> p (n k) t")
                        high = PT[:, g % 2, 0, 2 * r:2 * r + 2].rearrange("p n k t -> p (n k) t")
                        dve.tensor_tensor(low, pT[r][:], high, ALU.subtract).then_inc(s_PT, 1)

                def maxima(b, u, g):
                    dve.wait_ge(s_S, 4 * b + g + 1)
                    dve.tensor_reduce(mx[:, g % 2], pS[g % 2][:], AX.X, ALU.max).then_inc(s_mx, 1)
                    dve.wait_ge(s_mx, 4 * b + g + 1)
                    if g >= 2:
                        dve.wait_ge(s_E, 4 * b + g - 1)
                    else:
                        wait(dve, s_E, 4 * b + g - 1)
                    dve.tensor_scalar(mxs[:, g % 2], mx[:, g % 2], -DH1 ** -0.5, None, ALU.mult).then_inc(s_mxs, 1)

                def o_norm(b, u, g):
                    dve.wait_ge(s_O, 4 * b + g + 1)
                    if g >= 1:
                        dve.wait_ge(s_On, 4 * b + g)
                    else:
                        wait(dve, s_x, b)
                    if g % 2 == 0:
                        wait(dve, s_OTp, 2 * b + g // 2 - 1 if g else 2 * b)
                    dve.reciprocal(rs[:], psO[:, :, DH1]).then_inc(s_rs, 1)
                    dve.wait_ge(s_rs, 4 * b + g + 1)
                    on = heads_of(On[:].rearrange("p (h d) -> p h d", d=DH1), g)
                    for r in range(2):
                        ins = dve.tensor_tensor(on[:, r], psO[:, 2 * r:2 * r + 2, 0:DH1],
                                                rs[:, 2 * r:2 * r + 2].unsqueeze(2).broadcast_to([P, 2, DH1]),
                                                ALU.mult)
                    ins.then_inc(s_On, 1)

                def o_low(b, u, g):
                    dve.wait_ge(s_OTh, 2 * b + g + 1)
                    dve.tensor_tensor(OT[:, 1, 4 * g:4 * g + 4].rearrange("p m t -> p (m t)"), turned_o[g],
                                      OT[:, 0, 4 * g:4 * g + 4].rearrange("p m t -> p (m t)"),
                                      ALU.subtract).then_inc(s_OTl, 1)

                def norm_new(b):
                    dve.wait_ge(s_r1, b + 1)
                    dve.tensor_scalar(row(rows, b), xw[:], mv1[:, 0:1], r1[:], ALU.subtract,
                                      ALU.mult).then_inc(s_xr, 1)

                def greatest(b):
                    dve.tensor_reduce(C["greatest"][:, bass.ds(b, 1)], row(rows, b), AX.X, ALU.max,
                                      apply_absolute_value=True).then_inc(s_amb, 1)

                def add(b, u, i):
                    if not isinstance(b, int) or b >= 1:
                        norm_new(b - 1)
                        dve.wait_ge(s_xr, b)
                    dve.wait_ge(s_y, b + 1)
                    wait(dve, s_keep, b)
                    dve.scalar_tensor_tensor(xw[:], pO[:, 0:D], tg[:, 1:2], row(xres, b), ALU.mult,
                                             ALU.add).then_inc(s_x, 1)
                    dve.wait_ge(s_x, b + 1)
                    dve.bn_stats(stats[:], xw[:]).then_inc(s_bs, 1)
                    dve.wait_ge(s_bs, b + 1)
                    dve.tensor_scalar(row(xres, b), xw[:], 0.0, None, ALU.add).then_inc(s_keep, 1)
                    dve.bn_aggr(mv1[:], stats[:]).then_inc(s_mv1, 1)
                    if not isinstance(b, int) or b >= 1:
                        greatest(b - 1)

                for i in range(3):
                    low(i)
                combine(0)
                dve.wait_ge(s_rs2, 1)
                dve.wait_ge(s_cx, 16)
                dve.wait_ge(s_gb, 16)
                norm(0, 0, 0)
                scale(0, 0, 0)
                interleaved(dve, {"T": for_next(scale), "norm": for_next(norm), "v low": v},
                            {"maxima": maxima, "PT low": p_low, "O": o_norm, "OT low": o_low, "y": add})
                norm_new(NB - 1)
                dve.wait_ge(s_xr, NB)
                greatest(NB - 1)


ORDER = [("A", "S", 0), ("F", "q", 1), ("A", "maxima", 0), ("A", "exp", 0), ("F", "k", 0), ("A", "S", 1),
         ("A", "PT", 0), ("A", "maxima", 1), ("A", "exp", 1), ("A", "S", 2), ("F", "k", 1),
         ("A", "PT low", 0), ("A", "maxima", 2), ("A", "PT", 1), ("F", "k", 2), ("A", "PT low", 1),
         ("A", "PV", 0), ("A", "O", 0), ("A", "exp", 2), ("A", "S", 3), ("F", "k", 3), ("A", "PT", 2),
         ("A", "maxima", 3), ("A", "exp", 3), ("F", "norm", 0), ("A", "PV", 1), ("A", "O", 1),
         ("A", "PT low", 2), ("F", "v", 0), ("F", "v low", 0), ("A", "OT", 0), ("A", "PT", 3),
         ("A", "PV", 2), ("A", "PT low", 3), ("A", "O", 2), ("A", "OT low", 0), ("F", "v", 1),
         ("F", "v low", 1), ("A", "PV", 3), ("A", "O", 3), ("F", "T", 0), ("F", "v", 2),
         ("F", "v low", 2), ("A", "OT", 1), ("A", "OT low", 1), ("F", "v", 3), ("F", "v low", 3),
         ("F", "q0", 0), ("A", "y", 0)]


def stage_linear(nc, T, C, out, tag="D"):
    xres, tg, ident, rows, wq = (C[k] for k in ("xres", "tg", "ident", "rows", "linear_wq"))
    with ExitStack() as ctx:
        def sb(name, shape, dt=F32):
            return ctx.enter_context(nc.sbuf_tensor(tag + name, shape, dt))

        def sem(name):
            return nc.alloc_semaphore(name=tag + name)

        GB = 2
        bias = sb("bias", [P, D])
        xq = sb("xq", [P, NB, D], BF16)
        place = sb("place", [P, 2, 2, GB * D])
        am = sb("am", [P, 1])
        amr = sb("amr", [P, 1])
        sc = sb("sc", [P, 2])
        back = sb("back", [P, 1])
        idb = sb("idb", [P, P], BF16)
        xT = sb("xT", [P, 2, KT, P], BF16)
        yf = sb("yf", [P, 2, D])
        yb = sb("yb", [P, 2, D], BF16)
        yg = sb("yg", [P, 2, D])
        fin = sb("fin", [P, 2, D])
        pT = [ctx.enter_context(nc.psum_tensor(f"{tag}pT{i}", [P, KT, P], BF16)) for i in range(2)]
        pY = [ctx.enter_context(nc.psum_tensor(f"{tag}pY{i}", [P, 512], F32)) for i in range(2)]

        s_in = sem("bias_in")
        s_id = sem("identity")
        s_am = sem("greatest_of_partition")
        s_amr = sem("greatest")
        s_c = sem("scale_steps")
        s_back = sem("output_scale")
        s_q = sem("rounding_steps")
        s_xq = sem("x_rounded")
        s_Tp = sem("xT_in_psum")
        s_T = sem("xT")
        s_y = sem("y_in_psum")
        s_yf = sem("y_scaled")
        s_yb = sem("y_rounded")
        s_yg = sem("y_gated")
        s_fin = sem("out_ready")
        s_out = [sem(f"out_stored{u}") for u in range(2)]

        with nc.Block() as block:
            @block.sync
            def _(sp):
                sp.dma_start(bias[:], T["D_bias"].partition_broadcast(P)).then_inc(s_in, 16)
                for b in range(NB):
                    sp.wait_ge(s_fin, b + 1)
                    sp.dma_start(out[:, b], fin[:, b % 2]).then_inc(s_out[b % 2], 16)
                for u in range(2):
                    sp.wait_ge(s_out[u], 16 * NB // 2)

            @block.gpsimd
            def _(pool):
                pool.tensor_copy(idb[:], ident[:]).then_inc(s_id, 1)
                pool.wait_ge(s_am, 1)
                pool.partition_all_reduce(amr[:], am[:], P, bass.bass_isa.ReduceOp.max).then_inc(s_amr, 1)
                for b in range(NB):
                    u = b % 2
                    pool.wait_ge(s_yg, b + 1)
                    if b >= 2:
                        pool.wait_ge(s_out[u], 16 * (b // 2))
                    pool.tensor_tensor(fin[:, u], yg[:, u], xres[:, b], ALU.add).then_inc(s_fin, 1)

            @block.scalar
            def _(act):
                def gate(b):
                    u = b % 2
                    act.wait_ge(s_yf, b + 1)
                    act.activation(yb[:, u], yf[:, u], ACT.Copy).then_inc(s_yb, 1)
                    act.wait_ge(s_yb, b + 1)
                    if b >= 2:
                        act.wait_ge(s_fin, b - 1)
                    act.activation(yg[:, u], yb[:, u], ACT.Copy, scale=tg[:, 3:4]).then_inc(s_yg, 1)

                for b in range(NB):
                    u = b % 2
                    act.wait_ge(s_Tp, b + 1)
                    if b >= 2:
                        act.wait_ge(s_y, b - 1)
                    act.activation(xT[:, u], pT[u][:], ACT.Copy).then_inc(s_T, 1)
                    if b >= 1:
                        gate(b - 1)
                gate(NB - 1)

            @block.tensor
            def _(pe):
                pe.wait_ge(s_id, 1)

                def turn(b):
                    u = b % 2
                    pe.wait_ge(s_xq, b // GB + 1)
                    if b >= 2:
                        pe.wait_ge(s_T, b - 1)
                    for k in range(KT):
                        mm = pe.transpose(pT[u][:, k], xq[:, b, k * P:(k + 1) * P], idb[:])
                    mm.then_inc(s_Tp, 1)

                turn(0)
                for b in range(NB):
                    u = b % 2
                    if b + 1 < NB:
                        turn(b + 1)
                    pe.wait_ge(s_T, b + 1)
                    if b >= 2:
                        pe.wait_ge(s_yf, b - 1)
                    for k in range(KT):
                        mm = pe.matmul(pY[u][:, 0:D], xT[:, u, k], wq[:, k], start=(k == 0), stop=(k == KT - 1))
                    mm.then_inc(s_y, 1)

            @block.vector
            def _(dve):
                dve.tensor_reduce(am[:], C["greatest"][:], AX.X, ALU.max).then_inc(s_am, 1)
                dve.wait_ge(s_amr, 1)
                fp8_scale(dve, sc, amr, s_c)
                dve.tensor_tensor(back[:], sc[:, 1:2], C["linear_sc"][:, 1:2], ALU.mult).then_inc(s_back, 1)

                def scale(b):
                    u = b % 2
                    if b == 0:
                        dve.wait_ge(s_in, 16)
                        dve.wait_ge(s_back, 1)
                    dve.wait_ge(s_y, b + 1)
                    if b >= 2:
                        dve.wait_ge(s_yb, b - 1)
                    dve.scalar_tensor_tensor(yf[:, u], pY[u][:, 0:D], back[:], bias[:], ALU.mult,
                                             ALU.add).then_inc(s_yf, 1)

                for r in range(NB // GB):
                    if r >= 2:
                        dve.wait_ge(s_xq, r - 1)
                    cols = slice(GB * r, GB * (r + 1))
                    to_fp8(dve, xq[:, cols].rearrange("p b n -> p (b n)"), rows[:, cols].rearrange("p b n -> p (b n)"),
                           sc, (place[:, r % 2, 0], place[:, r % 2, 1]), s_q, FP8_STEPS * r, s_xq,
                           between=lambda i: scale(GB * r - 3 + i) if GB * r - 3 + i >= 0 else None)
                for b in range(NB - 3, NB):
                    scale(b)


def build(nc, T, out):
    with ExitStack() as ctx:
        def sb(name, shape, dt=F32):
            return ctx.enter_context(nc.sbuf_tensor(name, shape, dt))

        def sem(name):
            return ctx.enter_context(nc.semaphore(name))

        C = {}
        C["xres"] = xres = sb("xres", [P, NB, D])
        C["ident"] = ident = sb("ident", [P, P])
        C["first"] = first = sb("first", [P, 1])
        C["rest"] = rest = sb("rest", [P, 1])
        C["mv"] = sb("mv", [P, NB, 2])
        C["rstd"] = sb("rstd", [P, NB])
        C["tg"] = tg = sb("tg", [P, 4])
        C["half"] = half = sb("half", [P, NB])
        C["vare"] = sb("vare", [P, NB])
        C["bstats"] = sb("bstats", [P, NB, 6])
        C["s_ident"] = s_ident = sem("ident_ready")
        C["s_masks"] = s_masks = sem("masks_ready")
        C["s_tanh"] = s_tanh = sem("tanh_ready")
        C["ctx_mv"] = sb("ctx_mv", [P, NB, 2])
        C["ctx_rstd"] = sb("ctx_rstd", [P, NB])
        C["pos"] = sb("pos", [P, NB, 2], I32)
        C["zero"] = sb("zero", [P, D])
        C["eps"] = sb("eps", [P, 1])
        C["wide"] = sb("wide", [P, 2 * max(WCOLS + KT * NTOK, 4 * KT * H1 * DH1)], BF16)
        C["slot_of"] = sb("slot_of", [P, NB], I32)
        C["croute"] = sb("croute", [P, NB])
        C["linear_w"] = sb("linear_w", [P, KT, D])
        C["linear_wq"] = sb("linear_wq", [P, KT, D], BF16)
        C["linear_sc"] = sb("linear_sc", [P, 2])
        C["s_pos"] = sem("pos_in")
        C["s_zero"] = sem("zeros_made")
        C["s_zeroed"] = sem("slots_zeroed")
        C["s_wide"] = sem("resampler_weights_in")
        C["slots"] = nc.dram_tensor("slots", (NT, P, D), F32, kind="Internal").ap()
        C["results"] = nc.dram_tensor("results", (NT, P, D), F32, kind="Internal").ap()
        C["s_x"] = s_x = [sem(f"x_in{c}") for c in range(NB // GC)]
        s_g = sem("gates_in")
        s_m = sem("setup_memsets")

        with nc.Block() as block:
            @block.sync
            def _(sp):
                sp.dma_start(tg[:], T["gates"].partition_broadcast(P)).then_inc(s_g, 16)
                sp.dma_start(C["pos"][:], T["pos"]).then_inc(C["s_pos"], 16)
                sp.dma_start(xres[:, 0:GC], T["x"][:, 0:GC]).then_inc(s_x[0], 16)

            @block.scalar
            def _(act):
                act.wait_ge(s_g, 16)
                act.activation(tg[:], tg[:], ACT.Tanh).then_inc(s_tanh, 1)

            @block.gpsimd
            def _(pool):
                pool.memset(C["zero"][:], 0.0).then_inc(C["s_zero"], 1)
                pool.memset(ident[:], 0.0).then_inc(s_m, 1)
                pool.memset(half[:], -0.5).then_inc(s_m, 1)
                pool.memset(C["eps"][:], EPS).then_inc(s_m, 1)
                pool.memset(first[:], 0.0).then_inc(s_m, 1)
                pool.memset(rest[:], 0.0).then_inc(s_m, 1)
                pool.wait_ge(s_m, 5)
                pool.affine_select(out=ident[:], in_=ident[:], compare_op=ALU.not_equal, fill=1.0, base=0,
                                   pattern=[[-1, P]], channel_multiplier=1).then_inc(s_ident, 1)
                pool.affine_select(out=first[:], in_=first[:], compare_op=ALU.not_equal, fill=1.0, base=0,
                                   pattern=[[0, 1]], channel_multiplier=1).then_inc(s_masks, 1)
                pool.affine_select(out=rest[:], in_=rest[:], compare_op=ALU.is_equal, fill=1.0, base=0,
                                   pattern=[[0, 1]], channel_multiplier=1).then_inc(s_masks, 1)

        with nc.cleanup_on_exit():
            stage_rope_attention(nc, T, C)
        with nc.cleanup_on_exit():
            stage_experts(nc, T, C)
        C["rows"] = sb("rows", [P, NB, D])
        C["greatest"] = sb("greatest", [P, NB])
        with nc.cleanup_on_exit():
            stage_resampler(nc, T, C)
        stage_linear(nc, T, C, out)


def kernel(**inputs):
    import concourse.bacc as bacc
    from concourse.bass_utils import run_bass_kernel_spmd

    a = {k: np.asarray(v) for k, v in inputs.items()}

    def kmajor(w):
        return np.ascontiguousarray(w.T.reshape(KT, P, -1).transpose(1, 0, 2))

    def expert(w1, w3, w2):
        w2t = np.zeros((FT * P, D), w2.dtype)
        w2t[:FF] = w2.T
        parts = [kmajor(w1).reshape(P, -1), kmajor(w3).reshape(P, -1),
                 w2t.reshape(FT, P, D).transpose(1, 0, 2).reshape(P, -1)]
        return np.concatenate(parts, axis=1).reshape(P, 4, QC).transpose(1, 0, 2)

    def outof(w):
        return w.reshape(-1, P, w.shape[1]).transpose(1, 0, 2).reshape(P, -1)

    def bypart(v):
        return v.reshape(KT, P).T

    wkv = a["L1_xattn_Wkv"]
    arrays = {
        "ctx": np.ascontiguousarray(a["ctx_1024"].transpose(1, 0, 2)),
        "C_w": np.stack([outof(a["L1_xattn_Wq"]), outof(wkv[:, :H1 * DH1]), outof(wkv[:, H1 * DH1:]),
                         outof(a["L1_xattn_Wout"])]),
        "C_gb": np.stack([np.stack([bypart(a["L1_xattn_ln_m_g"]), bypart(a["L1_xattn_ln_m_b"])], 1),
                          np.stack([bypart(a["L1_xattn_ln_l_g"]), bypart(a["L1_xattn_ln_l_b"])], 1)], 1),
        "D_w": kmajor(a["L1_ffn_weight"]),
        "D_bias": a["L1_ffn_bias"],
        "B_rw": kmajor(a["L0_ffn_router_w"]),
        "B_rb": a["L0_ffn_routing_bias"],
        "B_ws": np.ascontiguousarray(expert(a["L0_ffn_sw1"], a["L0_ffn_sw3"], a["L0_ffn_sw2"])),
        "B_we": np.concatenate([expert(a["L0_ffn_ew1"][e], a["L0_ffn_ew3"][e], a["L0_ffn_ew2"][e])
                                for e in range(NE)]),
        "x": np.ascontiguousarray(a["x"].transpose(1, 0, 2)),
        "ctxT": np.ascontiguousarray(a["ctx_1024"].transpose(0, 2, 1).reshape(NB, KT, P, P).transpose(0, 2, 1, 3)),
        "pos": np.ascontiguousarray(a["itok_BxSx2_0_63"].transpose(1, 0, 2)),
        "gates": np.concatenate([a["g_xattn"], a["g_ffn"]]),
        "A_wq": kmajor(a["L0_xattn_Wq"]),
        "A_wkv": kmajor(np.concatenate([a["L0_xattn_Wk"], a["L0_xattn_Wv"]])),
        "A_wp": kmajor(a["L0_xattn_Wp"]),
        "A_bias": np.concatenate([a["L0_xattn_bq"], a["L0_xattn_bk"], a["L0_xattn_bv"], a["L0_xattn_bp"]]),
    }
    nc = bacc.Bacc("TRN2", target_bir_lowering=False, num_devices=1)
    T = {n: nc.dram_tensor(f"in_{n}", v.shape, mybir.dt.from_np(v.dtype), kind="ExternalInput").ap()
         for n, v in arrays.items()}
    out = nc.dram_tensor("out", (P, NB, D), F32, kind="ExternalOutput").ap()
    build(nc, T, out)
    r = run_bass_kernel_spmd(nc, [{f"in_{n}": v for n, v in arrays.items()}], core_ids=[0])
    return np.ascontiguousarray(r.results[0]["out"].transpose(1, 0, 2))
```
